# Optimizing a Trainium2 kernel written in Bass

```python
import numpy as np
import jax
import jax.numpy as jnp

def _softmax(x, axis=-1):
    return jax.nn.softmax(x, axis=axis)

def _gelu(x):
    return jax.nn.gelu(x, approximate=True)

def _silu(x):
    return jax.nn.silu(x)

def _sigmoid(x):
    return jax.nn.sigmoid(x)

def _layernorm(x, axis=-1, eps=1e-05):
    m = jnp.mean(x, axis=axis, keepdims=True)
    v = jnp.var(x, axis=axis, keepdims=True)
    return (x - m) / jnp.sqrt(v + eps)

def _scatter_add(tgt, idx, src, axis=0):
    return tgt.at[idx].add(src)

def _segment_sum(src, seg, n):
    return jax.ops.segment_sum(src, seg, n)
kernel_name = 'mk_decoder_preln_d4_seqx_r8_64dc4b'

def setup_inputs(seed: int=0):
    np.random.seed(seed)
    _w = jnp.asarray

    def _rec_inputs():
        import jax
        import jax.numpy as jnp
        _rk = jax.random.key(seed)
        x = 7.22e-05 + 1 * jax.random.normal(jax.random.fold_in(_rk, 1), (16, 128, 128), jnp.float32)
        _lenS = 128 - jax.random.randint(jax.random.fold_in(_rk, 7), (16,), 0, max(1, 128 // 4) + 1, jnp.int32)
        _lenS2 = 77 - jax.random.randint(jax.random.fold_in(_rk, 8), (16,), 0, max(1, 77 // 4) + 1, jnp.int32)
        _ctx_1024P = jax.random.normal(jax.random.fold_in(_rk, 11), (16, 16, 128), jnp.float32)
        _ctx_1024c = jax.random.dirichlet(jax.random.fold_in(_rk, 511), 0.3 * jnp.ones((16,), jnp.float32), (16, 77))
        _ctx_1024t = jnp.einsum('bsk,bkd->bsd', _ctx_1024c, _ctx_1024P)
        _ctx_1024t = _ctx_1024t * jax.lax.rsqrt(jnp.mean(jnp.square(_ctx_1024t)) + 1e-12) * 0.953939
        ctx_1024 = 4.13588e-05 + 0.999923 * (_ctx_1024t + 0.3 * jax.random.normal(jax.random.fold_in(_rk, 611), (16, 77, 128), jnp.float32))
        return (x, ctx_1024)
    x, ctx_1024 = _rec_inputs()

    def _L0_attn_setup():
        import jax, jax.numpy as jnp
        import numpy as np
        B, N, DIM = (2, 256, 128)
        H = 16
        HD = DIM // H
        key = jax.random.key(seed)
        ks = jax.random.split(key, 4)
        x = jax.random.normal(ks[0], (B, N, DIM), dtype=jnp.float32)
        w_qkv = jax.random.normal(ks[1], (DIM, 3 * DIM), dtype=jnp.float32) / np.sqrt(DIM)
        w_proj = jax.random.normal(ks[2], (DIM, DIM), dtype=jnp.float32) / np.sqrt(DIM)
        b_proj = jax.random.normal(ks[3], (DIM,), dtype=jnp.float32) * 0.01
        return {'x': x, 'w_qkv': w_qkv, 'w_proj': w_proj, 'b_proj': b_proj}
    _L0_attn_all = _L0_attn_setup()
    _L0_attn_in = {k: v for k, v in _L0_attn_all.items() if k in ('w_qkv', 'w_proj', 'b_proj')}
    del _L0_attn_all

    def _L0_xattn_setup():
        import jax, jax.numpy as jnp
        import numpy as np
        B, S, D = (4, 256, 128)
        key = jax.random.key(seed)
        kq, kk, kv = jax.random.split(key, 3)
        q = jax.random.normal(kq, (B, S, D), dtype=jnp.float32)
        k = jax.random.normal(kk, (B, S, D), dtype=jnp.float32)
        v = jax.random.normal(kv, (B, S, D), dtype=jnp.float32)
        return {'q': q, 'k': k, 'v': v}
    _L0_xattn_all = _L0_xattn_setup()
    _L0_xattn_in = {k: v for k, v in _L0_xattn_all.items() if k in ()}
    del _L0_xattn_all

    def _L0_ffn_setup():
        import jax, jax.numpy as jnp
        import numpy as np
        B, S, D = (2, 128, 128)
        L, H = (64, 16)
        HD = L // H
        F, E, K = (256, 8, 2)
        THETA = 10000.0
        EPS = 1e-05

        def _rmsnorm(x, g):
            return x * g * jax.lax.rsqrt(jnp.mean(x * x, axis=-1, keepdims=True) + EPS)

        def _rope(t, pos):
            inv_freq = 1.0 / THETA ** (jnp.arange(0, HD, 2, dtype=jnp.float32) / HD)
            ang = pos[:, None].astype(jnp.float32) * inv_freq[None, :]
            cos, sin = (jnp.cos(ang), jnp.sin(ang))
            t1, t2 = (t[..., 0::2], t[..., 1::2])
            r1 = t1 * cos - t2 * sin
            r2 = t1 * sin + t2 * cos
            return jnp.stack([r1, r2], axis=-1).reshape(t.shape)

        def _forward(x, g1, g2, w_down, wq, wk, wv, w_up, router_w, w1, w2, w3):
            b, s, _ = x.shape
            pos = jnp.arange(s)
            h = _rmsnorm(x, g1)
            c = h @ w_down
            split = lambda t: t.reshape(b, s, H, HD).transpose(0, 2, 1, 3)
            q = _rope(split(c @ wq), pos)
            k = _rope(split(c @ wk), pos)
            v = split(c @ wv)
            scores = jnp.einsum('bhqd,bhkd->bhqk', q, k) / jnp.sqrt(jnp.float32(HD))
            causal = jnp.tril(jnp.ones((s, s), bool))
            scores = jnp.where(causal, scores, -jnp.inf)
            attn = jax.nn.softmax(scores, axis=-1)
            o = jnp.einsum('bhqk,bhkd->bhqd', attn, v).transpose(0, 2, 1, 3).reshape(b, s, L)
            x = x + o @ w_up
            res = x
            t = _rmsnorm(x, g2).reshape(-1, D)
            probs = jax.nn.softmax(t @ router_w, axis=-1)
            vals, idx = jax.lax.top_k(probs, K)
            w = vals / jnp.sum(vals, axis=-1, keepdims=True)
            gate = jnp.sum(jax.nn.one_hot(idx, E, dtype=t.dtype) * w[..., None], axis=1)
            hid = jax.nn.silu(jnp.einsum('td,edf->tef', t, w1)) * jnp.einsum('td,edf->tef', t, w3)
            y_e = jnp.einsum('tef,efd->ted', hid, w2)
            y = jnp.einsum('ted,te->td', y_e, gate)
            return res + y.reshape(b, s, D)
        key = jax.random.key(seed)
        ks = jax.random.split(key, 12)
        g = lambda k, shape, scale: jax.random.normal(k, shape, dtype=jnp.float32) * scale
        return {'x': g(ks[0], (B, S, D), 1.0), 'g1': jnp.ones((D,), jnp.float32), 'g2': jnp.ones((D,), jnp.float32), 'w_down': g(ks[1], (D, L), 0.02), 'wq': g(ks[2], (L, L), 0.02), 'wk': g(ks[3], (L, L), 0.02), 'wv': g(ks[4], (L, L), 0.02), 'w_up': g(ks[5], (L, D), 0.02), 'router_w': g(ks[6], (D, E), 0.02), 'w1': g(ks[7], (E, D, F), 0.02), 'w3': g(ks[8], (E, D, F), 0.02), 'w2': g(ks[9], (E, F, D), 0.02)}
    _L0_ffn_all = _L0_ffn_setup()
    _L0_ffn_in = {k: v for k, v in _L0_ffn_all.items() if k in ('g1', 'g2', 'w_down', 'wq', 'wk', 'wv', 'w_up', 'router_w', 'w1', 'w2', 'w3')}
    del _L0_ffn_all

    def _L1_attn_setup():
        import jax, jax.numpy as jnp
        import numpy as np
        NUM_HEADS = 16
        ROPE_BASE = 10000.0

        def _rotate_half(x):
            xr = x.reshape(*x.shape[:-1], -1, 2)
            x1, x2 = (xr[..., 0], xr[..., 1])
            return jnp.stack((-x2, x1), axis=-1).reshape(x.shape)

        def _rope(x):
            hd = x.shape[-1]
            n = x.shape[-2]
            inv_freq = 1.0 / ROPE_BASE ** (jnp.arange(0, hd, 2, dtype=jnp.float32) / hd)
            freqs = jnp.outer(jnp.arange(n, dtype=jnp.float32), inv_freq)
            freqs = jnp.repeat(freqs, 2, axis=-1)
            return x * jnp.cos(freqs) + _rotate_half(x) * jnp.sin(freqs)
        key = jax.random.key(seed)
        k0, k1, k2 = jax.random.split(key, 3)
        B, N, D = (2, 256, 128)
        X = jax.random.normal(k0, (B, N, D), jnp.float32)
        Wqkv = jax.random.normal(k1, (D, 3 * D), jnp.float32) * D ** (-0.5)
        Wout = jax.random.normal(k2, (D, D), jnp.float32) * D ** (-0.5)
        bout = jnp.zeros((D,), jnp.float32)
        return {'X': X, 'Wqkv': Wqkv, 'Wout': Wout, 'bout': bout}
    _L1_attn_all = _L1_attn_setup()
    _L1_attn_in = {k: v for k, v in _L1_attn_all.items() if k in ('Wqkv', 'Wout', 'bout')}
    del _L1_attn_all

    def _L1_xattn_setup():
        import jax, jax.numpy as jnp
        import numpy as np
        B, C_LEN, Q_LEN, D = (8, 256, 64, 128)
        key = jax.random.key(seed)
        ks = jax.random.split(key, 10)
        scale = 1.0 / np.sqrt(D)
        return {'c': jax.random.normal(ks[0], (B, C_LEN, D), dtype=jnp.float32), 'q': jax.random.normal(ks[1], (B, Q_LEN, D), dtype=jnp.float32), 'w_cq': jax.random.normal(ks[2], (D,), dtype=jnp.float32) * scale, 'b_cq': jax.random.normal(ks[3], (), dtype=jnp.float32) * scale, 'w_c': jax.random.normal(ks[4], (D,), dtype=jnp.float32) * scale, 'b_c': jax.random.normal(ks[5], (), dtype=jnp.float32) * scale, 'w_q': jax.random.normal(ks[6], (D,), dtype=jnp.float32) * scale, 'b_q': jax.random.normal(ks[7], (), dtype=jnp.float32) * scale, 'W_l': jax.random.normal(ks[8], (D, 4 * D), dtype=jnp.float32) * (1.0 / np.sqrt(4 * D)), 'b_l': jax.random.normal(ks[9], (D,), dtype=jnp.float32) * (1.0 / np.sqrt(4 * D))}
    _L1_xattn_all = _L1_xattn_setup()
    _L1_xattn_in = {k: v for k, v in _L1_xattn_all.items() if k in ('w_cq', 'b_cq', 'w_c', 'b_c', 'w_q', 'b_q', 'W_l', 'b_l')}
    del _L1_xattn_all

    def _L1_ffn_setup():
        import jax, jax.numpy as jnp
        import numpy as np
        TOP_K = 2
        EPS = 1e-09
        key = jax.random.key(seed)
        ks = jax.random.split(key, 6)
        B, T, D, H, E = (4, 256, 128, 256, 8)
        x = jax.random.normal(ks[0], (B, T, D), dtype=jnp.float32)
        Wg = jax.random.normal(ks[1], (E, D), dtype=jnp.float32) * 0.02
        W1 = jax.random.normal(ks[2], (E, 2 * H, D), dtype=jnp.float32) * 0.02
        b1 = jax.random.normal(ks[3], (E, 2 * H), dtype=jnp.float32) * 0.02
        Wo = jax.random.normal(ks[4], (D, H), dtype=jnp.float32) * 0.02
        bo = jax.random.normal(ks[5], (D,), dtype=jnp.float32) * 0.02
        return {'x': x, 'Wg': Wg, 'W1': W1, 'b1': b1, 'Wo': Wo, 'bo': bo}
    _L1_ffn_all = _L1_ffn_setup()
    _L1_ffn_in = {k: v for k, v in _L1_ffn_all.items() if k in ('Wg', 'W1', 'b1', 'Wo', 'bo')}
    del _L1_ffn_all

    def _L2_attn_setup():
        import jax, jax.numpy as jnp
        import numpy as np
        H, DK, DV, CHUNK = (4, 32, 32, 32)

        def _silu(x):
            return x * jax.nn.sigmoid(x)

        def _l2norm(x, eps=1e-06):
            return x * jax.lax.rsqrt(jnp.sum(x * x, -1, keepdims=True) + eps)

        def _rmsnorm(x, w, eps=1e-05):
            return x * jax.lax.rsqrt(jnp.mean(x * x, -1, keepdims=True) + eps) * w

        def _causal_dwconv(x, w):
            C = x.shape[-1]
            K = w.shape[-1]
            xp = jnp.pad(x, ((0, 0), (K - 1, 0), (0, 0))).transpose(0, 2, 1)
            y = jax.lax.conv_general_dilated(xp, w[:, None, :], (1,), 'VALID', feature_group_count=C, dimension_numbers=('NCH', 'OIH', 'NCH'))
            return y.transpose(0, 2, 1)

        def _fir(x, filt):
            B, L, h, d = x.shape
            y = _causal_dwconv(x.reshape(B, L, h * d), filt.reshape(h * d, -1))
            return y.reshape(B, L, h, d)

        def _delta_rule_chunkwise(q, k, v, beta):
            b, h, L, dk = q.shape
            dv = v.shape[-1]
            n = L // CHUNK
            q = _l2norm(q)
            k = _l2norm(k)
            v = v * beta[..., None]
            k_beta = k * beta[..., None]
            rs = lambda t: t.reshape(b, h, n, CHUNK, -1)
            q, k, v, k_beta = (rs(q), rs(k), rs(v), rs(k_beta))
            eye = jnp.eye(CHUNK, dtype=q.dtype)
            strict_lower = jnp.tril(jnp.ones((CHUNK, CHUNK), bool), -1)
            A = jnp.where(strict_lower, jnp.einsum('bhncd,bhnsd->bhncs', k_beta, k), 0.0)
            attn_inv = jax.scipy.linalg.solve_triangular(eye + A, jnp.broadcast_to(eye, A.shape), lower=True)
            u = attn_inv @ v
            w = attn_inv @ k_beta
            incl_lower = jnp.tril(jnp.ones((CHUNK, CHUNK), bool))

            def step(S, inp):
                q_i, k_i, u_i, w_i = inp
                attn_local = jnp.where(incl_lower, q_i @ jnp.swapaxes(k_i, -1, -2), 0.0)
                u_t = u_i - w_i @ S
                o_i = q_i @ S + attn_local @ u_t
                return (S + jnp.swapaxes(k_i, -1, -2) @ u_t, o_i)
            S0 = jnp.zeros((b, h, dk, dv), q.dtype)
            xs = tuple((jnp.moveaxis(t, 2, 0) for t in (q, k, u, w)))
            S, out = jax.lax.scan(step, S0, xs)
            return (jnp.moveaxis(out, 0, 2).reshape(b, h, L, dv), S)

        def _stats(x):
            return jnp.stack([x.mean(-1), x.var(-1), jnp.abs(x).mean(-1), jnp.sqrt(jnp.sum(x * x, -1))], -1)

        def _forward(x, Wq, Wk, Wv, Wb, conv_q, conv_k, conv_v, fir_long, fir_short, W1, b1, W2, b2, log_temp, base_bias, conv_residual_logit, rms_w, Wo):
            B, L, D = x.shape
            q = _silu(_causal_dwconv(x @ Wq, conv_q)).reshape(B, L, H, DK)
            k = _silu(_causal_dwconv(x @ Wk, conv_k)).reshape(B, L, H, DK)
            v = _silu(_causal_dwconv(x @ Wv, conv_v)).reshape(B, L, H, DV)
            beta = jax.nn.sigmoid(x @ Wb)
            delta, _S = _delta_rule_chunkwise(q.transpose(0, 2, 1, 3), k.transpose(0, 2, 1, 3), v.transpose(0, 2, 1, 3), beta.transpose(0, 2, 1))
            delta = delta.transpose(0, 2, 1, 3)
            f_short = _fir(v, fir_short)
            f_long = _fir(v, fir_long)
            stats = jnp.concatenate([_stats(f_short), _stats(f_long), _stats(delta), _stats(v)], -1)
            hidden_exp = jnp.broadcast_to(x[:, :, None, :], (B, L, H, D))
            gate_in = jnp.concatenate([hidden_exp, stats], -1)
            h1 = jax.nn.gelu(gate_in @ W1 + b1, approximate=False)
            logits = h1 @ W2 + b2 + base_bias
            temp = jax.nn.softplus(log_temp) + 0.0001
            p = jax.nn.softmax(logits / temp[:, None], -1)
            eps = 0.05
            p = jnp.maximum(p, jnp.array([eps, eps, 0.0, 0.0], p.dtype))
            p = p / jnp.sum(p, -1, keepdims=True)
            o = p[..., 0:1] * f_short + p[..., 1:2] * f_long + p[..., 2:3] * delta + p[..., 3:4] * v
            o = o + 0.5 * jax.nn.sigmoid(conv_residual_logit)[None, None, :, None] * f_short
            o = _rmsnorm(o, rms_w)
            return o.reshape(B, L, H * DV) @ Wo
        key = jax.random.key(seed)
        ks = jax.random.split(key, 13)
        B, L, D = (2, 256, 128)
        f = jnp.float32
        n = lambda k, shape, s=0.02: jax.random.normal(k, shape, f) * s
        return {'x': jax.random.normal(ks[0], (B, L, D), f), 'Wq': n(ks[1], (D, D)), 'Wk': n(ks[2], (D, D)), 'Wv': n(ks[3], (D, D)), 'Wb': n(ks[4], (D, H)), 'conv_q': n(ks[5], (D, 4), 0.1), 'conv_k': n(ks[6], (D, 4), 0.1), 'conv_v': n(ks[7], (D, 4), 0.1), 'fir_long': n(ks[8], (H, DV, 64)), 'fir_short': n(ks[9], (H, DV, 5)), 'W1': n(ks[10], (D + 16, D)), 'b1': jnp.zeros((D,), f), 'W2': n(ks[11], (D, 4)), 'b2': jnp.zeros((4,), f), 'log_temp': jnp.full((H,), float(np.log(np.expm1(0.7))), f), 'base_bias': jnp.tile(jnp.array([-0.5, -0.5, 1.0, 3.0], f), (H, 1)), 'conv_residual_logit': jnp.full((H,), -2.0, f), 'rms_w': jnp.ones((DV,), f), 'Wo': n(ks[12], (D, D))}
    _L2_attn_all = _L2_attn_setup()
    _L2_attn_in = {k: v for k, v in _L2_attn_all.items() if k in ('Wq', 'Wk', 'Wv', 'Wb', 'conv_q', 'conv_k', 'conv_v', 'fir_long', 'fir_short', 'W1', 'b1', 'W2', 'b2', 'log_temp', 'base_bias', 'conv_residual_logit', 'rms_w', 'Wo')}
    del _L2_attn_all

    def _L2_xattn_setup():
        import jax, jax.numpy as jnp
        import numpy as np
        D_MODEL = 128
        N_HEADS = 16
        HEAD_DIM = D_MODEL // N_HEADS

        def sparsemax(x):
            x = x - jnp.max(x, axis=-1, keepdims=True)
            zs = -jnp.sort(-x, axis=-1)
            L = x.shape[-1]
            rho = jnp.arange(1, L + 1, dtype=x.dtype)
            cssv = jnp.cumsum(zs, axis=-1) - 1.0
            support = zs > cssv / rho
            k = jnp.maximum(jnp.sum(support, axis=-1, keepdims=True), 1)
            tau = jnp.take_along_axis(cssv, k - 1, axis=-1) / k.astype(x.dtype)
            return jnp.clip(x - tau, 0.0)

        def _split_heads(x):
            B, L, _ = x.shape
            return x.reshape(B, L, N_HEADS, HEAD_DIM).transpose(0, 2, 1, 3)
        key = jax.random.key(seed)
        ks = jax.random.split(key, 11)
        B, L = (2, 256)
        s = 0.02
        inp = {'q': jax.random.normal(ks[0], (B, L, D_MODEL), jnp.float32), 'k': jax.random.normal(ks[1], (B, L, D_MODEL), jnp.float32), 'v': jax.random.normal(ks[2], (B, L, D_MODEL), jnp.float32), 'Wq': jax.random.normal(ks[3], (D_MODEL, D_MODEL), jnp.float32) * s, 'bq': jnp.zeros((D_MODEL,), jnp.float32), 'Wk': jax.random.normal(ks[4], (D_MODEL, D_MODEL), jnp.float32) * s, 'bk': jnp.zeros((D_MODEL,), jnp.float32), 'Wv': jax.random.normal(ks[5], (D_MODEL, D_MODEL), jnp.float32) * s, 'bv': jnp.zeros((D_MODEL,), jnp.float32), 'Wo': jax.random.normal(ks[6], (D_MODEL, D_MODEL), jnp.float32) * s, 'bo': jnp.zeros((D_MODEL,), jnp.float32)}
        return inp
    _L2_xattn_all = _L2_xattn_setup()
    _L2_xattn_in = {k: v for k, v in _L2_xattn_all.items() if k in ('Wq', 'bq', 'Wk', 'bk', 'Wv', 'bv', 'Wo', 'bo')}
    del _L2_xattn_all

    def _L2_ffn_setup():
        import jax, jax.numpy as jnp
        import numpy as np
        NUM_EXPERTS = 8
        EXPERT_CAPACITY = 2.0
        key = jax.random.key(seed)
        k1, k2, k3, k4 = jax.random.split(key, 4)
        B, T, C, H, E = (4, 512, 128, 512, NUM_EXPERTS)
        x = jax.random.normal(k1, (B, T, C), jnp.float32)
        gate_w = jax.random.normal(k2, (C, E), jnp.float32) * 0.02
        w1 = jax.random.normal(k3, (E, C, H), jnp.float32) * 0.02
        w2 = jax.random.normal(k4, (E, H, C), jnp.float32) * 0.02
        return {'x': x, 'gate_w': gate_w, 'w1': w1, 'w2': w2}
    _L2_ffn_all = _L2_ffn_setup()
    _L2_ffn_in = {k: v for k, v in _L2_ffn_all.items() if k in ('gate_w', 'w1', 'w2')}
    del _L2_ffn_all

    def _L3_attn_setup():
        import jax, jax.numpy as jnp
        import numpy as np
        EPS = 1e-05
        H, N, F = (128, 16, 512)

        def layernorm(x, g, b):
            mu = jnp.mean(x, axis=-1, keepdims=True)
            var = jnp.mean(jnp.square(x - mu), axis=-1, keepdims=True)
            return (x - mu) * jax.lax.rsqrt(var + EPS) * g + b

        def _selective_ssm(xn, delta, Bm, Cm, A, D):
            Bsz = xn.shape[0]
            xs = (jnp.moveaxis(delta, 1, 0), jnp.moveaxis(Bm, 1, 0), jnp.moveaxis(Cm, 1, 0), jnp.moveaxis(xn, 1, 0))

            def step(h, t):
                d_t, b_t, c_t, x_t = t
                dA = jnp.exp(d_t[:, :, None] * A)
                dBx = d_t[:, :, None] * b_t[:, None, :] * x_t[:, :, None]
                h = dA * h + dBx
                y = jnp.einsum('bhn,bn->bh', h, c_t)
                return (h, y)
            h0 = jnp.zeros((Bsz, H, N), xn.dtype)
            _, ys = jax.lax.scan(step, h0, xs)
            y = jnp.moveaxis(ys, 0, 1)
            return y + D * xn
        key = jax.random.key(seed)
        ks = jax.random.split(key, 12)
        B, L = (2, 256)
        s = lambda fan_in: 1.0 / np.sqrt(fan_in)
        inp = {'x': jax.random.normal(ks[0], (B, L, H), jnp.float32), 'ln1_g': jnp.ones((H,), jnp.float32), 'ln1_b': jnp.zeros((H,), jnp.float32), 'Wd': jax.random.uniform(ks[1], (H, H), jnp.float32, -s(H), s(H)), 'bd': jnp.zeros((H,), jnp.float32), 'Wbc': jax.random.uniform(ks[2], (2 * N, H), jnp.float32, -s(H), s(H)), 'bbc': jnp.zeros((2 * N,), jnp.float32), 'A_log': jnp.log(jnp.tile(jnp.arange(1, N + 1, dtype=jnp.float32), (H, 1))), 'D': jnp.ones((H,), jnp.float32), 'ln2_g': jnp.ones((H,), jnp.float32), 'ln2_b': jnp.zeros((H,), jnp.float32), 'W1': jax.random.uniform(ks[3], (F, H), jnp.float32, -s(H), s(H)), 'b1': jnp.zeros((F,), jnp.float32), 'W2': jax.random.uniform(ks[4], (H, F), jnp.float32, -s(F), s(F)), 'b2': jnp.zeros((H,), jnp.float32)}
        return inp
    _L3_attn_all = _L3_attn_setup()
    _L3_attn_in = {k: v for k, v in _L3_attn_all.items() if k in ('ln1_g', 'ln1_b', 'Wd', 'bd', 'Wbc', 'bbc', 'A_log', 'D', 'ln2_g', 'ln2_b', 'W1', 'b1', 'W2', 'b2')}
    del _L3_attn_all

    def _L3_xattn_setup():
        import jax, jax.numpy as jnp
        import numpy as np
        from jax import lax
        BIG = jnp.float32(1e+30)

        def _pairwise_euclidean(a, b):
            aa = jnp.sum(a * a, axis=-1)[:, None]
            bb = jnp.sum(b * b, axis=-1)[None, :]
            ab = a @ b.T
            return jnp.sqrt(jnp.maximum(aa + bb - 2.0 * ab, 0.0))

        def _dtw_cost(D):
            row0 = jnp.cumsum(D[0])

            def row_step(prev_row, d_row):
                first = d_row[0] + prev_row[0]

                def col_step(left, inp):
                    d_ij, up, diag = inp
                    r = d_ij + jnp.minimum(jnp.minimum(up, left), diag)
                    return (r, r)
                _, rest = lax.scan(col_step, first, (d_row[1:], prev_row[1:], prev_row[:-1]))
                row = jnp.concatenate([first[None], rest])
                return (row, row)
            _, rows = lax.scan(row_step, row0, D[1:])
            return jnp.concatenate([row0[None], rows], axis=0)

        def _backtrack(R, T1, T2):
            L = T1 + T2 - 1

            def step(carry, _):
                i, j, done = carry
                valid = jnp.logical_not(done)
                cd = jnp.where((i > 0) & (j > 0), R[jnp.maximum(i - 1, 0), jnp.maximum(j - 1, 0)], BIG)
                cu = jnp.where(i > 0, R[jnp.maximum(i - 1, 0), j], BIG)
                cl = jnp.where(j > 0, R[i, jnp.maximum(j - 1, 0)], BIG)
                choice = jnp.argmin(jnp.stack([cd, cu, cl]))
                ni = jnp.where(choice <= 1, i - 1, i)
                nj = jnp.where((choice == 0) | (choice == 2), j - 1, j)
                at_origin = (i == 0) & (j == 0)
                ni = jnp.where(at_origin, 0, ni)
                nj = jnp.where(at_origin, 0, nj)
                return ((ni, nj, done | at_origin), (i, j, valid))
            init = (jnp.int32(T1 - 1), jnp.int32(T2 - 1), jnp.bool_(False))
            _, (i_idx, j_idx, valid) = lax.scan(step, init, None, length=L)
            return (i_idx, j_idx, valid)

        def _align_one(small, large):
            T_small, d = small.shape
            T_large = large.shape[0]
            D = _pairwise_euclidean(small, large)
            R = _dtw_cost(D)
            i_idx, j_idx, valid = _backtrack(R, T_small, T_large)
            contrib = small[i_idx] * valid[:, None].astype(small.dtype)
            expanded = jnp.zeros((T_large, d), dtype=small.dtype).at[j_idx].add(contrib)
            return expanded
        key = jax.random.key(seed)
        k1, k2 = jax.random.split(key)
        teacher = jax.random.normal(k1, (16, 50, 128), dtype=jnp.float32)
        student = jax.random.normal(k2, (16, 75, 128), dtype=jnp.float32)
        return {'teacher_features': teacher, 'student_features': student}
    _L3_xattn_all = _L3_xattn_setup()
    _L3_xattn_in = {k: v for k, v in _L3_xattn_all.items() if k in ()}
    del _L3_xattn_all

    def _L3_ffn_setup():
        import jax, jax.numpy as jnp
        import numpy as np
        B, T, D, H = (4, 256, 128, 256)
        E, S, K = (8, 2, 2)

        def _swiglu_stacked(x, w1, b1, w2, b2, w3, b3):
            p1 = jnp.einsum('btd,ndh->nbth', x, w1) + b1[:, None, None, :]
            p2 = jnp.einsum('btd,ndh->nbth', x, w2) + b2[:, None, None, :]
            glu = jax.nn.silu(p1) * p2
            return jnp.einsum('nbth,nhd->nbtd', glu, w3) + b3[:, None, None, :]
        key = jax.random.key(seed)
        ks = jax.random.split(key, 10)
        s = 0.02
        return {'x': jax.random.normal(ks[0], (B, T, D), jnp.float32), 'gate_w': jax.random.normal(ks[1], (D, E), jnp.float32) * s, 'gate_b': jnp.zeros((E,), jnp.float32), 'rw1': jax.random.normal(ks[2], (E, D, H), jnp.float32) * s, 'rb1': jnp.zeros((E, H), jnp.float32), 'rw2': jax.random.normal(ks[3], (E, D, H), jnp.float32) * s, 'rb2': jnp.zeros((E, H), jnp.float32), 'rw3': jax.random.normal(ks[4], (E, H, D), jnp.float32) * s, 'rb3': jnp.zeros((E, D), jnp.float32), 'sw1': jax.random.normal(ks[5], (S, D, H), jnp.float32) * s, 'sb1': jnp.zeros((S, H), jnp.float32), 'sw2': jax.random.normal(ks[6], (S, D, H), jnp.float32) * s, 'sb2': jnp.zeros((S, H), jnp.float32), 'sw3': jax.random.normal(ks[7], (S, H, D), jnp.float32) * s, 'sb3': jnp.zeros((S, D), jnp.float32)}
    _L3_ffn_all = _L3_ffn_setup()
    _L3_ffn_in = {k: v for k, v in _L3_ffn_all.items() if k in ('gate_w', 'gate_b', 'rw1', 'rb1', 'rw2', 'rb2', 'rw3', 'rb3', 'sw1', 'sb1', 'sw2', 'sb2', 'sw3', 'sb3')}
    del _L3_ffn_all
    return {'x': x, 'ctx_1024': ctx_1024, 'L0_attn_w_qkv': _L0_attn_in['w_qkv'], 'L0_attn_w_proj': _L0_attn_in['w_proj'], 'L0_attn_b_proj': _L0_attn_in['b_proj'], 'L0_ffn_g1': _L0_ffn_in['g1'], 'L0_ffn_g2': _L0_ffn_in['g2'], 'L0_ffn_w_down': _L0_ffn_in['w_down'], 'L0_ffn_wq': _L0_ffn_in['wq'], 'L0_ffn_wk': _L0_ffn_in['wk'], 'L0_ffn_wv': _L0_ffn_in['wv'], 'L0_ffn_w_up': _L0_ffn_in['w_up'], 'L0_ffn_router_w': _L0_ffn_in['router_w'], 'L0_ffn_w1': _L0_ffn_in['w1'], 'L0_ffn_w2': _L0_ffn_in['w2'], 'L0_ffn_w3': _L0_ffn_in['w3'], 'L1_attn_Wqkv': _L1_attn_in['Wqkv'], 'L1_attn_Wout': _L1_attn_in['Wout'], 'L1_attn_bout': _L1_attn_in['bout'], 'L1_xattn_w_cq': _L1_xattn_in['w_cq'], 'L1_xattn_b_cq': _L1_xattn_in['b_cq'], 'L1_xattn_w_c': _L1_xattn_in['w_c'], 'L1_xattn_b_c': _L1_xattn_in['b_c'], 'L1_xattn_w_q': _L1_xattn_in['w_q'], 'L1_xattn_b_q': _L1_xattn_in['b_q'], 'L1_xattn_W_l': _L1_xattn_in['W_l'], 'L1_xattn_b_l': _L1_xattn_in['b_l'], 'L1_ffn_Wg': _L1_ffn_in['Wg'], 'L1_ffn_W1': _L1_ffn_in['W1'], 'L1_ffn_b1': _L1_ffn_in['b1'], 'L1_ffn_Wo': _L1_ffn_in['Wo'], 'L1_ffn_bo': _L1_ffn_in['bo'], 'L2_attn_Wq': _L2_attn_in['Wq'], 'L2_attn_Wk': _L2_attn_in['Wk'], 'L2_attn_Wv': _L2_attn_in['Wv'], 'L2_attn_Wb': _L2_attn_in['Wb'], 'L2_attn_conv_q': _L2_attn_in['conv_q'], 'L2_attn_conv_k': _L2_attn_in['conv_k'], 'L2_attn_conv_v': _L2_attn_in['conv_v'], 'L2_attn_fir_long': _L2_attn_in['fir_long'], 'L2_attn_fir_short': _L2_attn_in['fir_short'], 'L2_attn_W1': _L2_attn_in['W1'], 'L2_attn_b1': _L2_attn_in['b1'], 'L2_attn_W2': _L2_attn_in['W2'], 'L2_attn_b2': _L2_attn_in['b2'], 'L2_attn_log_temp': _L2_attn_in['log_temp'], 'L2_attn_base_bias': _L2_attn_in['base_bias'], 'L2_attn_conv_residual_logit': _L2_attn_in['conv_residual_logit'], 'L2_attn_rms_w': _L2_attn_in['rms_w'], 'L2_attn_Wo': _L2_attn_in['Wo'], 'L2_xattn_Wq': _L2_xattn_in['Wq'], 'L2_xattn_bq': _L2_xattn_in['bq'], 'L2_xattn_Wk': _L2_xattn_in['Wk'], 'L2_xattn_bk': _L2_xattn_in['bk'], 'L2_xattn_Wv': _L2_xattn_in['Wv'], 'L2_xattn_bv': _L2_xattn_in['bv'], 'L2_xattn_Wo': _L2_xattn_in['Wo'], 'L2_xattn_bo': _L2_xattn_in['bo'], 'L2_ffn_gate_w': _L2_ffn_in['gate_w'], 'L2_ffn_w1': _L2_ffn_in['w1'], 'L2_ffn_w2': _L2_ffn_in['w2'], 'L3_attn_ln1_g': _L3_attn_in['ln1_g'], 'L3_attn_ln1_b': _L3_attn_in['ln1_b'], 'L3_attn_Wd': _L3_attn_in['Wd'], 'L3_attn_bd': _L3_attn_in['bd'], 'L3_attn_Wbc': _L3_attn_in['Wbc'], 'L3_attn_bbc': _L3_attn_in['bbc'], 'L3_attn_A_log': _L3_attn_in['A_log'], 'L3_attn_D': _L3_attn_in['D'], 'L3_attn_ln2_g': _L3_attn_in['ln2_g'], 'L3_attn_ln2_b': _L3_attn_in['ln2_b'], 'L3_attn_W1': _L3_attn_in['W1'], 'L3_attn_b1': _L3_attn_in['b1'], 'L3_attn_W2': _L3_attn_in['W2'], 'L3_attn_b2': _L3_attn_in['b2'], 'L3_ffn_gate_w': _L3_ffn_in['gate_w'], 'L3_ffn_gate_b': _L3_ffn_in['gate_b'], 'L3_ffn_rw1': _L3_ffn_in['rw1'], 'L3_ffn_rb1': _L3_ffn_in['rb1'], 'L3_ffn_rw2': _L3_ffn_in['rw2'], 'L3_ffn_rb2': _L3_ffn_in['rb2'], 'L3_ffn_rw3': _L3_ffn_in['rw3'], 'L3_ffn_rb3': _L3_ffn_in['rb3'], 'L3_ffn_sw1': _L3_ffn_in['sw1'], 'L3_ffn_sb1': _L3_ffn_in['sb1'], 'L3_ffn_sw2': _L3_ffn_in['sw2'], 'L3_ffn_sb2': _L3_ffn_in['sb2'], 'L3_ffn_sw3': _L3_ffn_in['sw3'], 'L3_ffn_sb3': _L3_ffn_in['sb3']}

def reference(x, ctx_1024, L0_attn_w_qkv, L0_attn_w_proj, L0_attn_b_proj, L0_ffn_g1, L0_ffn_g2, L0_ffn_w_down, L0_ffn_wq, L0_ffn_wk, L0_ffn_wv, L0_ffn_w_up, L0_ffn_router_w, L0_ffn_w1, L0_ffn_w2, L0_ffn_w3, L1_attn_Wqkv, L1_attn_Wout, L1_attn_bout, L1_xattn_w_cq, L1_xattn_b_cq, L1_xattn_w_c, L1_xattn_b_c, L1_xattn_w_q, L1_xattn_b_q, L1_xattn_W_l, L1_xattn_b_l, L1_ffn_Wg, L1_ffn_W1, L1_ffn_b1, L1_ffn_Wo, L1_ffn_bo, L2_attn_Wq, L2_attn_Wk, L2_attn_Wv, L2_attn_Wb, L2_attn_conv_q, L2_attn_conv_k, L2_attn_conv_v, L2_attn_fir_long, L2_attn_fir_short, L2_attn_W1, L2_attn_b1, L2_attn_W2, L2_attn_b2, L2_attn_log_temp, L2_attn_base_bias, L2_attn_conv_residual_logit, L2_attn_rms_w, L2_attn_Wo, L2_xattn_Wq, L2_xattn_bq, L2_xattn_Wk, L2_xattn_bk, L2_xattn_Wv, L2_xattn_bv, L2_xattn_Wo, L2_xattn_bo, L2_ffn_gate_w, L2_ffn_w1, L2_ffn_w2, L3_attn_ln1_g, L3_attn_ln1_b, L3_attn_Wd, L3_attn_bd, L3_attn_Wbc, L3_attn_bbc, L3_attn_A_log, L3_attn_D, L3_attn_ln2_g, L3_attn_ln2_b, L3_attn_W1, L3_attn_b1, L3_attn_W2, L3_attn_b2, L3_ffn_gate_w, L3_ffn_gate_b, L3_ffn_rw1, L3_ffn_rb1, L3_ffn_rw2, L3_ffn_rb2, L3_ffn_rw3, L3_ffn_rb3, L3_ffn_sw1, L3_ffn_sb1, L3_ffn_sw2, L3_ffn_sb2, L3_ffn_sw3, L3_ffn_sb3):
    import jax
    import jax.numpy as jnp

    def _L0_attn_ref(x, w_qkv, w_proj, b_proj):
        import jax, jax.numpy as jnp
        import numpy as np
        B, N, DIM = (2, 256, 128)
        H = 16
        HD = DIM // H
        b, n, c = x.shape
        scale = HD ** (-0.5)
        qkv = jnp.einsum('bnc,cd->bnd', x, w_qkv)
        qkv = qkv.reshape(b, n, 3, H, HD).transpose(2, 0, 3, 1, 4)
        q, k, v = (qkv[0], qkv[1], qkv[2])
        q = q * scale
        attn = jnp.einsum('bhnd,bhmd->bhnm', q, k)
        attn = jax.nn.softmax(attn, axis=-1)
        out = jnp.einsum('bhnm,bhmd->bhnd', attn, v)
        out = out.transpose(0, 2, 1, 3).reshape(b, n, c)
        return jnp.einsum('bnc,cd->bnd', out, w_proj) + b_proj

    def _L0_xattn_ref(q, k, v):
        import jax, jax.numpy as jnp
        import numpy as np
        B, S, D = (4, 256, 128)
        d = q.shape[-1]
        scores = jnp.einsum('bik,bjk->bij', q, k) / jnp.sqrt(jnp.asarray(d, q.dtype))
        attn = jax.nn.softmax(scores, axis=-1)
        out = jnp.einsum('bij,bjk->bik', attn, v)
        return out

    def _L0_ffn_ref(x, g1, g2, w_down, wq, wk, wv, w_up, router_w, w1, w2, w3):
        import jax, jax.numpy as jnp
        import numpy as np
        B, S, D = (2, 128, 128)
        L, H = (64, 16)
        HD = L // H
        F, E, K = (256, 8, 2)
        THETA = 10000.0
        EPS = 1e-05

        def _rmsnorm(x, g):
            return x * g * jax.lax.rsqrt(jnp.mean(x * x, axis=-1, keepdims=True) + EPS)

        def _rope(t, pos):
            inv_freq = 1.0 / THETA ** (jnp.arange(0, HD, 2, dtype=jnp.float32) / HD)
            ang = pos[:, None].astype(jnp.float32) * inv_freq[None, :]
            cos, sin = (jnp.cos(ang), jnp.sin(ang))
            t1, t2 = (t[..., 0::2], t[..., 1::2])
            r1 = t1 * cos - t2 * sin
            r2 = t1 * sin + t2 * cos
            return jnp.stack([r1, r2], axis=-1).reshape(t.shape)

        def _forward(x, g1, g2, w_down, wq, wk, wv, w_up, router_w, w1, w2, w3):
            b, s, _ = x.shape
            pos = jnp.arange(s)
            h = _rmsnorm(x, g1)
            c = h @ w_down
            split = lambda t: t.reshape(b, s, H, HD).transpose(0, 2, 1, 3)
            q = _rope(split(c @ wq), pos)
            k = _rope(split(c @ wk), pos)
            v = split(c @ wv)
            scores = jnp.einsum('bhqd,bhkd->bhqk', q, k) / jnp.sqrt(jnp.float32(HD))
            causal = jnp.tril(jnp.ones((s, s), bool))
            scores = jnp.where(causal, scores, -jnp.inf)
            attn = jax.nn.softmax(scores, axis=-1)
            o = jnp.einsum('bhqk,bhkd->bhqd', attn, v).transpose(0, 2, 1, 3).reshape(b, s, L)
            x = x + o @ w_up
            res = x
            t = _rmsnorm(x, g2).reshape(-1, D)
            probs = jax.nn.softmax(t @ router_w, axis=-1)
            vals, idx = jax.lax.top_k(probs, K)
            w = vals / jnp.sum(vals, axis=-1, keepdims=True)
            gate = jnp.sum(jax.nn.one_hot(idx, E, dtype=t.dtype) * w[..., None], axis=1)
            hid = jax.nn.silu(jnp.einsum('td,edf->tef', t, w1)) * jnp.einsum('td,edf->tef', t, w3)
            y_e = jnp.einsum('tef,efd->ted', hid, w2)
            y = jnp.einsum('ted,te->td', y_e, gate)
            return res + y.reshape(b, s, D)
        return _forward(x, g1, g2, w_down, wq, wk, wv, w_up, router_w, w1, w2, w3)

    def _L1_attn_ref(X, Wqkv, Wout, bout):
        import jax, jax.numpy as jnp
        import numpy as np
        NUM_HEADS = 16
        ROPE_BASE = 10000.0

        def _rotate_half(x):
            xr = x.reshape(*x.shape[:-1], -1, 2)
            x1, x2 = (xr[..., 0], xr[..., 1])
            return jnp.stack((-x2, x1), axis=-1).reshape(x.shape)

        def _rope(x):
            hd = x.shape[-1]
            n = x.shape[-2]
            inv_freq = 1.0 / ROPE_BASE ** (jnp.arange(0, hd, 2, dtype=jnp.float32) / hd)
            freqs = jnp.outer(jnp.arange(n, dtype=jnp.float32), inv_freq)
            freqs = jnp.repeat(freqs, 2, axis=-1)
            return x * jnp.cos(freqs) + _rotate_half(x) * jnp.sin(freqs)
        B, N, D = X.shape
        H = NUM_HEADS
        hd = D // H
        scale = hd ** (-0.5)
        qkv = X @ Wqkv
        q, k, v = jnp.split(qkv, 3, axis=-1)

        def to_heads(t):
            return t.reshape(B, N, H, hd).transpose(0, 2, 1, 3)
        Q, K, V = (to_heads(q), to_heads(k), to_heads(v))
        Q = _rope(Q)
        K = _rope(K)
        scores = jnp.einsum('bhnd,bhmd->bhnm', Q, K) * scale
        causal = jnp.tril(jnp.ones((N, N), dtype=bool))
        scores = jnp.where(causal, scores, -jnp.inf)
        attn = jax.nn.softmax(scores, axis=-1)
        out = jnp.einsum('bhnm,bhmd->bhnd', attn, V)
        out = out.transpose(0, 2, 1, 3).reshape(B, N, D)
        return out @ Wout + bout

    def _L1_xattn_ref(c, q, w_cq, b_cq, w_c, b_c, w_q, b_q, W_l, b_l):
        import jax, jax.numpy as jnp
        import numpy as np
        B, C_LEN, Q_LEN, D = (8, 256, 64, 128)
        cq = jnp.einsum('bcd,bqd,d->bcq', c, q, w_cq) + b_cq
        s = (c @ w_c + b_c)[:, :, None] + (q @ w_q + b_q)[:, None, :] + cq
        a = jax.nn.softmax(s, axis=2)
        c2q_att = jnp.einsum('bcq,bqd->bcd', a, q)
        b_att = jax.nn.softmax(jnp.max(s, axis=2), axis=1)
        q2c_att = jnp.einsum('bc,bcd->bd', b_att, c)[:, None, :]
        x = jnp.concatenate([c, c2q_att, c * c2q_att, c * q2c_att], axis=-1)
        z = x @ W_l.T + b_l
        return z

    def _L1_ffn_ref(x, Wg, W1, b1, Wo, bo):
        import jax, jax.numpy as jnp
        import numpy as np
        TOP_K = 2
        EPS = 1e-09
        E = Wg.shape[0]
        gate_logits = jnp.einsum('btd,ed->bte', x, Wg)
        gate_scores = jax.nn.softmax(gate_logits, axis=-1)
        topk_val, topk_idx = jax.lax.top_k(gate_scores, TOP_K)
        topk_val = topk_val / (topk_val.sum(axis=-1, keepdims=True) + EPS)
        comb = (jax.nn.one_hot(topk_idx, E, dtype=x.dtype) * topk_val[..., None]).sum(axis=-2)
        out = jnp.zeros_like(x)
        for e in range(E):
            h = jnp.einsum('btd,hd->bth', x, W1[e]) + b1[e]
            a, b = jnp.split(h, 2, axis=-1)
            g = a * jax.nn.sigmoid(b)
            eo = jnp.einsum('bth,dh->btd', g, Wo) + bo
            out = out + eo * comb[..., e:e + 1]
        return out

    def _L2_attn_ref(x, Wq, Wk, Wv, Wb, conv_q, conv_k, conv_v, fir_long, fir_short, W1, b1, W2, b2, log_temp, base_bias, conv_residual_logit, rms_w, Wo):
        import jax, jax.numpy as jnp
        import numpy as np
        H, DK, DV, CHUNK = (4, 32, 32, 32)

        def _silu(x):
            return x * jax.nn.sigmoid(x)

        def _l2norm(x, eps=1e-06):
            return x * jax.lax.rsqrt(jnp.sum(x * x, -1, keepdims=True) + eps)

        def _rmsnorm(x, w, eps=1e-05):
            return x * jax.lax.rsqrt(jnp.mean(x * x, -1, keepdims=True) + eps) * w

        def _causal_dwconv(x, w):
            C = x.shape[-1]
            K = w.shape[-1]
            xp = jnp.pad(x, ((0, 0), (K - 1, 0), (0, 0))).transpose(0, 2, 1)
            y = jax.lax.conv_general_dilated(xp, w[:, None, :], (1,), 'VALID', feature_group_count=C, dimension_numbers=('NCH', 'OIH', 'NCH'))
            return y.transpose(0, 2, 1)

        def _fir(x, filt):
            B, L, h, d = x.shape
            y = _causal_dwconv(x.reshape(B, L, h * d), filt.reshape(h * d, -1))
            return y.reshape(B, L, h, d)

        def _delta_rule_chunkwise(q, k, v, beta):
            b, h, L, dk = q.shape
            dv = v.shape[-1]
            n = L // CHUNK
            q = _l2norm(q)
            k = _l2norm(k)
            v = v * beta[..., None]
            k_beta = k * beta[..., None]
            rs = lambda t: t.reshape(b, h, n, CHUNK, -1)
            q, k, v, k_beta = (rs(q), rs(k), rs(v), rs(k_beta))
            eye = jnp.eye(CHUNK, dtype=q.dtype)
            strict_lower = jnp.tril(jnp.ones((CHUNK, CHUNK), bool), -1)
            A = jnp.where(strict_lower, jnp.einsum('bhncd,bhnsd->bhncs', k_beta, k), 0.0)
            attn_inv = jax.scipy.linalg.solve_triangular(eye + A, jnp.broadcast_to(eye, A.shape), lower=True)
            u = attn_inv @ v
            w = attn_inv @ k_beta
            incl_lower = jnp.tril(jnp.ones((CHUNK, CHUNK), bool))

            def step(S, inp):
                q_i, k_i, u_i, w_i = inp
                attn_local = jnp.where(incl_lower, q_i @ jnp.swapaxes(k_i, -1, -2), 0.0)
                u_t = u_i - w_i @ S
                o_i = q_i @ S + attn_local @ u_t
                return (S + jnp.swapaxes(k_i, -1, -2) @ u_t, o_i)
            S0 = jnp.zeros((b, h, dk, dv), q.dtype)
            xs = tuple((jnp.moveaxis(t, 2, 0) for t in (q, k, u, w)))
            S, out = jax.lax.scan(step, S0, xs)
            return (jnp.moveaxis(out, 0, 2).reshape(b, h, L, dv), S)

        def _stats(x):
            return jnp.stack([x.mean(-1), x.var(-1), jnp.abs(x).mean(-1), jnp.sqrt(jnp.sum(x * x, -1))], -1)

        def _forward(x, Wq, Wk, Wv, Wb, conv_q, conv_k, conv_v, fir_long, fir_short, W1, b1, W2, b2, log_temp, base_bias, conv_residual_logit, rms_w, Wo):
            B, L, D = x.shape
            q = _silu(_causal_dwconv(x @ Wq, conv_q)).reshape(B, L, H, DK)
            k = _silu(_causal_dwconv(x @ Wk, conv_k)).reshape(B, L, H, DK)
            v = _silu(_causal_dwconv(x @ Wv, conv_v)).reshape(B, L, H, DV)
            beta = jax.nn.sigmoid(x @ Wb)
            delta, _S = _delta_rule_chunkwise(q.transpose(0, 2, 1, 3), k.transpose(0, 2, 1, 3), v.transpose(0, 2, 1, 3), beta.transpose(0, 2, 1))
            delta = delta.transpose(0, 2, 1, 3)
            f_short = _fir(v, fir_short)
            f_long = _fir(v, fir_long)
            stats = jnp.concatenate([_stats(f_short), _stats(f_long), _stats(delta), _stats(v)], -1)
            hidden_exp = jnp.broadcast_to(x[:, :, None, :], (B, L, H, D))
            gate_in = jnp.concatenate([hidden_exp, stats], -1)
            h1 = jax.nn.gelu(gate_in @ W1 + b1, approximate=False)
            logits = h1 @ W2 + b2 + base_bias
            temp = jax.nn.softplus(log_temp) + 0.0001
            p = jax.nn.softmax(logits / temp[:, None], -1)
            eps = 0.05
            p = jnp.maximum(p, jnp.array([eps, eps, 0.0, 0.0], p.dtype))
            p = p / jnp.sum(p, -1, keepdims=True)
            o = p[..., 0:1] * f_short + p[..., 1:2] * f_long + p[..., 2:3] * delta + p[..., 3:4] * v
            o = o + 0.5 * jax.nn.sigmoid(conv_residual_logit)[None, None, :, None] * f_short
            o = _rmsnorm(o, rms_w)
            return o.reshape(B, L, H * DV) @ Wo
        return _forward(x, Wq, Wk, Wv, Wb, conv_q, conv_k, conv_v, fir_long, fir_short, W1, b1, W2, b2, log_temp, base_bias, conv_residual_logit, rms_w, Wo)

    def _L2_xattn_ref(q, k, v, Wq, bq, Wk, bk, Wv, bv, Wo, bo):
        import jax, jax.numpy as jnp
        import numpy as np
        D_MODEL = 128
        N_HEADS = 16
        HEAD_DIM = D_MODEL // N_HEADS

        def sparsemax(x):
            x = x - jnp.max(x, axis=-1, keepdims=True)
            zs = -jnp.sort(-x, axis=-1)
            L = x.shape[-1]
            rho = jnp.arange(1, L + 1, dtype=x.dtype)
            cssv = jnp.cumsum(zs, axis=-1) - 1.0
            support = zs > cssv / rho
            k = jnp.maximum(jnp.sum(support, axis=-1, keepdims=True), 1)
            tau = jnp.take_along_axis(cssv, k - 1, axis=-1) / k.astype(x.dtype)
            return jnp.clip(x - tau, 0.0)

        def _split_heads(x):
            B, L, _ = x.shape
            return x.reshape(B, L, N_HEADS, HEAD_DIM).transpose(0, 2, 1, 3)
        qh = _split_heads(q @ Wq + bq)
        kh = _split_heads(k @ Wk + bk)
        vh = _split_heads(v @ Wv + bv)
        scale = HEAD_DIM ** (-0.5)
        scores = jnp.einsum('bhqd,bhkd->bhqk', qh, kh) * scale
        attn = sparsemax(scores)
        out = jnp.einsum('bhqk,bhkd->bhqd', attn, vh)
        B, L = (q.shape[0], q.shape[1])
        out = out.transpose(0, 2, 1, 3).reshape(B, L, D_MODEL)
        return out @ Wo + bo

    def _L2_ffn_ref(x, gate_w, w1, w2):
        import jax, jax.numpy as jnp
        import numpy as np
        NUM_EXPERTS = 8
        EXPERT_CAPACITY = 2.0
        B, T, C = x.shape
        E = gate_w.shape[1]
        cap = int(EXPERT_CAPACITY * T / E)
        scores = jnp.einsum('BTC,CE->BTE', x, gate_w)
        probs = jax.nn.softmax(scores, axis=-1)
        probs_et = jnp.transpose(probs, (0, 2, 1))
        top_p, top_idx = jax.lax.top_k(probs_et, cap)
        xin = jnp.take_along_axis(x[:, None, :, :], top_idx[..., None], axis=2)
        h = jax.nn.gelu(jnp.einsum('BElC,ECH->BElH', xin, w1), approximate=False)
        y = jnp.einsum('BElH,EHC->BElC', h, w2)
        y = y * top_p[..., None]
        b_idx = jnp.arange(B)[:, None, None]
        out = jnp.zeros((B, T, C), x.dtype).at[b_idx, top_idx].add(y)
        return out

    def _L3_attn_ref(x, ln1_g, ln1_b, Wd, bd, Wbc, bbc, A_log, D, ln2_g, ln2_b, W1, b1, W2, b2):
        import jax, jax.numpy as jnp
        import numpy as np
        EPS = 1e-05
        H, N, F = (128, 16, 512)

        def layernorm(x, g, b):
            mu = jnp.mean(x, axis=-1, keepdims=True)
            var = jnp.mean(jnp.square(x - mu), axis=-1, keepdims=True)
            return (x - mu) * jax.lax.rsqrt(var + EPS) * g + b

        def _selective_ssm(xn, delta, Bm, Cm, A, D):
            Bsz = xn.shape[0]
            xs = (jnp.moveaxis(delta, 1, 0), jnp.moveaxis(Bm, 1, 0), jnp.moveaxis(Cm, 1, 0), jnp.moveaxis(xn, 1, 0))

            def step(h, t):
                d_t, b_t, c_t, x_t = t
                dA = jnp.exp(d_t[:, :, None] * A)
                dBx = d_t[:, :, None] * b_t[:, None, :] * x_t[:, :, None]
                h = dA * h + dBx
                y = jnp.einsum('bhn,bn->bh', h, c_t)
                return (h, y)
            h0 = jnp.zeros((Bsz, H, N), xn.dtype)
            _, ys = jax.lax.scan(step, h0, xs)
            y = jnp.moveaxis(ys, 0, 1)
            return y + D * xn
        xn = layernorm(x, ln1_g, ln1_b)
        delta = jax.nn.softplus(xn @ Wd.T + bd)
        bc = xn @ Wbc.T + bbc
        Bm, Cm = (bc[..., :N], bc[..., N:])
        A = -jnp.exp(A_log)
        ssm_out = x + _selective_ssm(xn, delta, Bm, Cm, A, D)
        normed = layernorm(ssm_out, ln2_g, ln2_b)
        hff = jax.nn.gelu(normed @ W1.T + b1, approximate=False)
        ffn_out = hff @ W2.T + b2
        return ffn_out + ssm_out

    def _L3_xattn_ref(teacher_features, student_features):
        import jax, jax.numpy as jnp
        import numpy as np
        from jax import lax
        BIG = jnp.float32(1e+30)

        def _pairwise_euclidean(a, b):
            aa = jnp.sum(a * a, axis=-1)[:, None]
            bb = jnp.sum(b * b, axis=-1)[None, :]
            ab = a @ b.T
            return jnp.sqrt(jnp.maximum(aa + bb - 2.0 * ab, 0.0))

        def _dtw_cost(D):
            row0 = jnp.cumsum(D[0])

            def row_step(prev_row, d_row):
                first = d_row[0] + prev_row[0]

                def col_step(left, inp):
                    d_ij, up, diag = inp
                    r = d_ij + jnp.minimum(jnp.minimum(up, left), diag)
                    return (r, r)
                _, rest = lax.scan(col_step, first, (d_row[1:], prev_row[1:], prev_row[:-1]))
                row = jnp.concatenate([first[None], rest])
                return (row, row)
            _, rows = lax.scan(row_step, row0, D[1:])
            return jnp.concatenate([row0[None], rows], axis=0)

        def _backtrack(R, T1, T2):
            L = T1 + T2 - 1

            def step(carry, _):
                i, j, done = carry
                valid = jnp.logical_not(done)
                cd = jnp.where((i > 0) & (j > 0), R[jnp.maximum(i - 1, 0), jnp.maximum(j - 1, 0)], BIG)
                cu = jnp.where(i > 0, R[jnp.maximum(i - 1, 0), j], BIG)
                cl = jnp.where(j > 0, R[i, jnp.maximum(j - 1, 0)], BIG)
                choice = jnp.argmin(jnp.stack([cd, cu, cl]))
                ni = jnp.where(choice <= 1, i - 1, i)
                nj = jnp.where((choice == 0) | (choice == 2), j - 1, j)
                at_origin = (i == 0) & (j == 0)
                ni = jnp.where(at_origin, 0, ni)
                nj = jnp.where(at_origin, 0, nj)
                return ((ni, nj, done | at_origin), (i, j, valid))
            init = (jnp.int32(T1 - 1), jnp.int32(T2 - 1), jnp.bool_(False))
            _, (i_idx, j_idx, valid) = lax.scan(step, init, None, length=L)
            return (i_idx, j_idx, valid)

        def _align_one(small, large):
            T_small, d = small.shape
            T_large = large.shape[0]
            D = _pairwise_euclidean(small, large)
            R = _dtw_cost(D)
            i_idx, j_idx, valid = _backtrack(R, T_small, T_large)
            contrib = small[i_idx] * valid[:, None].astype(small.dtype)
            expanded = jnp.zeros((T_large, d), dtype=small.dtype).at[j_idx].add(contrib)
            return expanded
        return jax.vmap(_align_one)(teacher_features, student_features)

    def _L3_ffn_ref(x, gate_w, gate_b, rw1, rb1, rw2, rb2, rw3, rb3, sw1, sb1, sw2, sb2, sw3, sb3):
        import jax, jax.numpy as jnp
        import numpy as np
        B, T, D, H = (4, 256, 128, 256)
        E, S, K = (8, 2, 2)

        def _swiglu_stacked(x, w1, b1, w2, b2, w3, b3):
            p1 = jnp.einsum('btd,ndh->nbth', x, w1) + b1[:, None, None, :]
            p2 = jnp.einsum('btd,ndh->nbth', x, w2) + b2[:, None, None, :]
            glu = jax.nn.silu(p1) * p2
            return jnp.einsum('nbth,nhd->nbtd', glu, w3) + b3[:, None, None, :]
        scores = jax.nn.softmax(x @ gate_w + gate_b, axis=-1)
        weights, indices = jax.lax.top_k(scores, K)
        routed_all = _swiglu_stacked(x, rw1, rb1, rw2, rb2, rw3, rb3)
        out_bted = jnp.transpose(routed_all, (1, 2, 0, 3))
        gathered = jnp.take_along_axis(out_bted, indices[..., None], axis=2)
        routed = jnp.sum(weights[..., None] * gathered, axis=2)
        shared = _swiglu_stacked(x, sw1, sb1, sw2, sb2, sw3, sb3).mean(axis=0)
        return shared + routed
    x = x + _L0_attn_ref(_layernorm(x, axis=-1), L0_attn_w_qkv, L0_attn_w_proj, L0_attn_b_proj)
    x = x + _L0_xattn_ref(_layernorm(x, axis=-1), ctx_1024, ctx_1024)
    x = x + _L0_ffn_ref(_layernorm(x, axis=-1), L0_ffn_g1, L0_ffn_g2, L0_ffn_w_down, L0_ffn_wq, L0_ffn_wk, L0_ffn_wv, L0_ffn_w_up, L0_ffn_router_w, L0_ffn_w1, L0_ffn_w2, L0_ffn_w3)
    x = x + _L1_attn_ref(_layernorm(x, axis=-1), L1_attn_Wqkv, L1_attn_Wout, L1_attn_bout)
    x = x + _L1_xattn_ref(_layernorm(x, axis=-1), ctx_1024, L1_xattn_w_cq, L1_xattn_b_cq, L1_xattn_w_c, L1_xattn_b_c, L1_xattn_w_q, L1_xattn_b_q, L1_xattn_W_l, L1_xattn_b_l)
    x = x + _L1_ffn_ref(_layernorm(x, axis=-1), L1_ffn_Wg, L1_ffn_W1, L1_ffn_b1, L1_ffn_Wo, L1_ffn_bo)
    x = x + _L2_attn_ref(_layernorm(x, axis=-1), L2_attn_Wq, L2_attn_Wk, L2_attn_Wv, L2_attn_Wb, L2_attn_conv_q, L2_attn_conv_k, L2_attn_conv_v, L2_attn_fir_long, L2_attn_fir_short, L2_attn_W1, L2_attn_b1, L2_attn_W2, L2_attn_b2, L2_attn_log_temp, L2_attn_base_bias, L2_attn_conv_residual_logit, L2_attn_rms_w, L2_attn_Wo)
    x = x + _L2_xattn_ref(_layernorm(x, axis=-1), ctx_1024, ctx_1024, L2_xattn_Wq, L2_xattn_bq, L2_xattn_Wk, L2_xattn_bk, L2_xattn_Wv, L2_xattn_bv, L2_xattn_Wo, L2_xattn_bo)
    x = x + _L2_ffn_ref(_layernorm(x, axis=-1), L2_ffn_gate_w, L2_ffn_w1, L2_ffn_w2)
    x = x + _L3_attn_ref(_layernorm(x, axis=-1), L3_attn_ln1_g, L3_attn_ln1_b, L3_attn_Wd, L3_attn_bd, L3_attn_Wbc, L3_attn_bbc, L3_attn_A_log, L3_attn_D, L3_attn_ln2_g, L3_attn_ln2_b, L3_attn_W1, L3_attn_b1, L3_attn_W2, L3_attn_b2)
    x = x + _L3_xattn_ref(ctx_1024, _layernorm(x, axis=-1))
    x = x + _L3_ffn_ref(_layernorm(x, axis=-1), L3_ffn_gate_w, L3_ffn_gate_b, L3_ffn_rw1, L3_ffn_rb1, L3_ffn_rw2, L3_ffn_rb2, L3_ffn_rw3, L3_ffn_rb3, L3_ffn_sw1, L3_ffn_sb1, L3_ffn_sw2, L3_ffn_sb2, L3_ffn_sw3, L3_ffn_sb3)
    return x

_drawn_inputs = setup_inputs


def setup_inputs(seed=0):
    import zlib

    import numpy as np

    out = dict(_drawn_inputs(seed))
    spreads = {'L0_ffn_g1': (1.0, 0.6),
     'L0_ffn_g2': (1.0, 0.6),
     'L1_attn_bout': (0.0, 0.1),
     'L2_attn_b1': (0.0, 0.8),
     'L2_attn_b2': (0.0, 0.8),
     'L2_attn_log_temp': (0.013658997602760792, 0.6),
     'L2_attn_conv_residual_logit': (-2.0, 0.6),
     'L2_attn_rms_w': (1.0, 0.538),
     'L2_xattn_bq': (0.0, 0.8),
     'L2_xattn_bk': (0.0, 2.0),
     'L2_xattn_bv': (0.0, 0.644),
     'L2_xattn_bo': (0.0, 0.1),
     'L3_attn_ln1_g': (1.0, 0.2),
     'L3_attn_ln1_b': (0.0, 0.1),
     'L3_attn_bd': (0.0, 0.35),
     'L3_attn_bbc': (0.0, 0.1),
     'L3_attn_D': (1.0, 0.2),
     'L3_attn_ln2_g': (1.0, 0.6),
     'L3_attn_ln2_b': (0.0, 0.8),
     'L3_attn_b1': (0.0, 0.408),
     'L3_attn_b2': (0.0, 0.274),
     'L3_ffn_gate_b': (0.0, 0.8),
     'L3_ffn_rb1': (0.0, 0.8),
     'L3_ffn_rb2': (0.0, 0.8),
     'L3_ffn_rb3': (0.0, 0.8),
     'L3_ffn_sb1': (0.0, 0.8),
     'L3_ffn_sb2': (0.0, 0.8),
     'L3_ffn_sb3': (0.0, 0.555)}
    factors = {'L0_ffn_w_down': 8.0,
     'L0_ffn_wq': 8.0,
     'L0_ffn_wk': 8.0,
     'L0_ffn_wv': 8.0,
     'L0_ffn_w_up': 8.0,
     'L0_ffn_router_w': 8.0,
     'L0_ffn_w1': 8.0,
     'L0_ffn_w2': 2.991,
     'L0_ffn_w3': 3.113,
     'L1_ffn_Wg': 4.981,
     'L1_ffn_W1': 5.221,
     'L1_ffn_b1': 3.149,
     'L1_ffn_Wo': 4.481,
     'L2_attn_Wq': 8.0,
     'L2_attn_Wk': 8.0,
     'L2_attn_Wb': 8.0,
     'L2_attn_conv_q': 8.0,
     'L2_attn_conv_k': 8.0,
     'L2_attn_fir_long': 8.0,
     'L2_attn_fir_short': 9.408,
     'L2_attn_W1': 8.0,
     'L2_attn_W2': 8.0,
     'L2_xattn_Wq': 4.463,
     'L2_xattn_Wv': 3.105,
     'L2_ffn_gate_w': 8.0,
     'L2_ffn_w1': 7.842,
     'L2_ffn_w2': 7.801,
     'L3_ffn_gate_w': 8.0,
     'L3_ffn_rw1': 8.0,
     'L3_ffn_rw2': 8.0,
     'L3_ffn_rw3': 8.0,
     'L3_ffn_sw1': 8.0,
     'L3_ffn_sw2': 8.0,
     'L3_ffn_sw3': 8.0}
    for name, (base, spread) in spreads.items():
        noise = np.random.default_rng([zlib.crc32(name.encode()), seed]).standard_normal(out[name].shape)
        drawn = base * np.exp(spread * noise) if base else spread * noise
        out[name] = jnp.asarray(drawn.astype(out[name].dtype))
    for name, factor in factors.items():
        out[name] = (out[name] * factor).astype(out[name].dtype)
    return out
```

```python
from contextlib import ExitStack
from itertools import islice

import numpy as np

import concourse.bass as bass
from concourse import mybir

ALU = mybir.AluOpType
ACT = mybir.ActivationFunctionType
F32 = mybir.dt.float32
BF16 = mybir.dt.bfloat16
AX = mybir.AxisListType

P = 128
B = 16
T = 128
D = 128
CTX = 77
HEADS = 16
EXPERTS = 8
GROUP = 4
GROUPS = B // GROUP
NEG = -1e30
LN_EPS = 1e-5
LEVELS = 7
ALL_RANKS = 8 * -(-CTX // 8)
FEW_RANKS = ALL_RANKS // 16 * 8



def rope_tables(heads, head_dim):
    inv = (1.0 / 10000.0 ** (np.arange(0, head_dim, 2, dtype=np.float32) / np.float32(head_dim))).astype(np.float32)
    angle = (np.arange(T, dtype=np.float32)[None, :] * inv[:, None]).astype(np.float32)
    angle = np.tile(np.repeat(angle, 2, axis=0), (heads, 1))
    c = heads * head_dim
    swap = np.zeros((c, c), np.float32)
    for k in range(0, c, 2):
        swap[k + 1, k] = -1.0
        swap[k, k + 1] = 1.0
    return np.cos(angle).astype(np.float32), np.sin(angle).astype(np.float32), swap


def constants():
    out = {"ident": np.eye(P, dtype=np.float32)}
    t = np.arange(P)
    out["causal"] = np.where(t[None, :] <= t[:, None], 0.0, NEG).astype(np.float32)
    out["ones"] = np.ones((P, P), np.float32)
    for ranks in (FEW_RANKS, ALL_RANKS):
        rank = np.arange(ranks, dtype=np.float32) + 1
        out[f"scan_keep{ranks}"] = np.tile((rank > 1).astype(np.float32), (P, HEADS // 2))
        out[f"inv_rank{ranks}"] = np.tile(np.float32(1) / rank, (P, HEADS // 2))
    out["before"] = (t[:, None] < t[None, :]).astype(np.float32)
    out["upto"] = (t[:, None] <= t[None, :]).astype(np.float32)
    out["headmask32"] = (t[:, None] // 32 == np.arange(4)[None, :]).astype(np.float32)
    for level in range(LEVELS):
        m = 1 << level
        pair = ((t[None, :] // m) % 2 == 1) & (t[:, None] // m == t[None, :] // m - 1)
        out[f"level{level}"] = pair.astype(np.float32)
    out["level0_lower"] = out["level0"].T.copy()
    out["expert_order"] = np.tile(EXPERTS - np.arange(EXPERTS, dtype=np.float32), (P, 1))
    for hd in (8, 4):
        c = HEADS * hd
        out[f"headmask{hd}"] = (np.arange(c)[:, None] // hd == np.arange(HEADS)[None, :]).astype(np.float32)
        cos, sin, swap = rope_tables(HEADS, hd)
        out[f"cos{hd}"] = np.concatenate([cos, cos], 1)
        out[f"sin{hd}"] = np.concatenate([sin, sin], 1)
        out[f"swap{hd}"] = swap
    return out


CONST = constants()
CONST_AT = {}
for _name, _a in CONST.items():
    CONST_AT[_name] = (sum(w for _, _, w in CONST_AT.values()), _a.shape[0], _a.shape[1])
CONST_W = sum(w for _, _, w in CONST_AT.values())


def constant_blob():
    blob = np.zeros((P, CONST_W), np.float32)
    for name, (at, rows, width) in CONST_AT.items():
        blob[:rows, at:at + width] = CONST[name]
    return blob



def wait(eng, sem, value, alone=None):
    if isinstance(value, int):
        if value > 0:
            eng.wait_ge(sem, value)
        return
    eng.wait_ge(sem, value)
    if alone is not None:
        eng.sem_inc(alone, 1)


class Chain:

    def __init__(self, eng, sem, per=0, alone=None):
        self.eng, self.sem, self.per, self.n, self.k, self.alone = eng, sem, per, 0, 0, alone

    def turn(self, n):
        assert self.k in (0, self.per), f"a turn has {self.k} steps, not {self.per}"
        self.n, self.k = n, 0

    def link(self, ins, lag=0):
        self.k += 1
        ins.then_inc(self.sem, 1)
        wait(self.eng, self.sem, self.n * self.per + self.k - lag, self.alone)


class Stage:

    def __init__(self, nc):
        self.nc, self.ctx, self.sems = nc, ExitStack(), []
        self.tag = f"_{nc.next_id()}"

    def __enter__(self):
        return self

    def sb(self, name, shape, dt=F32):
        return self.ctx.enter_context(self.nc.sbuf_tensor(name + self.tag, shape, dt))

    def ps(self, name, shape, dt=F32):
        return self.ctx.enter_context(self.nc.psum_tensor(name + self.tag, shape, dt))

    def sem(self, name):
        self.sems.append(self.nc.alloc_semaphore(name=name + self.tag))
        return self.sems[-1]

    def block(self):
        return self.nc.Block()

    def __exit__(self, *exc):
        if exc[0] is None:
            self.nc.clear_and_free_semaphores(self.sems)
            self.nc.all_engine_barrier()
        self.ctx.close()


def pairs(t):
    return t.rearrange("p (i j) n -> p i j n", j=2)


def over_pairs(eng, turn):
    for j in range(2):
        turn(j, j, 0)
    with eng.Fori(1, B // 2 - 1) as i:
        for j in range(2):
            turn(i * 2 + j, j, i)
    for j in range(2):
        turn(B - 2 + j, j, B // 2 - 1)


def bcast(ap, axis, n):
    ap = ap.unsqueeze(axis)
    shape = list(ap.shape)
    shape[axis] = n
    return ap.broadcast_to(shape)



def layernorm(nc, K, x, xn, xT, scale=None, bias=None, eps=LN_EPS, rms=False):
    with Stage(nc) as s:
        sq = s.sb("ln_square", [P, B, D])
        mean, var = s.sb("ln_mean", [P, B]), s.sb("ln_var", [P, B])
        pt = s.ps("ln_transposed", [P, 4, GROUP, T])
        chain = s.sem("ln_chain")
        centred, squared, summed, std_ready = (s.sem(n) for n in ("ln_centred", "ln_squared", "ln_summed", "ln_std"))
        normed, transposed = s.sem("ln_normed"), s.sem("ln_transposed_s")
        with s.block() as block:
            @block.vector
            def _(dve):
                c = Chain(dve, chain)
                src = x
                if rms:
                    dve.engine_nop().then_inc(centred, 1)
                else:
                    c.link(dve.tensor_reduce(mean[:], x, AX.X, ALU.add))
                    c.link(dve.tensor_scalar(mean[:], mean[:], 1.0 / D, None, ALU.mult))
                    dve.tensor_tensor(xn, x, bcast(mean[:], 2, D), ALU.subtract).then_inc(centred, 1)
                    dve.wait_ge(centred, 1)
                    src = xn
                dve.wait_ge(squared, 1)
                c.link(dve.tensor_reduce(var[:], sq[:], AX.X, ALU.add))
                dve.tensor_scalar(var[:], var[:], 1.0 / D, eps, ALU.mult, ALU.add).then_inc(summed, 1)
                dve.wait_ge(std_ready, 1)
                c.link(dve.reciprocal(mean[:], var[:]))
                for g in range(GROUPS):
                    part = slice(GROUP * g, GROUP * g + GROUP)
                    dve.tensor_tensor(xn[:, part], src[:, part], bcast(mean[:, part], 2, D), ALU.mult).then_inc(normed, 1)

            @block.scalar
            def _(act):
                act.wait_ge(centred, 1)
                act.activation(sq[:], x if rms else xn, ACT.Square).then_inc(squared, 1)
                act.wait_ge(summed, 1)
                act.activation(var[:], var[:], ACT.Sqrt).then_inc(std_ready, 1)
                for g in range(GROUPS):
                    act.wait_ge(transposed, g + 1)
                    act.activation(xT[:, GROUP * g:GROUP * g + GROUP], pt[:, g], ACT.Identity,
                                   bias=bias if bias is not None else 0.0, scale=scale if scale is not None else 1.0)

            @block.tensor
            def _(pe):
                for g in range(GROUPS):
                    pe.wait_ge(normed, g + 1)
                    for j in range(GROUP):
                        last = pe.transpose(pt[:, g, j], xn[:, GROUP * g + j], K["ident"])
                    last.then_inc(transposed, 1)



def attention(nc, K, name, C, hd, q_src, kv_src, keys, wq, wk, wv, wo, res_in, res_out, bo=None, bqkv=None,
              rope=False, causal=False, ranks=None, tails=None):
    sparse = ranks is not None
    HALF = HEADS // 2
    QUADS = HEADS // GROUP
    TURNED = 1 if rope else 2
    same = kv_src is q_src
    din = q_src.shape[0]
    dout = wo.shape[1]
    sc = float(hd) ** -0.5
    with Stage(nc) as s:
        xs = s.sb("x_staged", [din, 2, T])
        cs = xs if same else s.sb("ctx_staged", [kv_src.shape[0], 2, keys])
        qT = s.sb("qT", [C, 2, T])
        kT = s.sb("kT", [C, 2, keys])
        rot = s.sb("rotated", [C, 2 * T]) if rope else None
        wr = s.sb("w_rotated", [din, 2, C]) if rope else None
        wT = s.sb("w_transposed", [C, 2, din]) if rope else None
        kspread = s.sb("k_spread", [C, 2, HEADS, keys])
        vh = s.sb("v_held", [keys, 2, C])
        va = s.sb("v_and_ones", [keys, 2, HEADS, hd + 1])
        top = s.sb("row_max", [P, 2, 2, HALF])
        pr = s.sb("probs", [P, 2, 2, HALF, keys])
        prT = s.sb("probs_transposed", [keys, QUADS, GROUP, T])
        inv = s.sb("inverse_sum", [P, 2, HEADS])
        o = s.sb("mixed_o", [P, 2, C])
        oT = s.sb("oT", [C, 2, T])
        if sparse:
            work = s.sb("unsorted_rest", [P, 2, HALF, keys])
            ranked = s.sb("sorted", [P, 2, HALF, ranks])
            sums = s.sb("sorted_sums", [P, 2, HALF, ranks])
            tau = s.sb("threshold", [P, 2, HALF])
        p_qk = s.ps("p_qk", [P, 4, T])
        p_misc = s.ps("p_misc", [P, 512])
        p_v = (s.ps("p_v", [keys, C]) if rope else p_qk[0:keys, 2])[:, 0:C]
        p_s = s.ps("p_scores", [P, 2, HALF, T])
        p_t = s.ps("p_probsT", [P, TURNED, GROUP, T])
        p_o = p_misc[:, 128:128 + HEADS * (hd + 1)]
        p_oT = p_misc[0:C, 272:400]
        p_y = p_misc[:, 272:272 + dout]
        names = ("staged projected qkv_ready scores_ready shifted probs_ready probsT_ready probsT_copied mixed "
                 "normed oT_ready oT_copied out_ready added ones_ready w_turned w_turned_copied w_rotated "
                 "w_rotated_copied v_ready tau_ready passed chain_sparse chain_in chain_top chain_inv")
        S = {n: s.sem(f"{name}_{n}") for n in names.split()}
        q4, kv4 = pairs(q_src), pairs(kv_src)
        rin, rout = pairs(res_in), pairs(res_out)

        with s.block() as block:
            @block.gpsimd
            def _(pool):
                pool.memset(va[:], 1.0).then_inc(S["ones_ready"], 1)

                def stage(n, j, i):
                    wait(pool, S["projected"], n - 1, alone=S["passed"])
                    last = pool.tensor_copy(xs[:, j], q4[:, i, j])
                    if not same:
                        last = pool.tensor_copy(cs[:, j], kv4[:, i, j])
                    last.then_inc(S["staged"], 1)

                def spread_v(n, j):
                    wait(pool, S["qkv_ready"], n + 1, alone=S["passed"])
                    wait(pool, S["mixed"], n - 1, alone=S["passed"])
                    pool.tensor_copy(va[:, j, :, 0:hd], vh[:, j].rearrange("k (h d) -> k h d", d=hd)).then_inc(S["v_ready"], 1)

                def threshold(n, j):
                    for hf in range(2):
                        wait(pool, S["tau_ready"], n * 2 + hf + 1)
                        pool.tensor_tensor(pr[:, j, hf], pr[:, j, hf], bcast(tau[:, hf], 2, keys),
                                           ALU.subtract).then_inc(S["probs_ready"], 1)

                def turn(n, j, i):
                    if isinstance(n, int) and n == 0:
                        pool.wait_ge(S["ones_ready"], 1)
                        stage(0, 0, 0)
                    if not (isinstance(n, int) and n == B - 1):
                        stage(n + 1, 1 - j, i if j == 0 else i + 1)
                    spread_v(n, j)
                    if sparse:
                        threshold(n, j)
                over_pairs(pool, turn)

            @block.tensor
            def _(pe):
                if rope:
                    for m, w in enumerate((wq, wk)):
                        last = pe.transpose(p_t[0:C, 0, m, 0:din], w, K["ident"][0:din, 0:din])
                    last.then_inc(S["w_turned"], 1)
                    pe.wait_ge(S["w_turned_copied"], 1)
                    for m in range(2):
                        last = pe.matmul(p_misc[0:din, m * C:(m + 1) * C], wT[:, m], K[f"swap{hd}"], start=True, stop=True)
                    last.then_inc(S["w_rotated"], 1)
                    pe.wait_ge(S["w_rotated_copied"], 1)

                def project(n, j):
                    wait(pe, S["staged"], n + 1, alone=S["passed"] if C < P else None)
                    wait(pe, S["qkv_ready"], n, alone=S["passed"] if C < P else None)
                    pe.matmul(p_qk[0:C, 0, 0:T], wq, xs[:, j], start=True, stop=True)
                    pe.matmul(p_qk[0:C, 1, 0:keys], wk, cs[:, j], start=True, stop=True)
                    if rope:
                        pe.matmul(p_qk[0:C, 2, 0:T], wr[:, 0], xs[:, j], start=True, stop=True)
                        pe.matmul(p_qk[0:C, 3, 0:T], wr[:, 1], xs[:, j], start=True, stop=True)
                    last = pe.matmul(p_v, cs[:, j], wv, start=True, stop=bqkv is None)
                    if bqkv is not None:
                        last = pe.matmul(p_v, K["ones"][0:1, 0:keys], bqkv[2], start=False, stop=True)
                    last.then_inc(S["projected"], 1)

                def scores(n, j, hf):
                    u = n * 2 + hf
                    if hf == 0:
                        wait(pe, S["qkv_ready"], n + 1)
                    wait(pe, S["shifted"], u - 1)
                    for b2 in range(2):
                        h = hf * HALF + 4 * b2
                        last = pe.matmul(p_s[:, hf, 4 * b2:4 * b2 + 4, 0:keys], qT[:, j], kspread[:, j, h:h + 4],
                                         start=True, stop=not causal)
                        if causal:
                            last = pe.matmul(p_s[:, hf, 4 * b2:4 * b2 + 4, 0:keys], K["ident_bf16"],
                                             bcast(K["causal_bf16"], 1, 4), start=False, stop=True)
                    last.then_inc(S["scores_ready"], 1)

                def mix(n, j):
                    def turn_quad(q):
                        if q % 2 == 0:
                            wait(pe, S["probs_ready"], n * 2 + q // 2 + 1)
                        wait(pe, S["probsT_copied"], n * QUADS + q - TURNED + 1)
                        for h in range(GROUP):
                            last = pe.transpose(p_t[0:keys, q % TURNED, h], pr[:, j, q // 2, (q % 2) * GROUP + h], K["ident"])
                        last.then_inc(S["probsT_ready"], 1)

                    turn_quad(0)
                    for q in range(QUADS):
                        if q < QUADS - 1 and TURNED > 1:
                            turn_quad(q + 1)
                        if q == 0:
                            wait(pe, S["added"], n)
                            wait(pe, S["v_ready"], n + 1)
                        wait(pe, S["probsT_copied"], n * QUADS + q + 1)
                        if q < QUADS - 1 and TURNED == 1:
                            turn_quad(q + 1)
                        for h in range(GROUP):
                            hh = q * GROUP + h
                            last = pe.matmul(p_o[:, hh * (hd + 1):(hh + 1) * (hd + 1)], prT[:, q, h], va[:, j, hh],
                                             start=True, stop=True)
                    last.then_inc(S["mixed"], 1)

                def output(n, j):
                    wait(pe, S["normed"], n + 1, alone=S["passed"] if C < P else None)
                    pe.transpose(p_oT, o[:, j], K["ident"]).then_inc(S["oT_ready"], 1)
                    wait(pe, S["oT_copied"], n + 1)
                    last = pe.matmul(p_y, oT[:, j], wo, start=True, stop=bo is None)
                    if bo is not None:
                        last = pe.matmul(p_y, K["ones"][0:1, :], bo, start=False, stop=True)
                    last.then_inc(S["out_ready"], 1)

                def turn(n, j, i):
                    if isinstance(n, int) and n == 0:
                        project(0, 0)
                    for hf in range(2):
                        scores(n, j, hf)
                    if not (isinstance(n, int) and n < 2):
                        output(n - 2, j)
                    if not (isinstance(n, int) and n == B - 1):
                        project(n + 1, 1 - j)
                    if not (isinstance(n, int) and n == 0):
                        mix(n - 1, 1 - j)
                over_pairs(pe, turn)
                output(B - 2, 0)
                mix(B - 1, 1)
                output(B - 1, 1)

            @block.vector
            def _(dve):
                if rope:
                    dve.wait_ge(S["w_turned"], 1)
                    dve.tensor_copy(wT[:], p_t[0:C, 0, 0:2, 0:din]).then_inc(S["w_turned_copied"], 1)
                    dve.wait_ge(S["w_rotated"], 1)
                    dve.tensor_copy(wr[:], p_misc[0:din, 0:2 * C].rearrange("d (m c) -> d m c", m=2)).then_inc(S["w_rotated_copied"], 1)
                c_in = Chain(dve, S["chain_in"], 3 if rope else 1 if bqkv is not None else 0)
                c_top = Chain(dve, S["chain_top"], 2)
                c_inv = Chain(dve, S["chain_inv"], 1)

                def evacuate(n, j):
                    c_in.turn(n)
                    wait(dve, S["projected"], n + 1)
                    if rope:
                        cos = K[f"cos{hd}"].rearrange("c (a t) -> c a t", a=2)
                        sin = K[f"sin{hd}"].rearrange("c (a t) -> c a t", a=2)
                        r3 = rot[:].rearrange("c (a t) -> c a t", a=2)
                        c_in.link(dve.tensor_tensor(r3, p_qk[0:C, 2:4], sin, ALU.mult))
                        dve.tensor_tensor(qT[:, j], p_qk[0:C, 0], cos[:, 0], ALU.mult)
                        c_in.link(dve.tensor_tensor(kT[:, j], p_qk[0:C, 1], cos[:, 0], ALU.mult))
                        dve.tensor_tensor(qT[:, j], qT[:, j], rot[:, 0:T], ALU.add)
                        c_in.link(dve.tensor_tensor(kT[:, j], kT[:, j], rot[:, T:2 * T], ALU.add))
                        ksrc = kT[:, j]
                    elif bqkv is not None:
                        dve.tensor_scalar(qT[:, j], p_qk[0:C, 0], bqkv[0], sc, ALU.add, ALU.mult)
                        c_in.link(dve.tensor_scalar(kT[:, j], p_qk[0:C, 1, 0:keys], bqkv[1], None, ALU.add))
                        ksrc = kT[:, j]
                    else:
                        dve.tensor_copy(qT[:, j], p_qk[0:C, 0])
                        ksrc = p_qk[0:C, 1, 0:keys]
                    dve.tensor_tensor(kspread[:, j], bcast(ksrc, 1, HEADS), bcast(K[f"headmask{hd}"], 2, keys), ALU.mult)
                    wait(dve, S["v_ready"], n - 1)
                    dve.tensor_copy(vh[:, j], p_v).then_inc(S["qkv_ready"], 1)

                def shift(n, j, hf):
                    u = n * 2 + hf
                    wait(dve, S["scores_ready"], u + 1)
                    sv = p_s[:, hf, :, 0:keys]
                    c_top.link(dve.tensor_reduce(top[:, j, hf], sv, AX.X, ALU.max))
                    wait(dve, S["probsT_ready"], (n - 2) * QUADS + 2 * (hf + 1))
                    dve.tensor_tensor(pr[:, j, hf], sv, bcast(top[:, j, hf], 2, keys), ALU.subtract).then_inc(S["shifted"], 1)

                c_sp = Chain(dve, S["chain_sparse"], 2 * (2 * (ranks // 8) + 1) if sparse else 0, alone=S["passed"])

                def find_thresholds(n, j, i):
                    wait(dve, S["shifted"], n * 2 + 2, alone=S["passed"])
                    for r in range(ranks // 8):
                        for hf in range(2):
                            for h in range(HALF):
                                last = dve.max(ranked[:, hf, h, 8 * r:8 * r + 8], (work[:, hf, h] if r else pr[:, j, hf, h]))
                            c_sp.link(last, lag=1)
                        if r < ranks // 8 - 1:
                            for hf in range(2):
                                for h in range(HALF):
                                    last = dve.match_replace(work[:, hf, h], ranked[:, hf, h, 8 * r:8 * r + 8],
                                                             (work[:, hf, h] if r else pr[:, j, hf, h]), NEG)
                                c_sp.link(last, lag=1)
                    flat = "p h k -> p (h k)"
                    for hf in range(2):
                        c_sp.link(dve.tensor_tensor_scan(sums[:, hf].rearrange(flat), K[f"scan_keep{ranks}"],
                                                         ranked[:, hf].rearrange(flat), 0.0, ALU.mult, ALU.add), lag=1)
                    for hf in range(2):
                        c_sp.link(dve.scalar_tensor_tensor(sums[:, hf].rearrange(flat), sums[:, hf].rearrange(flat), -1.0,
                                                           K[f"inv_rank{ranks}"], ALU.add, ALU.mult), lag=1 - hf)
                    wait(dve, S["probs_ready"], n * 2)
                    for hf in range(2):
                        dve.tensor_reduce(tau[:, hf], sums[:, hf], AX.X, ALU.max).then_inc(S["tau_ready"], 1)
                    if tails is not None:
                        wait(dve, S["tau_ready"], n * 2 + 2)
                        dve.tensor_tensor(tails[:, i, j], ranked[:, :, :, ranks - 1], tau[:], ALU.subtract)

                def normalise(n, j):
                    c_inv.turn(n)
                    wait(dve, S["mixed"], n + 1)
                    o4 = p_o.rearrange("p (h d) -> p h d", d=hd + 1)
                    c_inv.link(dve.reciprocal(inv[:, j], o4[:, :, hd]))
                    dve.tensor_tensor(o[:, j].rearrange("p (h d) -> p h d", d=hd), o4[:, :, 0:hd],
                                      bcast(inv[:, j], 2, hd), ALU.mult).then_inc(S["normed"], 1)

                def add(n, j, i):
                    wait(dve, S["out_ready"], n + 1)
                    dve.tensor_tensor(rout[:, i, j], rin[:, i, j], p_y, ALU.add).then_inc(S["added"], 1)

                def turn(n, j, i):
                    if isinstance(n, int) and n == 0:
                        evacuate(0, 0)
                    c_top.turn(n)
                    c_sp.turn(n)
                    for hf in range(2):
                        shift(n, j, hf)
                    if not (isinstance(n, int) and n < 2):
                        add(n - 2, j, i - 1)
                    if not (isinstance(n, int) and n == B - 1):
                        evacuate(n + 1, 1 - j)
                    if sparse:
                        find_thresholds(n, j, i)
                    if not (isinstance(n, int) and n == 0):
                        normalise(n - 1, 1 - j)
                over_pairs(dve, turn)
                add(B - 2, 0, B // 2 - 1)
                normalise(B - 1, 1)
                add(B - 1, 1, B // 2 - 1)

            @block.scalar
            def _(act):
                def probs(n, j, hf):
                    u = n * 2 + hf
                    wait(act, S["shifted"], u + 1)
                    act.activation(pr[:, j, hf], pr[:, j, hf], ACT.Exp, scale=sc).then_inc(S["probs_ready"], 1)

                def copy_quads(n, hf):
                    for q in (2 * hf, 2 * hf + 1):
                        wait(act, S["probsT_ready"], n * QUADS + q + 1)
                        wait(act, S["mixed"], n)
                        act.activation(prT[:, q], p_t[0:keys, q % TURNED], ACT.Relu if sparse else ACT.Copy).then_inc(
                            S["probsT_copied"], 1)

                def copy_o(n, j):
                    wait(act, S["oT_ready"], n + 1)
                    act.copy(oT[:, j], p_oT).then_inc(S["oT_copied"], 1)

                def turn(n, j, i):
                    if not (isinstance(n, int) and n < 2):
                        copy_o(n - 2, j)
                    for hf in range(2):
                        if not sparse:
                            probs(n, j, hf)
                        if not (isinstance(n, int) and n == 0):
                            copy_quads(n - 1, hf)
                over_pairs(act, turn)
                copy_o(B - 2, 0)
                for hf in range(2):
                    copy_quads(B - 1, hf)
                copy_o(B - 1, 1)



def load_constants(nc, K, K_tile, X, x_dram, consts, ctx, ctxT, ctx_dram):
    with Stage(nc) as s:
        loaded = s.sem("loaded")
        turned, copied = s.sem("ctx_turned"), s.sem("ctx_copied")
        pt = s.ps("p_ctxT", [P, GROUPS, GROUP, T])
        with s.block() as block:
            @block.sync
            def _(sp):
                sp.dma_start(X, x_dram.rearrange("b t d -> t b d")).then_inc(loaded, 16)
                sp.dma_start(K_tile, consts).then_inc(loaded, 16)

            @block.scalar
            def _(act):
                act.dma_start(ctx, ctx_dram.rearrange("b k d -> k b d")).then_inc(loaded, 16)
                for g in range(GROUPS):
                    act.wait_ge(turned, g + 1)
                    act.copy(ctxT[:, GROUP * g:GROUP * g + GROUP], pt[:, g, :, 0:CTX]).then_inc(copied, 1)

            @block.vector
            def _(dve):
                dve.wait_ge(loaded, 48)
                dve.tensor_copy(K["ident_bf16"], K["ident"])
                dve.tensor_copy(K["causal_bf16"], K["causal"])

            @block.tensor
            def _(pe):
                pe.wait_ge(loaded, 48)
                for g in range(GROUPS):
                    for j in range(GROUP):
                        last = pe.transpose(pt[:, g, j, 0:CTX], ctx[:, GROUP * g + j], K["ident"][0:CTX, 0:CTX])
                    last.then_inc(turned, 1)


def store_result(nc, X, out):
    with Stage(nc) as s:
        stored = s.sem("stored")
        with s.block() as block:
            @block.sync
            def _(sp):
                sp.dma_start(out.rearrange("b t d -> t b d"), X).then_inc(stored, 16)
                sp.wait_ge(stored, 16)


def load(nc, s, loads):
    loaded = s.sem("weights_loaded")
    with s.block() as block:
        @block.sync
        def _(sp):
            for dst, src in loads[0::2]:
                sp.dma_start(dst, src).then_inc(loaded, 16)

        @block.scalar
        def _(act):
            for dst, src in loads[1::2]:
                act.dma_start(dst, src).then_inc(loaded, 16)
            act.wait_ge(loaded, 16 * len(loads))


def row(ap):
    return ap.rearrange("(a n) -> a n", a=1)


def column(ap):
    return ap.rearrange("(p a) -> p a", a=1)


def program(nc, w, out, first=0, last=12):
    ctx = ExitStack()
    with ctx:
        def sb(name, shape, dt=F32):
            return ctx.enter_context(nc.sbuf_tensor(name, shape, dt))

        X = sb("x_residual", [P, B, D])
        XN = sb("x_normed", [P, B, D])
        XT = sb("x_transposed", [P, B, T])
        KT = sb("constants", [P, CONST_W])
        K = {n: KT[:rows, at:at + width] for n, (at, rows, width) in CONST_AT.items()}
        K["ident_bf16"], K["causal_bf16"] = sb("ident_bf16", [P, P], BF16)[:], sb("causal_bf16", [P, P], BF16)[:]
        K["ctx"] = sb("context", [CTX, B, D])[:]
        K["ctxT"] = sb("context_transposed", [D, B, CTX])[:]
        load_constants(nc, K, KT[:], X[:], w["x"], w["constants"], K["ctx"], K["ctxT"], w["ctx_1024"])
        stages = [l0_attn, l0_xattn, l0_ffn, l1_attn, l1_xattn, l1_ffn, l2_attn, l2_xattn, l2_ffn, l3_attn, l3_xattn,
                  l3_ffn]
        for stage in stages[first:last]:
            stage(nc, K, w, X[:], XN[:], XT[:])
        store_result(nc, X[:], out)


def l0_attn(nc, K, w, X, XN, XT):
    layernorm(nc, K, X, XN, XT)
    with Stage(nc) as s:
        wqkv, wp, bp = s.sb("w_qkv", [D, 3 * D]), s.sb("w_proj", [D, D]), s.sb("b_proj", [1, D])
        load(nc, s, [(wqkv[:], w["L0_attn_w_qkv"]), (wp[:], w["L0_attn_w_proj"]), (bp[:], row(w["L0_attn_b_proj"]))])
        attention(nc, K, "l0a", D, 8, XT, XT, T, wqkv[:, 0:D], wqkv[:, D:2 * D], wqkv[:, 2 * D:], wp[:], X, X, bo=bp[:])


def l1_attn(nc, K, w, X, XN, XT):
    layernorm(nc, K, X, XN, XT)
    with Stage(nc) as s:
        wqkv, wp, bp = s.sb("w_qkv", [D, 3 * D]), s.sb("w_out", [D, D]), s.sb("b_out", [1, D])
        load(nc, s, [(wqkv[:], w["L1_attn_Wqkv"]), (wp[:], w["L1_attn_Wout"]), (bp[:], row(w["L1_attn_bout"]))])
        attention(nc, K, "l1a", D, 8, XT, XT, T, wqkv[:, 0:D], wqkv[:, D:2 * D], wqkv[:, 2 * D:], wp[:], X, X, bo=bp[:],
                  rope=True, causal=True)


def l0_xattn(nc, K, w, X, XN, XT):
    layernorm(nc, K, X, XN, XT)
    sc = float(D) ** -0.5
    with Stage(nc) as s:
        top = s.sb("row_max", [P, B])
        inv = s.sb("inverse_sum", [P, B])
        pr = s.sb("probs", [P, B, CTX])
        prT = s.sb("probs_transposed", [CTX, B, T])
        mixed = s.sb("mixed", [P, B, D])
        p_s = s.ps("p_scores", [P, 2, GROUP, T])
        p_t = s.ps("p_probsT", [P, 2, GROUP, T])
        p_o = s.ps("p_mixed", [P, 2, GROUP, D])
        scores_ready, shifted, probs_ready, turned, turned_copied, mixed_ready, scaled, chain = (
            s.sem("x0_" + n) for n in "scores_ready shifted probs_ready turned turned_copied mixed_ready scaled chain".split())

        def group(g):
            return slice(GROUP * g, GROUP * g + GROUP)

        with s.block() as block:
            @block.tensor
            def _(pe):
                def scores(g):
                    wait(pe, shifted, g - 1)
                    for j in range(GROUP):
                        last = pe.matmul(p_s[:, g % 2, j, 0:CTX], XT[:, GROUP * g + j], K["ctxT"][:, GROUP * g + j],
                                         start=True, stop=True)
                    last.then_inc(scores_ready, 1)

                def mix(g):
                    pe.wait_ge(probs_ready, g + 1)
                    wait(pe, turned_copied, g - 1)
                    for j in range(GROUP):
                        last = pe.transpose(p_t[0:CTX, g % 2, j], pr[:, GROUP * g + j], K["ident"])
                    last.then_inc(turned, 1)
                    pe.wait_ge(turned_copied, g + 1)
                    wait(pe, scaled, g - 1)
                    for j in range(GROUP):
                        last = pe.matmul(p_o[:, g % 2, j], prT[:, GROUP * g + j], K["ctx"][:, GROUP * g + j],
                                         start=True, stop=True)
                    last.then_inc(mixed_ready, 1)

                scores(0)
                for g in range(GROUPS):
                    if g < GROUPS - 1:
                        scores(g + 1)
                    mix(g)

            @block.vector
            def _(dve):
                c = Chain(dve, chain)

                def softmax(g):
                    dve.wait_ge(scores_ready, g + 1)
                    c.link(dve.tensor_reduce(top[:, group(g)], p_s[:, g % 2, :, 0:CTX], AX.X, ALU.max))
                    dve.tensor_tensor(pr[:, group(g)], p_s[:, g % 2, :, 0:CTX], bcast(top[:, group(g)], 2, CTX),
                                      ALU.subtract).then_inc(shifted, 1)
                    dve.wait_ge(probs_ready, g + 1)
                    c.link(dve.tensor_reduce(inv[:, group(g)], pr[:, group(g)], AX.X, ALU.add))
                    c.link(dve.reciprocal(inv[:, group(g)], inv[:, group(g)]))

                def add(g):
                    dve.wait_ge(mixed_ready, g + 1)
                    dve.tensor_tensor(mixed[:, group(g)], p_o[:, g % 2], bcast(inv[:, group(g)], 2, D),
                                      ALU.mult).then_inc(scaled, 1)
                    dve.wait_ge(scaled, g + 1)
                    c.link(dve.tensor_tensor(X[:, group(g)], X[:, group(g)], mixed[:, group(g)], ALU.add))

                for g in range(GROUPS):
                    softmax(g)
                    if g:
                        add(g - 1)
                add(GROUPS - 1)

            @block.scalar
            def _(act):
                for g in range(GROUPS):
                    act.wait_ge(shifted, g + 1)
                    act.activation(pr[:, group(g)], pr[:, group(g)], ACT.Exp, scale=sc).then_inc(probs_ready, 1)
                    act.wait_ge(turned, g + 1)
                    act.copy(prT[:, group(g)], p_t[0:CTX, g % 2]).then_inc(turned_copied, 1)


def l2_xattn(nc, K, w, X, XN, XT):
    layernorm(nc, K, X, XN, XT)
    with Stage(nc) as s:
        wq, wk, wv, wo = (s.sb(n, [D, D]) for n in ("w_q", "w_k", "w_v", "w_o"))
        bq, bk = s.sb("b_q", [D, 1]), s.sb("b_k", [D, 1])
        bv, bo = s.sb("b_v", [1, D]), s.sb("b_o", [1, D])
        load(nc, s, [(wq[:], w["L2_xattn_Wq"]), (wk[:], w["L2_xattn_Wk"]), (wv[:], w["L2_xattn_Wv"]),
                     (wo[:], w["L2_xattn_Wo"]), (bq[:], column(w["L2_xattn_bq"])), (bk[:], column(w["L2_xattn_bk"])),
                     (bv[:], row(w["L2_xattn_bv"])), (bo[:], row(w["L2_xattn_bo"]))])
        tails = s.sb("tails", [P, B // 2, 2, 2, HEADS // 2])
        unresolved = s.sb("unresolved", [1, 1], mybir.dt.int32)

        def attend(ranks, tails=None):
            attention(nc, K, f"l2x{ranks}", D, 8, XT, K["ctxT"], CTX, wq[:], wk[:], wv[:], wo[:], X, XN, bo=bo[:],
                      bqkv=(bq[:], bk[:], bv[:]), ranks=ranks, tails=tails)
        attend(FEW_RANKS, tails[:])
        any_above_zero(nc, K, tails[:].rearrange("p i j f h -> p (i j f h)"), unresolved[:])
        with nc.If(nc.values_load(unresolved[:], min_val=0, max_val=1) > 0):
            nc.all_engine_barrier()
            attend(ALL_RANKS)
        copy_all(nc, X, XN)


def any_above_zero(nc, K, values, flag):
    with Stage(nc) as s:
        most = s.sb("most", [P, 1])
        top = s.sb("top", [1, 1])
        pt = s.ps("p_most", [1, P])
        reduced, turned, chain = (s.sem("any_" + n) for n in ("reduced", "turned", "chain"))
        with s.block() as block:
            @block.vector
            def _(dve):
                dve.tensor_reduce(most[:], values, AX.X, ALU.max).then_inc(reduced, 1)
                dve.wait_ge(turned, 1)
                Chain(dve, chain).link(dve.tensor_reduce(top[:], pt[:], AX.X, ALU.max))
                dve.tensor_scalar(flag, top[:], 0.0, None, ALU.is_gt)

            @block.tensor
            def _(pe):
                pe.wait_ge(reduced, 1)
                pe.transpose(pt[:], most[:], K["ident"]).then_inc(turned, 1)


def copy_all(nc, dst, src):
    with Stage(nc) as s:
        with s.block() as block:
            @block.vector
            def _(dve):
                dve.tensor_copy(dst[:, 0:7], src[:, 0:7])

            @block.scalar
            def _(act):
                act.copy(dst[:, 7:12], src[:, 7:12])

            @block.gpsimd
            def _(pool):
                pool.tensor_copy(dst[:, 12:B], src[:, 12:B])



def first_then_loop(eng, count, turn):
    for j in range(2):
        turn(j, j, 0)
    if count > 2:
        with eng.Fori(1, count // 2) as i:
            for j in range(2):
                turn(i * 2 + j, j, i)


def pair_of(src, i, j):
    if len(src.shape) == 2:
        return src.rearrange("(i j) a -> i j a", j=2)[i, j]
    return src.rearrange("(i j) a b -> i j a b", j=2)[i, j]


def router(nc, K, tT, wr, gates, gate_bias=None, top2=True, renorm=True, eps=0.0, probs_out=None):
    with Stage(nc) as s:
        pr = probs_out if probs_out is not None else s.sb("probs", [P, B, EXPERTS])
        rank, rest, first = (s.sb(n, [P, B, EXPERTS]) for n in ("rank", "rest", "first"))
        m, m2, r = (s.sb(n, [P, B]) for n in ("largest", "second", "rank_best"))
        pl = s.ps("p_logits", [P, B, EXPERTS])
        logits_ready, shifted, exp_ready, chain = (s.sem("router_" + n) for n in ("logits", "shifted", "exp", "chain"))
        with s.block() as block:
            @block.tensor
            def _(pe):
                for b in range(B):
                    last = pe.matmul(pl[:, b], tT[:, b], wr, start=True, stop=gate_bias is None)
                    if gate_bias is not None:
                        last = pe.matmul(pl[:, b], K["ones"][0:1, :], gate_bias, start=False, stop=True)
                last.then_inc(logits_ready, 1)

            @block.scalar
            def _(act):
                act.wait_ge(shifted, 1)
                act.activation(pr[:], pr[:], ACT.Exp).then_inc(exp_ready, 1)

            @block.vector
            def _(dve):
                c = Chain(dve, chain)
                E = EXPERTS
                dve.wait_ge(logits_ready, 1)
                c.link(dve.tensor_reduce(m[:], pl[:], AX.X, ALU.max))
                dve.tensor_tensor(pr[:], pl[:], bcast(m[:], 2, E), ALU.subtract).then_inc(shifted, 1)
                dve.wait_ge(exp_ready, 1)
                c.link(dve.tensor_reduce(m[:], pr[:], AX.X, ALU.add))
                c.link(dve.reciprocal(m[:], m[:]))
                c.link(dve.tensor_tensor(pr[:], pr[:], bcast(m[:], 2, E), ALU.mult))
                if not top2:
                    return

                def one_hot(src, largest, dst):
                    c.link(dve.tensor_reduce(largest, src, AX.X, ALU.max))
                    c.link(dve.tensor_tensor(rank[:], src, bcast(largest, 2, E), ALU.is_equal))
                    c.link(dve.tensor_tensor(rank[:], rank[:], bcast(K["expert_order"], 1, B), ALU.mult))
                    c.link(dve.tensor_reduce(r[:], rank[:], AX.X, ALU.max))
                    c.link(dve.tensor_tensor(dst, rank[:], bcast(r[:], 2, E), ALU.is_equal))

                one_hot(pr[:], m[:], first[:])
                c.link(dve.scalar_tensor_tensor(rest[:], first[:], -2.0, pr[:], ALU.mult, ALU.add))
                one_hot(rest[:], m2[:], gates)
                c.link(dve.tensor_tensor(gates, gates, bcast(m2[:], 2, E), ALU.mult))
                c.link(dve.tensor_tensor(first[:], first[:], bcast(m[:], 2, E), ALU.mult))
                c.link(dve.tensor_tensor(gates, gates, first[:], ALU.add))
                if renorm:
                    c.link(dve.scalar_tensor_tensor(m[:], m[:], eps, m2[:], ALU.add, ALU.add))
                    c.link(dve.reciprocal(m[:], m[:]))
                    c.link(dve.tensor_tensor(gates, gates, bcast(m[:], 2, E), ALU.mult))


def experts(nc, K, name, tT, gates, acc, count, F, func, w_in, w_mul, w_out, b_in=None, b_mul=None, b_out=None,
            shared_out=False, tiles=None):
    NC = F // P
    with Stage(nc) as s:
        w1 = s.sb("w_in", [P, 2, F])
        w2 = s.sb("w_mul", [P, 2, F]) if w_mul is not None else None
        wo = s.sb("w_out", [P, 2, NC, D])
        b1 = s.sb("b_in", [P, 2, NC]) if b_in is not None else None
        b2 = s.sb("b_mul", [P, 2, NC]) if b_mul is not None else None
        bo = s.sb("b_out", [1, 2, D]) if b_out is not None else None
        acted = s.sb("activated", [P, 2, GROUP * T]) if w_mul is not None else None
        hid = s.sb("hidden", [P, 2, NC, GROUP * T])
        gated = s.sb("gated", [P, 2, GROUP, D])
        p1 = s.ps("p_in", [P, 2, GROUP * T])
        p2 = s.ps("p_mul", [P, 2, GROUP * T])
        py = s.ps("p_out", [P, 2, GROUP, D])
        S = {n: s.sem(f"{name}_{n}") for n in
             "in_ready mul_ready act_done hidden_ready out_ready gated_s added passed loaded0 loaded1".split()}
        loaded = (S["loaded0"], S["loaded1"])
        loads = [(w1, w_in, lambda a: a)]
        if w_mul is not None:
            loads.append((w2, w_mul, lambda a: a))
        loads.append((wo, w_out, lambda a: a.rearrange("(c p) d -> p c d", p=P)))
        for tile, src in ((b1, b_in), (b2, b_mul)):
            if src is not None:
                loads.append((tile, src, lambda a: a))
        if b_out is not None:
            loads.append((bo, b_out, lambda a: row(a)))
        hid_sem = S["hidden_ready"] if w_mul is not None else S["act_done"]
        last_i = count // 2 - 1

        with s.block() as block:
            @block.sync
            def _(sp):
                def turn(e, j, i):
                    wait(sp, S["out_ready"], (e - 1) * GROUPS)
                    for tile, src, view in loads:
                        one = src[2 * i + j] if src.shape[0] == count and isinstance(e, int) else (
                            pair_of(src, i, j) if src.shape[0] == count else src[0])
                        sp.dma_start(tile[:, j], view(one)).then_inc(loaded[j], 16)
                first_then_loop(sp, count, turn)

            @block.tensor
            def _(pe):
                def project(e, j, i, g):
                    u = e * GROUPS + g
                    if g == 0:
                        pe.wait_ge(loaded[j], (i + 1) * (16 * len(loads)))
                    for c in range(NC):
                        q = u * NC + c
                        wait(pe, S["act_done"], q - 1)
                        pe.matmul(p1[:, c % 2], w1[:, j, c * P:(c + 1) * P], tT[:, GROUP * g:GROUP * g + GROUP],
                                  start=True, stop=True).then_inc(S["in_ready"], 1)
                        if w2 is not None:
                            wait(pe, S["hidden_ready"], q - 1)
                            pe.matmul(p2[:, c % 2], w2[:, j, c * P:(c + 1) * P], tT[:, GROUP * g:GROUP * g + GROUP],
                                      start=True, stop=True).then_inc(S["mul_ready"], 1)

                def combine(e, j, g):
                    u = e * GROUPS + g
                    wait(pe, hid_sem, (u + 1) * NC)
                    wait(pe, S["gated_s"], u - 1)
                    for t in range(GROUP):
                        for c in range(NC):
                            last = pe.matmul(py[:, g % 2, t], hid[:, g % 2, c, t * P:(t + 1) * P], wo[:, j, c],
                                             start=c == 0, stop=bo is None and c == NC - 1)
                        if bo is not None:
                            last = pe.matmul(py[:, g % 2, t], K["ones"][0:1, :], bo[:, j], start=False, stop=True)
                    last.then_inc(S["out_ready"], 1)

                def turn(e, j, i):
                    for g in range(GROUPS):
                        project(e, j, i, g)
                        if g:
                            combine(e, j, g - 1)
                        elif not (isinstance(e, int) and e == 0):
                            combine(e - 1, 1 - j, GROUPS - 1)
                first_then_loop(pe, count, turn)
                combine(count - 1, 1, GROUPS - 1)

            @block.scalar
            def _(act):
                def turn(e, j, i):
                    for g in range(GROUPS):
                        u = e * GROUPS + g
                        for c in range(NC):
                            q = u * NC + c
                            wait(act, S["in_ready"], q + 1)
                            bias = b1[:, j, c:c + 1] if b1 is not None else 0.0
                            if w2 is None:
                                if c == 0:
                                    wait(act, S["out_ready"], u - 1)
                                act.activation(hid[:, g % 2, c], p1[:, c % 2], func, bias=bias).then_inc(S["act_done"], 1)
                            else:
                                wait(act, S["hidden_ready"], q - 1)
                                act.activation(acted[:, c % 2], p1[:, c % 2], func, bias=bias).then_inc(S["act_done"], 1)
                first_then_loop(act, count, turn)

            @block.vector
            def _(dve):
                ge = gates.rearrange("p b (i j) -> p b i j", j=2)

                def weigh(e, j, i, g):
                    u = e * GROUPS + g
                    wait(dve, S["out_ready"], u + 1)
                    wait(dve, S["added"], u - 1)
                    dve.tensor_tensor(gated[:, g % 2], py[:, g % 2], bcast(ge[:, GROUP * g:GROUP * g + GROUP, i, j], 2, D),
                                      ALU.mult).then_inc(S["gated_s"], 1)

                def turn(e, j, i):
                    for g in range(GROUPS):
                        u = e * GROUPS + g
                        if w2 is not None:
                            for c in range(NC):
                                q = u * NC + c
                                wait(dve, S["mul_ready"], q + 1)
                                wait(dve, S["act_done"], q + 1)
                                if c == 0:
                                    wait(dve, S["out_ready"], u - 1)
                                if b2 is not None:
                                    ins = dve.scalar_tensor_tensor(hid[:, g % 2, c], p2[:, c % 2], b2[:, j, c:c + 1],
                                                                   acted[:, c % 2], ALU.add, ALU.mult)
                                else:
                                    ins = dve.tensor_tensor(hid[:, g % 2, c], p2[:, c % 2], acted[:, c % 2], ALU.mult)
                                ins.then_inc(S["hidden_ready"], 1)
                        if g:
                            weigh(e, j, i, g - 1)
                        elif not (isinstance(e, int) and e == 0):
                            weigh(e - 1, 1 - j, i - 1 if j == 0 else i, GROUPS - 1)
                first_then_loop(dve, count, turn)
                weigh(count - 1, 1, last_i, GROUPS - 1)

            @block.gpsimd
            def _(pool):
                def turn(e, j, i):
                    for g in range(GROUPS):
                        u = e * GROUPS + g
                        wait(pool, S["gated_s"], u + 1, alone=S["passed"])
                        part = acc[:, GROUP * g:GROUP * g + GROUP]
                        pool.tensor_tensor(part, part, gated[:, g % 2], ALU.add).then_inc(S["added"], 1)
                first_then_loop(pool, count, turn)


def add_into(nc, dst, src):
    with Stage(nc) as s:
        with s.block() as block:
            @block.vector
            def _(dve):
                dve.tensor_tensor(dst, dst, src, ALU.add)


def project_all(nc, src, w, dst):
    C = w.shape[1]
    with Stage(nc) as s:
        p = s.ps("p_project", [P, GROUPS, GROUP, T])
        ready = s.sem("project_ready")
        with s.block() as block:
            @block.tensor
            def _(pe):
                for g in range(GROUPS):
                    pe.matmul(p[0:C, g], w, src[:, GROUP * g:GROUP * g + GROUP], start=True, stop=True).then_inc(ready, 1)

            @block.scalar
            def _(act):
                for g in range(GROUPS):
                    act.wait_ge(ready, g + 1)
                    act.copy(dst[:, GROUP * g:GROUP * g + GROUP], p[0:C, g])


def l0_ffn(nc, K, w, X, XN, XT):
    L = w["L0_ffn_w_down"].shape[1]
    F = w["L0_ffn_w1"].shape[2]
    layernorm(nc, K, X, XN, XT)
    with Stage(nc) as s:
        wd, wr, wup = s.sb("w_down", [D, L]), s.sb("w_router", [D, EXPERTS]), s.sb("w_up", [L, D])
        wqkv = s.sb("w_qkv", [L, 3, L])
        g1, g2 = s.sb("g1", [D, 1]), s.sb("g2", [D, 1])
        res = s.sb("latent_residual", [P, B, D])
        gates = s.sb("gates", [P, B, EXPERTS])
        load(nc, s, [(wd[:], w["L0_ffn_w_down"]), (wr[:], w["L0_ffn_router_w"]), (wup[:], w["L0_ffn_w_up"]),
                     (wqkv[:, 0], w["L0_ffn_wq"]), (wqkv[:, 1], w["L0_ffn_wk"]), (wqkv[:, 2], w["L0_ffn_wv"]),
                     (g1[:], column(w["L0_ffn_g1"])), (g2[:], column(w["L0_ffn_g2"]))])
        layernorm(nc, K, XN, res[:], XT, scale=g1[:], eps=1e-5, rms=True)
        with Stage(nc) as s2:
            cT = s2.sb("latent", [L, B, T])
            project_all(nc, XT, wd[:], cT[:])
            attention(nc, K, "l0f", L, L // HEADS, cT[:], cT[:], T, wqkv[:, 0], wqkv[:, 1], wqkv[:, 2], wup[:], XN, res[:],
                      rope=True, causal=True)
        layernorm(nc, K, res[:], XN, XT, scale=g2[:], eps=1e-5, rms=True)
        add_into(nc, X, res[:])
        router(nc, K, XT, wr[:], gates[:])
        experts(nc, K, "l0e", XT, gates[:], X, EXPERTS, F, ACT.Silu, w["L0_ffn_w1"], w["L0_ffn_w3"], w["L0_ffn_w2"])


def l1_ffn(nc, K, w, X, XN, XT):
    H = w["L1_ffn_Wo"].shape[0]
    layernorm(nc, K, X, XN, XT)
    with Stage(nc) as s:
        wg = s.sb("w_gate", [D, EXPERTS])
        gates = s.sb("gates", [P, B, EXPERTS])
        load(nc, s, [(wg[:], w["L1_ffn_Wg"])])
        router(nc, K, XT, wg[:], gates[:], eps=1e-9)
        w1, b1 = w["L1_ffn_W1"], w["L1_ffn_b1"]
        experts(nc, K, "l1e", XT, gates[:], X, EXPERTS, H, ACT.Sigmoid, w1[:, :, H:2 * H], w1[:, :, 0:H],
                w["L1_ffn_Wo"].rearrange("(a f) d -> a f d", a=1), b1[:, :, H // P:2 * H // P], b1[:, :, 0:H // P],
                w["L1_ffn_bo"].rearrange("(a d) -> a d", a=1))


def l3_ffn(nc, K, w, X, XN, XT):
    F = w["L3_ffn_rw1"].shape[2]
    layernorm(nc, K, X, XN, XT)
    with Stage(nc) as s:
        wg, bg = s.sb("w_gate", [D, EXPERTS]), s.sb("b_gate", [1, EXPERTS])
        gates = s.sb("gates", [P, B, EXPERTS])
        halves = s.sb("shared_gates", [P, B, 2])
        load(nc, s, [(wg[:], w["L3_ffn_gate_w"]), (bg[:], row(w["L3_ffn_gate_b"]))])
        with s.block() as block:
            @block.vector
            def _(dve):
                dve.memset(halves[:], 0.5)
        router(nc, K, XT, wg[:], gates[:], gate_bias=bg[:], renorm=False)
        for kind, g, n in (("r", gates, EXPERTS), ("s", halves, 2)):
            v = {k: w[f"L3_ffn_{kind}{k}"] for k in ("w1", "w2", "w3", "b1", "b2", "b3")}
            experts(nc, K, f"l3{kind}", XT, g[:], X, n, F, ACT.Silu, v["w1"], v["w2"], v["w3"], v["b1"], v["b2"], v["b3"])



def expert_choice(nc, K, probs, gates, capacity):
    assert B * EXPERTS == P and capacity % 8 == 0
    with Stage(nc) as s:
        by_pair, left, kept = (s.sb(n, [P, T]) for n in ("by_pair", "left", "kept"))
        best = s.sb("best", [P, 8])
        pt = s.ps("p_turned", [P, T])
        turned, chosen, back, chain = (s.sem("choice_" + n) for n in ("turned", "chosen", "back", "chain"))
        flat = "t b e -> t (b e)"
        with s.block() as block:
            @block.tensor
            def _(pe):
                pe.transpose(pt[:], probs.rearrange(flat), K["ident"]).then_inc(turned, 1)
                pe.wait_ge(chosen, 1)
                pe.transpose(pt[:], kept[:], K["ident"]).then_inc(back, 1)

            @block.vector
            def _(dve):
                c = Chain(dve, chain)
                dve.wait_ge(turned, 1)
                c.link(dve.tensor_copy(by_pair[:], pt[:]))
                src = by_pair
                for r in range(capacity // 8):
                    c.link(dve.max(best[:], src[:]))
                    c.link(dve.match_replace(left[:], best[:], src[:], -1.0))
                    src = left
                c.link(dve.tensor_scalar(left[:], left[:], 0.0, None, ALU.is_lt))
                dve.tensor_tensor(kept[:], by_pair[:], left[:], ALU.mult).then_inc(chosen, 1)
                dve.wait_ge(back, 1)
                dve.tensor_copy(gates.rearrange(flat), pt[:])


def l2_ffn(nc, K, w, X, XN, XT):
    F = w["L2_ffn_w1"].shape[2]
    layernorm(nc, K, X, XN, XT)
    with Stage(nc) as s:
        wg = s.sb("w_gate", [D, EXPERTS])
        probs, gates = s.sb("router_probs", [P, B, EXPERTS]), s.sb("gates", [P, B, EXPERTS])
        load(nc, s, [(wg[:], w["L2_ffn_gate_w"])])
        router(nc, K, XT, wg[:], None, top2=False, probs_out=probs)
        expert_choice(nc, K, probs[:], gates[:], 2 * T // EXPERTS)
        experts(nc, K, "l2e", XT, gates[:], X, EXPERTS, F, ACT.Gelu, w["L2_ffn_w1"], None, w["L2_ffn_w2"])


def l1_xattn(nc, K, w, X, XN, XT):
    layernorm(nc, K, X, XN, XT)
    with Stage(nc) as s:
        wcols = s.sb("w_cq_c_q", [D, 3])
        bs = s.sb("score_biases", [1, 3])
        wl, bl = s.sb("w_l", [D, 4, D]), s.sb("b_l", [1, D])
        qw = s.sb("ctx_weighted", [D, B, CTX])
        qs = s.sb("ctx_scored", [D, B, CTX])
        bsum, ball = s.sb("bias_sum", [1, 1]), s.sb("bias_all", [P, 1])
        sc = s.sb("scores", [P, B, CTX])
        top, inv = s.sb("row_max", [P, B]), s.sb("inverse_sum", [P, B])
        prT = s.sb("probs_transposed", [CTX, 2, GROUP, T])
        aT = s.sb("c2q_transposed", [D, B, T])
        bt = s.sb("b_att_transposed", [B, T])
        bm = s.sb("b_att_scalars", [B, 2])
        batt = s.sb("b_att", [P, B])
        q2c = s.sb("q2c", [D, B])
        cc = s.sb("c_times_c2q", [D, B, T])
        cq = s.sb("c_times_q2c", [D, B, T])
        load(nc, s, [(wcols[:, 0:1], column(w["L1_xattn_w_cq"])), (wcols[:, 1:2], column(w["L1_xattn_w_c"])),
                     (wcols[:, 2:3], column(w["L1_xattn_w_q"])), (bs[:, 0:1], row(w["L1_xattn_b_cq"])),
                     (bs[:, 1:2], row(w["L1_xattn_b_c"])), (bs[:, 2:3], row(w["L1_xattn_b_q"])),
                     (wl[:], w["L1_xattn_W_l"].rearrange("(c p) n -> p c n", p=P)), (bl[:], row(w["L1_xattn_b_l"]))])
        p_s = s.ps("p_scores", [P, 2, GROUP, T])
        p_t = s.ps("p_probsT", [P, GROUP, T])
        p_a = s.ps("p_c2q", [P, GROUP, T])
        p_z = s.ps("p_z", [P, 2, GROUP, D])
        p_m = s.ps("p_small", [P, 512])
        names = ("weighted bias_ready ball_ready ball_copied scores_ready scored shifted probs_ready normed turned turned_copied "
                 "c2q_ready c2q_copied tops_ready tops_turned tops_shifted b_exp b_normed b_back b_copied q2c_ready q2c_copied "
                 "products z_ready z_added chain chain_pool")
        S = {n: s.sem("x1_" + n) for n in names.split()}

        def group(g):
            return slice(GROUP * g, GROUP * g + GROUP)

        with s.block() as block:
            @block.tensor
            def _(pe):
                pe.wait_ge(S["bias_ready"], 1)
                pe.matmul(p_m[:, 0:1], K["ones"][0:1, :], bsum[:], start=True, stop=True).then_inc(S["ball_ready"], 1)

                def scores(g):
                    wait(pe, S["weighted"], 2)
                    wait(pe, S["scored"], g - 1)
                    for j in range(GROUP):
                        b = GROUP * g + j
                        pe.matmul(p_s[:, g % 2, j, 0:CTX], XT[:, b], qw[:, b], start=True, stop=False)
                        last = pe.matmul(p_s[:, g % 2, j, 0:CTX], K["ones"], qs[:, b], start=False, stop=True)
                    last.then_inc(S["scores_ready"], 1)

                def mix(g):
                    pe.wait_ge(S["normed"], g + 1)
                    wait(pe, S["turned_copied"], g)
                    for j in range(GROUP):
                        last = pe.transpose(p_t[0:CTX, j], sc[:, GROUP * g + j], K["ident"])
                    last.then_inc(S["turned"], 1)
                    pe.wait_ge(S["turned_copied"], g + 1)
                    wait(pe, S["c2q_copied"], g)
                    for j in range(GROUP):
                        last = pe.matmul(p_a[:, j], K["ctx"][:, GROUP * g + j], prT[:, g % 2, j], start=True, stop=True)
                    last.then_inc(S["c2q_ready"], 1)

                scores(0)
                for g in range(GROUPS):
                    if g < GROUPS - 1:
                        scores(g + 1)
                    mix(g)
                pe.wait_ge(S["tops_ready"], GROUPS)
                pe.wait_ge(S["ball_copied"], 1)
                pe.transpose(p_m[0:B, 0:T], top[:], K["ident"]).then_inc(S["tops_turned"], 1)
                pe.wait_ge(S["b_normed"], 1)
                pe.transpose(p_m[:, 128:128 + B], bt[:], K["ident"][0:B, 0:B]).then_inc(S["b_back"], 1)
                pe.wait_ge(S["b_copied"], 1)
                for b in range(B):
                    last = pe.matmul(p_m[:, 256 + b:257 + b], XN[:, b], batt[:, b:b + 1], start=True, stop=True)
                last.then_inc(S["q2c_ready"], 1)
                for g in range(GROUPS):
                    pe.wait_ge(S["products"], 2 * (g + 1))
                    wait(pe, S["z_added"], g - 1)
                    for j in range(GROUP):
                        b = GROUP * g + j
                        for n, part in enumerate((XT, aT, cc, cq)):
                            pe.matmul(p_z[:, g % 2, j], part[:, b], wl[:, n], start=n == 0, stop=False)
                        last = pe.matmul(p_z[:, g % 2, j], K["ones"][0:1, :], bl[:], start=False, stop=True)
                    last.then_inc(S["z_ready"], 1)

            @block.vector
            def _(dve):
                c = Chain(dve, S["chain"])
                dve.tensor_reduce(bsum[:], bs[:], AX.X, ALU.add).then_inc(S["bias_ready"], 1)
                dve.tensor_scalar(qw[:], K["ctxT"], wcols[:, 0:1], wcols[:, 1:2], ALU.mult, ALU.add).then_inc(S["weighted"], 1)
                dve.wait_ge(S["ball_ready"], 1)
                dve.tensor_copy(ball[:], p_m[:, 0:1]).then_inc(S["ball_copied"], 1)

                def softmax(g):
                    dve.wait_ge(S["scored"], g + 1)
                    dve.tensor_reduce(top[:, group(g)], sc[:, group(g)], AX.X, ALU.max).then_inc(S["tops_ready"], 1)
                    dve.wait_ge(S["tops_ready"], g + 1)
                    dve.tensor_tensor(sc[:, group(g)], sc[:, group(g)], bcast(top[:, group(g)], 2, CTX),
                                      ALU.subtract).then_inc(S["shifted"], 1)
                    dve.wait_ge(S["probs_ready"], g + 1)
                    c.link(dve.tensor_reduce(inv[:, group(g)], sc[:, group(g)], AX.X, ALU.add))
                    c.link(dve.reciprocal(inv[:, group(g)], inv[:, group(g)]))
                    dve.tensor_tensor(sc[:, group(g)], sc[:, group(g)], bcast(inv[:, group(g)], 2, CTX),
                                      ALU.mult).then_inc(S["normed"], 1)

                for g in range(GROUPS):
                    softmax(g)
                dve.wait_ge(S["tops_turned"], 1)
                c.link(dve.tensor_reduce(bm[:, 0:1], p_m[0:B, 0:T], AX.X, ALU.max))
                dve.tensor_scalar(bt[:], p_m[0:B, 0:T], bm[:, 0:1], None, ALU.subtract).then_inc(S["tops_shifted"], 1)
                dve.wait_ge(S["b_exp"], 1)
                c.link(dve.tensor_reduce(bm[:, 1:2], bt[:], AX.X, ALU.add))
                c.link(dve.reciprocal(bm[:, 1:2], bm[:, 1:2]))
                dve.tensor_scalar(bt[:], bt[:], bm[:, 1:2], None, ALU.mult).then_inc(S["b_normed"], 1)
                dve.wait_ge(S["b_back"], 1)
                dve.tensor_copy(batt[:], p_m[:, 128:128 + B]).then_inc(S["b_copied"], 1)
                dve.wait_ge(S["q2c_ready"], 1)
                dve.tensor_copy(q2c[:], p_m[:, 256:256 + B]).then_inc(S["q2c_copied"], 1)
                for g in range(GROUPS):
                    dve.wait_ge(S["c2q_copied"], g + 1)
                    dve.wait_ge(S["q2c_copied"], 1)
                    dve.tensor_tensor(cc[:, group(g)], XT[:, group(g)], aT[:, group(g)], ALU.mult).then_inc(S["products"], 1)
                    dve.tensor_tensor(cq[:, group(g)], XT[:, group(g)], bcast(q2c[:, group(g)], 2, T),
                                      ALU.mult).then_inc(S["products"], 1)
                for g in range(GROUPS):
                    dve.wait_ge(S["z_ready"], g + 1)
                    dve.tensor_tensor(X[:, group(g)], X[:, group(g)], p_z[:, g % 2], ALU.add).then_inc(S["z_added"], 1)

            @block.gpsimd
            def _(pool):
                pool.tensor_scalar(qs[:], K["ctxT"], wcols[:, 2:3], None, ALU.mult).then_inc(S["weighted"], 1)

            @block.scalar
            def _(act):
                act.wait_ge(S["ball_copied"], 1)
                for g in range(GROUPS):
                    act.wait_ge(S["scores_ready"], g + 1)
                    act.activation(sc[:, group(g)], p_s[:, g % 2, :, 0:CTX], ACT.Identity, bias=ball[:]).then_inc(S["scored"], 1)
                    act.wait_ge(S["shifted"], g + 1)
                    act.activation(sc[:, group(g)], sc[:, group(g)], ACT.Exp).then_inc(S["probs_ready"], 1)
                    act.wait_ge(S["turned"], g + 1)
                    wait(act, S["c2q_ready"], g - 1)
                    act.copy(prT[:, g % 2], p_t[0:CTX]).then_inc(S["turned_copied"], 1)
                    act.wait_ge(S["c2q_ready"], g + 1)
                    act.copy(aT[:, group(g)], p_a[:]).then_inc(S["c2q_copied"], 1)
                act.wait_ge(S["tops_shifted"], 1)
                act.activation(bt[:], bt[:], ACT.Exp).then_inc(S["b_exp"], 1)



def scan_channels(nc, K, w, xT, delta, bc, a, y):
    N = a.shape[1]
    HALF = B // 2
    with Stage(nc) as s:
        u = s.sb("delta_x", [P, B, T])
        decay = s.sb("decay", [P, 2, B, T])
        h = s.sb("states", [P, B, T])
        hc = s.sb("states_times_c", [P, 2, B, T])
        pick = s.sb("pick_row", [2 * N, 2, 2, P])
        p_b = s.ps("p_b", [P, 2, HALF, T])
        p_c = s.ps("p_c", [P, 2, HALF, T])
        names = "passed picked b_ready b_used c_ready c_used decayed cleared u_ready scanned added zeroed chain"
        S = {n: s.sem("ssm_" + n) for n in names.split()}
        flat = "p b t -> p (b t)"

        def halves(ap):
            return [ap[:, 0:HALF], ap[:, HALF:B]]

        with s.block() as block:
            @block.gpsimd
            def _(pool):
                pool.memset(y, 0.0).then_inc(S["zeroed"], 1)
                ident = K["ident"][0:2 * N, 0:2 * N].rearrange("r (k i j) -> r k i j", k=2, j=2)

                def pick_rows(n, j, i):
                    wait(pool, S["c_ready"], 2 * (n - 1), alone=S["passed"])
                    pool.tensor_copy(pick[:, j], bcast(ident[:, :, i, j], 2, P)).then_inc(S["picked"], 1)

                def clear(n, j, i):
                    wait(pool, S["decayed"], n + 1, alone=S["passed"])
                    pool.memset(decay[:, j, :, 0:1], 0.0).then_inc(S["cleared"], 1)

                def turn(n, j, i):
                    pick_rows(n, j, i)
                    clear(n, j, i)
                    if isinstance(n, int) and n == 0:
                        pool.wait_ge(S["zeroed"], 1)
                    else:
                        sum_up(n - 1, 1 - j)

                def sum_up(n, j):
                    for hf in range(2):
                        wait(pool, S["c_used"], 2 * n + hf + 1, alone=S["passed"])
                        wait(pool, S["added"], 2 * n + hf - 1, alone=S["passed"])
                        pool.tensor_tensor(halves(y)[hf], halves(y)[hf], halves(hc[:, j])[hf],
                                           ALU.add).then_inc(S["added"], 1)
                first_then_loop(pool, N, turn)
                sum_up(N - 1, 1)

            @block.tensor
            def _(pe):
                def turn(n, j, i):
                    wait(pe, S["picked"], n + 1)
                    for k, (p, ready, used) in enumerate(((p_b, "b_ready", "b_used"), (p_c, "c_ready", "c_used"))):
                        for hf in range(2):
                            wait(pe, S[used], 2 * n + hf - 1)
                            for q in range(2):
                                b = HALF * hf + GROUP * q
                                last = pe.matmul(p[:, hf, GROUP * q:GROUP * q + GROUP], pick[:, j, k], bc[:, b:b + GROUP],
                                                 start=True, stop=True)
                            last.then_inc(S[ready], 1)
                first_then_loop(pe, N, turn)

            @block.scalar
            def _(act):
                a2 = a.rearrange("p (i j) -> p i j", j=2)

                def turn(n, j, i):
                    wait(act, S["scanned"], n - 1)
                    act.activation(decay[:, j], delta, ACT.Exp, scale=a2[:, i, j:j + 1]).then_inc(S["decayed"], 1)
                first_then_loop(act, N, turn)

            @block.vector
            def _(dve):
                dve.tensor_tensor(u[:], delta, xT, ALU.mult).then_inc(S["u_ready"], 1)
                dve.wait_ge(S["u_ready"], 1)

                def turn(n, j, i):
                    wait(dve, S["added"], 2 * (n - 1))
                    for hf in range(2):
                        wait(dve, S["b_ready"], 2 * n + hf + 1)
                        dve.tensor_tensor(halves(hc[:, j])[hf], halves(u)[hf], p_b[:, hf], ALU.mult).then_inc(S["b_used"], 1)
                    wait(dve, S["b_used"], 2 * n + 2)
                    wait(dve, S["cleared"], n + 1)
                    wait(dve, S["c_used"], 2 * n)
                    dve.tensor_tensor_scan(h[:].rearrange(flat), decay[:, j].rearrange(flat), hc[:, j].rearrange(flat), 0.0,
                                           ALU.mult, ALU.add).then_inc(S["scanned"], 1)
                    wait(dve, S["scanned"], n + 1)
                    for hf in range(2):
                        wait(dve, S["c_ready"], 2 * n + hf + 1)
                        dve.tensor_tensor(halves(hc[:, j])[hf], halves(h)[hf], p_c[:, hf], ALU.mult).then_inc(S["c_used"], 1)
                first_then_loop(dve, N, turn)


def l3_attn(nc, K, w, X, XN, XT):
    N = w["L3_attn_A_log"].shape[1]
    F = w["L3_attn_W1"].shape[1]
    layernorm(nc, K, X, XN, XT)
    with Stage(nc) as s:
        cols = s.sb("columns", [D, 6])
        g1, b1, g2, b2, bd, dskip = (cols[:, k:k + 1] for k in range(6))
        wd, wbc, bbc = s.sb("w_delta", [D, D]), s.sb("w_bc", [D, 2 * N]), s.sb("b_bc", [2 * N, 1])
        a, bout = s.sb("a", [D, N]), s.sb("b_2", [1, D])
        ssm = s.sb("ssm_out", [P, B, D])
        load(nc, s, [(g1, column(w["L3_attn_ln1_g"])), (b1, column(w["L3_attn_ln1_b"])), (g2, column(w["L3_attn_ln2_g"])),
                     (b2, column(w["L3_attn_ln2_b"])), (bd, column(w["L3_attn_bd"])), (dskip, column(w["L3_attn_D"])),
                     (wd[:], w["L3_attn_Wd"]), (wbc[:], w["L3_attn_Wbc"]), (bbc[:], column(w["L3_attn_bbc"])),
                     (a[:], w["L3_attn_A_log"]), (bout[:], row(w["L3_attn_b2"]))])
        layernorm(nc, K, XN, ssm[:], XT, scale=g1, bias=b1)
        with Stage(nc) as s2:
            delta, bc, y = s2.sb("delta", [P, B, T]), s2.sb("b_and_c", [2 * N, B, T]), s2.sb("y", [P, B, T])
            with Stage(nc) as s3:
                z, soft = s3.sb("z", [P, B, T]), s3.sb("softplus", [P, B, T])
                p = s3.ps("p_delta", [P, 2, GROUP, T])
                pb = s3.ps("p_bc", [P, 2, GROUP, T])
                ready, copied, z_ready, a_ready, chain = (s3.sem("delta_" + n) for n in ("ready", "copied", "z", "a", "chain"))
                with s3.block() as block:
                    @block.tensor
                    def _(pe):
                        for g in range(GROUPS):
                            part = XT[:, GROUP * g:GROUP * g + GROUP]
                            wait(pe, copied, g - 1)
                            pe.matmul(p[:, g % 2], wd[:], part, start=True, stop=True)
                            pe.matmul(pb[0:2 * N, g % 2], wbc[:], part, start=True, stop=True).then_inc(ready, 1)

                    @block.scalar
                    def _(act):
                        c = Chain(act, chain)
                        c.link(act.activation(a[:], a[:], ACT.Exp))
                        act.mul(a[:], a[:], -1.0)
                        for g in range(GROUPS):
                            act.wait_ge(ready, g + 1)
                            part = slice(GROUP * g, GROUP * g + GROUP)
                            act.activation(z[:, part], p[:, g % 2], ACT.Identity, bias=bd)
                            act.activation(bc[:, part], pb[0:2 * N, g % 2], ACT.Identity, bias=bbc[:]).then_inc(copied, 1)
                        act.wait_ge(copied, GROUPS)
                        c.link(act.activation(soft[:], z[:], ACT.Abs))
                        c.link(act.activation(soft[:], soft[:], ACT.Exp, scale=-1.0))
                        act.activation(soft[:], soft[:], ACT.Ln, bias=1.0).then_inc(z_ready, 1)

                    @block.vector
                    def _(dve):
                        dve.wait_ge(z_ready, 1)
                        dve.scalar_tensor_tensor(delta[:], z[:], 0.0, soft[:], ALU.max, ALU.add)
            scan_channels(nc, K, w, XT, delta[:], bc[:], a[:], y[:])
            with Stage(nc) as s3:
                p = s3.ps("p_turned", [P, GROUPS, GROUP, D])
                pbias = s3.ps("p_bias", [P, D])
                bias = s3.sb("bias_rows", [P, D])
                skip, turned, bias_ready, chain = (s3.sem("ssmout_" + n) for n in ("skip", "turned", "bias", "chain"))
                with s3.block() as block:
                    @block.tensor
                    def _(pe):
                        pe.matmul(pbias[:], K["ones"][0:1, :], bout[:], start=True, stop=True).then_inc(bias_ready, 1)
                        pe.wait_ge(skip, 1)
                        for g in range(GROUPS):
                            for j in range(GROUP):
                                last = pe.transpose(p[:, g, j], y[:, GROUP * g + j], K["ident"])
                            last.then_inc(turned, 1)

                    @block.vector
                    def _(dve):
                        c = Chain(dve, chain)
                        dve.scalar_tensor_tensor(y[:], XT, dskip, y[:], ALU.mult, ALU.add).then_inc(skip, 1)
                        dve.wait_ge(bias_ready, 1)
                        c.link(dve.tensor_copy(bias[:], pbias[:]))
                        c.link(dve.tensor_tensor(X, X, bcast(bias[:], 1, B), ALU.add))
                        for g in range(GROUPS):
                            part = slice(GROUP * g, GROUP * g + GROUP)
                            dve.wait_ge(turned, g + 1)
                            c.link(dve.tensor_tensor(ssm[:, part], XN[:, part], p[:, g], ALU.add))
                            c.link(dve.tensor_tensor(X[:, part], X[:, part], ssm[:, part], ALU.add))
        layernorm(nc, K, ssm[:], XN, XT, scale=g2, bias=b2)
        gates = s.sb("gates_of_one", [P, B, 2])
        with s.block() as block:
            @block.vector
            def _(dve):
                dve.memset(gates[:], 1.0)
        experts(nc, K, "l3m", XT, gates[:], X, 2, F // 2, ACT.Gelu, w["L3_attn_W1"].rearrange("d (e f) -> e d f", e=2), None,
                w["L3_attn_W2"].rearrange("(e f) d -> e f d", e=2), b_in=w["L3_attn_b1"].rearrange("p (e c) -> e p c", e=2))


def l3_xattn(nc, K, w, X, XN, XT):
    layernorm(nc, K, X, XN, XT)
    BIG = 1e30
    I, J = CTX, T
    with Stage(nc) as s:
        path = s.sb("path", [I, B, J])
        with Stage(nc) as s2:
            lf = s2.sb("dist_then_left", [B, I, J + 1])
            R = s2.sb("cost_then_path", [B, I + 1, J + 1])
            W = s2.sb("diag_and_up", [B, I, 2, J], BF16)
            with Stage(nc) as s3:
                dist = s3.sb("distances", [I, B, J])
                sq = s3.sb("squares", [P, 2, GROUP, T])
                cm = s3.sb("ctxT_times_minus_2", [D, B, CTX])
                csq = s3.sb("ctx_squares", [CTX, B, D])
                aa = s3.sb("ctx_norms", [CTX, B])
                p_d = s3.ps("p_dist", [P, 2, GROUP, T])
                names = "scaled squared csq_ready dist_ready dist_copied rooted moved chain"
                S = {n: s3.sem("dist_" + n) for n in names.split()}

                def group(g):
                    return slice(GROUP * g, GROUP * g + GROUP)

                with s3.block() as block:
                    @block.gpsimd
                    def _(pool):
                        pool.tensor_scalar(cm[:], K["ctxT"], -2.0, None, ALU.mult).then_inc(S["scaled"], 1)

                    @block.scalar
                    def _(act):
                        act.activation(csq[:], K["ctx"], ACT.Square).then_inc(S["csq_ready"], 1)
                        for g in range(GROUPS):
                            wait(act, S["dist_ready"], g - 1)
                            act.activation(sq[:, g % 2], XT[:, group(g)], ACT.Square).then_inc(S["squared"], 1)
                        for g in range(GROUPS):
                            act.wait_ge(S["dist_copied"], g + 1)
                            act.activation(dist[:, group(g)], dist[:, group(g)], ACT.Sqrt).then_inc(S["rooted"], 1)

                    @block.tensor
                    def _(pe):
                        pe.wait_ge(S["scaled"], 1)
                        for g in range(GROUPS):
                            pe.wait_ge(S["squared"], g + 1)
                            wait(pe, S["dist_copied"], g - 1)
                            for j in range(GROUP):
                                pe.matmul(p_d[0:CTX, g % 2, j], cm[:, GROUP * g + j], XT[:, GROUP * g + j],
                                          start=True, stop=False)
                                last = pe.matmul(p_d[0:CTX, g % 2, j], K["ones"][:, 0:CTX], sq[:, g % 2, j],
                                                 start=False, stop=True)
                            last.then_inc(S["dist_ready"], 1)

                    @block.vector
                    def _(dve):
                        c = Chain(dve, S["chain"])
                        dve.wait_ge(S["csq_ready"], 1)
                        c.link(dve.tensor_reduce(aa[:], csq[:], AX.X, ALU.add))
                        for g in range(GROUPS):
                            dve.wait_ge(S["dist_ready"], g + 1)
                            c.link(dve.tensor_tensor(dist[:, group(g)], p_d[0:CTX, g % 2], bcast(aa[:, group(g)], 2, T), ALU.add))
                            dve.tensor_scalar(dist[:, group(g)], dist[:, group(g)], 0.0, None, ALU.max).then_inc(S["dist_copied"], 1)

                    @block.sync
                    def _(sp):
                        for b in range(B):
                            sp.wait_ge(S["rooted"], b // GROUP + 1)
                            sp.dma_start(lf[b:b + 1, :, 0:J], dist[:, b]).then_inc(S["moved"], 16)
                        sp.wait_ge(S["moved"], 16 * B)
            with Stage(nc) as s3:
                best = s3.sb("best_before", [B, J])
                taken = s3.sb("taken", [B, 2, J + 1])
                inflow = s3.sb("inflow", [B, J])
                chain = s3.sem("dtw_chain")
                fwd, back = s3.sem("dtw_forward"), s3.sem("dtw_back")
                moved = s3.sem("dtw_moved")
                on_row = s3.sb("path_row", [B, 2, J])
                left_row = s3.sb("left_row", [B, 2, J + 1])
                chosen, left_copied, row_ready, row_stored, passed = (
                    s3.sem("dtw_" + n) for n in ("chosen", "left_copied", "row_ready", "row_stored", "passed"))
                on = R[:, 0:I, 0:J]
                o_pairs = R[:, 0:I - 1, 0:J].rearrange("b (i a) j -> b i a j", a=2)
                l_pairs = lf[:, 0:I - 1].rearrange("b (i a) j -> b i a j", a=2)
                w_pairs = W[:, 1:I].rearrange("b (i a) m j -> b i a m j", a=2)
                with s3.block() as block:
                    @block.vector
                    def _(dve):
                        c = Chain(dve, chain)
                        c.link(dve.memset(R[:, 0], BIG))
                        c.link(dve.memset(R[:, :, 0:1], BIG))
                        c.link(dve.memset(R[:, 0, 0:1], 0.0))
                        before, now = R[:, 0:I], R[:, 1:I + 1]
                        f = Chain(dve, fwd, 2)
                        with dve.Fori(0, I) as i:
                            f.turn(i)
                            f.link(dve.tensor_tensor(best[:], before[:, i, 0:J], before[:, i, 1:J + 1], ALU.min))
                            f.link(dve.tensor_tensor_scan(now[:, i, 1:J + 1], best[:], lf[:, i, 0:J], BIG, ALU.min, ALU.add))
                        diag, up, left = before[:, :, 0:J], before[:, :, 1:J + 1], now[:, :, 0:J]
                        wd, wu, wl = W[:, :, 0], W[:, :, 1], lf[:, :, 0:J]
                        c.link(dve.tensor_tensor(wl, up, left, ALU.min))
                        c.link(dve.tensor_tensor(wd, diag, wl, ALU.is_le))
                        c.link(dve.tensor_tensor(wu, up, left, ALU.is_le))
                        c.link(dve.tensor_tensor(wl, wd, wu, ALU.max))
                        c.link(dve.tensor_tensor(wu, wu, wd, ALU.is_gt))
                        c.link(dve.tensor_scalar(wl, wl, -1.0, 1.0, ALU.mult, ALU.add))
                        c.link(dve.memset(lf[:, :, J:J + 1], 0.0))
                        dve.memset(taken[:], 0.0)
                        c.link(dve.memset(inflow[:], 0.0))
                        c.link(dve.memset(inflow[:, J - 1:J], 1.0))

                        def row_back(j):
                            return dve.tensor_tensor_scan(on_row[:, j, ::-1], left_row[:, j, J:0:-1], inflow[:, ::-1], 0.0,
                                                          ALU.mult, ALU.add)
                        dve.engine_nop().then_inc(chosen, 1)
                        dve.wait_ge(left_copied, 1)
                        row_back(0).then_inc(row_ready, 1)
                        k = Chain(dve, back, 2)
                        with dve.Fori(0, (I - 1) // 2) as n:
                            for j in range(2):
                                m = n * 2 + j
                                k.turn(m)
                                wait(dve, row_ready, m + 1, alone=passed)
                                k.link(dve.tensor_tensor(taken[:, :, 0:J], bcast(on_row[:, j], 1, 2),
                                                         w_pairs[:, (I - 1) // 2 - 1 - n, 1 - j], ALU.mult))
                                k.link(dve.tensor_tensor(inflow[:], taken[:, 0, 1:J + 1], taken[:, 1, 0:J], ALU.add))
                                dve.wait_ge(left_copied, m + 2)
                                dve.wait_ge(row_stored, n * 2 + 1)
                                row_back(1 - j).then_inc(row_ready, 1)

                    @block.scalar
                    def _(act):
                        act.wait_ge(chosen, 1)
                        act.copy(left_row[:, 0], lf[:, I - 1]).then_inc(left_copied, 1)
                        with act.Fori(0, (I - 1) // 2) as n:
                            for j in range(2):
                                act.wait_ge(row_ready, n * 2 + 1)
                                act.copy(left_row[:, 1 - j], l_pairs[:, (I - 1) // 2 - 1 - n, 1 - j]).then_inc(left_copied, 1)

                    @block.gpsimd
                    def _(pool):
                        pool.wait_ge(row_ready, 1)
                        pool.tensor_copy(on[:, I - 1], on_row[:, 0]).then_inc(row_stored, 1)
                        with pool.Fori(0, (I - 1) // 2) as n:
                            for j in range(2):
                                wait(pool, row_ready, n * 2 + (j + 2), alone=passed)
                                pool.tensor_copy(o_pairs[:, (I - 1) // 2 - 1 - n, 1 - j], on_row[:, 1 - j]).then_inc(row_stored, 1)

                    @block.sync
                    def _(sp):
                        sp.wait_ge(row_stored, I)
                        for b in range(B):
                            sp.dma_start(path[:, b], R[b:b + 1, 0:I, 0:J]).then_inc(moved, 16)
                        sp.wait_ge(moved, 16 * B)
        with Stage(nc) as s2:
            p = s2.ps("p_expanded", [P, GROUPS, GROUP, D])
            ready = s2.sem("expanded")
            with s2.block() as block:
                @block.tensor
                def _(pe):
                    for g in range(GROUPS):
                        for j in range(GROUP):
                            last = pe.matmul(p[:, g, j], path[:, GROUP * g + j], K["ctx"][:, GROUP * g + j], start=True, stop=True)
                        last.then_inc(ready, 1)

                @block.vector
                def _(dve):
                    for g in range(GROUPS):
                        part = slice(GROUP * g, GROUP * g + GROUP)
                        dve.wait_ge(ready, g + 1)
                        dve.tensor_tensor(X[:, part], X[:, part], p[:, g], ALU.add)



FIR_DVE, FIR_POOL = 33, 14
H4, DH = 4, 32
CONV, SHORT, LONG = 4, 5, 64


def by_head(ap):
    return ap.rearrange("t b (h d) -> t (b h) d", d=DH)


def taps(nc, K, w, XT, q_tok, k_tok, v_tok, fs_tok, fl_tok):
    PRODUCTS = 4
    PAD = LONG - 1
    FIR_PE = LONG - FIR_DVE - FIR_POOL
    HALF = B // 2
    with Stage(nc) as s:
        wqkv = s.sb("w_qkv", [D, 3, D])
        cw = s.sb("conv_taps", [P, 3, CONV])
        fl, fs = s.sb("fir_long", [P, LONG]), s.sb("fir_short", [P, SHORT])
        pre = s.sb("projected", [P, B, CONV - 1 + T])
        y = s.sb("convolved", [P, B, T])
        qk = s.sb("silu_qk", [P, B, T])
        vp = s.sb("v_padded", [P, B, PAD + T])
        diag = s.sb("diagonals", [P, FIR_PE + SHORT, P])
        product = s.sb("products", [P, PRODUCTS, HALF, T])
        part_dve, part_pool = s.sb("part_dve", [P, B, T]), s.sb("part_pool", [P, B, T])
        f = s.sb("filtered", [P, B, T])
        load(nc, s, [(wqkv[:, 0], w["L2_attn_Wq"]), (wqkv[:, 1], w["L2_attn_Wk"]), (wqkv[:, 2], w["L2_attn_Wv"]),
                     (cw[:, 0], w["L2_attn_conv_q"]), (cw[:, 1], w["L2_attn_conv_k"]), (cw[:, 2], w["L2_attn_conv_v"]),
                     (fl[:], w["L2_attn_fir_long"].rearrange("h d k -> (h d) k")),
                     (fs[:], w["L2_attn_fir_short"].rearrange("h d k -> (h d) k"))])
        p = s.ps("p_wide", [P, GROUPS, GROUP, T])
        pt = s.ps("p_turned", [P, GROUPS, GROUP, T])
        S = {n: s.sem("taps_" + n) for n in
             "padded projected copied convolved active diag_ready filtered_ready filtered turned turned_copied chain "
             "product pool_added".split()}

        def group(g):
            return slice(GROUP * g, GROUP * g + GROUP)

        halves = (slice(0, HALF), slice(HALF, B))

        with s.block() as block:
            @block.gpsimd
            def _(pool):
                pool.memset(pre[:, :, 0:CONV - 1], 0.0).then_inc(S["padded"], 1)
                pool.memset(vp[:, :, 0:PAD], 0.0).then_inc(S["padded"], 1)
                pool.tensor_tensor(diag[:, FIR_PE:], bcast(K["ident"], 1, SHORT), bcast(fs[:], 2, P), ALU.mult)
                pool.tensor_tensor(diag[:, 0:FIR_PE], bcast(K["ident"], 1, FIR_PE), bcast(fl[:, 0:FIR_PE], 2, P),
                                   ALU.mult).then_inc(S["diag_ready"], 1)
                for u in range(2 * FIR_POOL):
                    b = halves[u % 2]
                    pool.wait_ge(S["product"], u + 1)
                    wait(pool, S["pool_added"], u - 1)
                    if u < 2:
                        ins = pool.tensor_copy(part_pool[:, b], product[:, u % PRODUCTS])
                    else:
                        ins = pool.tensor_tensor(part_pool[:, b], part_pool[:, b], product[:, u % PRODUCTS], ALU.add)
                    ins.then_inc(S["pool_added"], 1)

            @block.tensor
            def _(pe):
                def turn_back(src, k):
                    for g in range(GROUPS):
                        wait(pe, S["turned_copied"], 4 * (k - 1) + g + 1)
                        for j in range(GROUP):
                            last = pe.transpose(pt[:, g, j], src[:, GROUP * g + j], K["ident"])
                        last.then_inc(S["turned"], 1)

                def project(m):
                    for g in range(GROUPS):
                        wait(pe, S["copied"], 4 * (m - 1) + g + 1)
                        pe.matmul(p[:, g], wqkv[:, m], XT[:, group(g)], start=True, stop=True).then_inc(S["projected"], 1)

                def fir(at, count, first, k):
                    for g in range(GROUPS):
                        wait(pe, S["copied"], 12)
                        wait(pe, S["filtered"], 4 * (k - 1) + g + 1)
                        for n in range(count):
                            last = pe.matmul(p[:, g], diag[:, at + n], vp[:, group(g), first + n:first + n + T],
                                             start=n == 0, stop=n == count - 1)
                        last.then_inc(S["filtered_ready"], 1)

                project(0)
                project(1)
                pe.wait_ge(S["active"], 1)
                turn_back(qk, 0)
                project(2)
                pe.wait_ge(S["active"], 2)
                turn_back(qk, 1)
                pe.wait_ge(S["active"], 3)
                turn_back(vp[:, :, PAD:], 2)
                pe.wait_ge(S["diag_ready"], 1)
                fir(FIR_PE, SHORT, LONG - SHORT, 0)
                pe.wait_ge(S["filtered"], 4)
                turn_back(f, 3)
                fir(0, FIR_PE, 0, 1)
                pe.wait_ge(S["filtered"], 8)
                turn_back(f, 4)

            @block.vector
            def _(dve):
                c = Chain(dve, S["chain"])
                dve.wait_ge(S["padded"], 2)
                for m in range(3):
                    dve.wait_ge(S["copied"], 4 * (m + 1))
                    wait(dve, S["active"], m)
                    for k in range(CONV):
                        src = pre[:, :, k:k + T]
                        if k == 0:
                            ins = dve.tensor_scalar(y[:], src, cw[:, m, 0:1], None, ALU.mult)
                        else:
                            ins = dve.scalar_tensor_tensor(y[:], src, cw[:, m, k:k + 1], y[:], ALU.mult, ALU.add)
                        if k < CONV - 1:
                            c.link(ins)
                    ins.then_inc(S["convolved"], 1)
                dve.wait_ge(S["active"], 3)
                for n in range(FIR_PE, FIR_PE + FIR_DVE):
                    for b in halves:
                        src, tap = vp[:, b, n:n + T], fl[:, n:n + 1]
                        if n == FIR_PE:
                            ins = dve.tensor_scalar(part_dve[:, b], src, tap, None, ALU.mult)
                        else:
                            ins = dve.scalar_tensor_tensor(part_dve[:, b], src, tap, part_dve[:, b], ALU.mult, ALU.add)
                        c.link(ins, lag=1)
                wait(dve, S["chain"], c.k)
                dve.wait_ge(S["pool_added"], 2 * FIR_POOL)
                c.link(dve.tensor_tensor(part_dve[:], part_dve[:], part_pool[:], ALU.add))
                for g in range(GROUPS):
                    dve.wait_ge(S["filtered_ready"], 4 + g + 1)
                    dve.tensor_tensor(f[:, group(g)], p[:, g], part_dve[:, group(g)], ALU.add).then_inc(S["filtered"], 1)

            @block.scalar
            def _(act):
                def project_out(m):
                    wait(act, S["padded"], 2)
                    wait(act, S["convolved"], m)
                    for g in range(GROUPS):
                        act.wait_ge(S["projected"], 4 * m + g + 1)
                        act.copy(pre[:, group(g), CONV - 1:], p[:, g]).then_inc(S["copied"], 1)

                def activate(m, dst):
                    act.wait_ge(S["convolved"], m + 1)
                    act.activation(dst, y[:], ACT.Silu).then_inc(S["active"], 1)

                units = iter(range(2 * FIR_POOL))

                def products(count):
                    for u in islice(units, count):
                        n = FIR_PE + FIR_DVE + u // 2
                        wait(act, S["pool_added"], u - PRODUCTS + 1)
                        act.activation(product[:, u % PRODUCTS], vp[:, halves[u % 2], n:n + T], ACT.Copy,
                                       scale=fl[:, n:n + 1]).then_inc(S["product"], 1)

                def turned_out(k, dst):
                    for g in range(GROUPS):
                        act.wait_ge(S["turned"], 4 * k + g + 1)
                        act.copy(dst[:, group(g)], pt[:, g]).then_inc(S["turned_copied"], 1)
                        if k in (2, 3):
                            products(3)

                def filtered_out():
                    for g in range(GROUPS):
                        act.wait_ge(S["filtered_ready"], g + 1)
                        act.copy(f[:, group(g)], p[:, g]).then_inc(S["filtered"], 1)

                project_out(0)
                activate(0, qk[:])
                project_out(1)
                turned_out(0, q_tok)
                activate(1, qk[:])
                project_out(2)
                turned_out(1, k_tok)
                activate(2, vp[:, :, PAD:])
                act.wait_ge(S["active"], 3)
                products(2)
                turned_out(2, v_tok)
                filtered_out()
                turned_out(3, fs_tok)
                products(2 * FIR_POOL)
                turned_out(4, fl_tok)


def delta_scales(nc, K, w, XT, q_tok, k_tok, v_tok, vb, beta, rq, rk):
    with Stage(nc) as s:
        wb = s.sb("w_beta", [D, H4])
        load(nc, s, [(wb[:], w["L2_attn_Wb"])])
        sq = s.sb("squares", [P, 2, B, D])
        p = s.ps("p_beta", [P, B, H4])
        beta_p, beta_ready, squared, summed, rooted, chain = (
            s.sem("dscale_" + n) for n in ("beta_p", "beta", "squared", "summed", "rooted", "chain"))
        with s.block() as block:
            @block.tensor
            def _(pe):
                for b in range(B):
                    last = pe.matmul(p[:, b], XT[:, b], wb[:], start=True, stop=True)
                last.then_inc(beta_p, 1)

            @block.scalar
            def _(act):
                act.activation(sq[:, 0], q_tok, ACT.Square).then_inc(squared, 1)
                act.activation(sq[:, 1], k_tok, ACT.Square).then_inc(squared, 1)
                act.wait_ge(beta_p, 1)
                act.activation(beta, p[:], ACT.Sigmoid).then_inc(beta_ready, 1)
                act.wait_ge(summed, 2)
                act.activation(rq, rq, ACT.Sqrt)
                act.activation(rk, rk, ACT.Sqrt).then_inc(rooted, 1)

            @block.vector
            def _(dve):
                c = Chain(dve, chain)
                for m, r in enumerate((rq, rk)):
                    dve.wait_ge(squared, m + 1)
                    flat = r.rearrange("p b h -> p (b h)")
                    c.link(dve.tensor_reduce(flat, by_head(sq[:, m]), AX.X, ALU.add))
                    dve.tensor_scalar(r, r, 1e-6, None, ALU.add).then_inc(summed, 1)
                dve.wait_ge(beta_ready, 1)
                dve.tensor_tensor(by_head(vb), by_head(v_tok), bcast(beta.rearrange("p b h -> p (b h)"), 2, DH), ALU.mult)
                dve.wait_ge(rooted, 1)
                dve.reciprocal(rq, rq)
                dve.reciprocal(rk, rk)


def delta_rule(nc, K, q_tok, k_tok, vb, beta, rq, rk, out):
    NL = LEVELS - 1
    with Stage(nc) as s:
        st = s.sb("scaled_tok", [P, 2, 3, D])
        ft = s.sb("scaled_ch", [P, 2, 3, T])
        fsp = s.sb("scaled_ch_spread", [P, 2, 3, H4, T])
        at = s.sb("a_turned", [P, 2, H4, T])
        atl = s.sb("a_by_level", [P, 2, NL, H4, T])
        lt = s.sb("local_turned", [P, 2, H4, T])
        x = s.sb("x_inverse", [P, 2, H4, T])
        yv = s.sb("y_inverse_turned", [P, 2, H4, T])
        t1 = s.sb("a_times_x", [P, 2, H4, T])
        u = s.sb("u", [P, 2, D])
        p1 = s.ps("p_one", [P, 2, H4, T])
        px = s.ps("p_x", [P, 2, H4, T])
        py = s.ps("p_y", [P, 2, H4, T])
        pu = s.ps("p_u", [P, 2, 512])
        names = ("passed scaled turned turned_copied a_ready a_masked local_ready local_masked levels_ready xy_started ax_ready "
                 "ax_copied step_ready updated u_ready u_copied o_ready stored chain_scale chain_mask chain_pool")
        S = {n: s.sem("delta_" + n) for n in names.split()}
        h3 = "p (h d) -> p h d"

        def tile4(ap):
            return bcast(ap, 1, H4)

        with s.block() as block:
            @block.gpsimd
            def _(pool):
                with pool.Fori(0, B // 2) as i:
                    for j in range(2):
                        wait(pool, S["a_masked"], i * 2 + (j + 1), alone=S["passed"])
                    for level in range(NL):
                        for j in range(2):
                            pool.tensor_tensor(atl[:, j, level], at[:, j], tile4(K[f"level{level + 1}"]),
                                               ALU.mult).then_inc(S["levels_ready"], 1)

            @block.vector
            def _(dve):
                cs = Chain(dve, S["chain_scale"], 2)
                cm = Chain(dve, S["chain_mask"], 4, alone=S["passed"])
                q4, k4, r_q, r_k, bt = (pairs(t) for t in (q_tok, k_tok, rq, rk, beta))
                out4 = pairs(out)
                with dve.Fori(0, B // 2) as i:
                    cs.turn(i)
                    for j in range(2):
                        kn, kb, qn = (st[:, j, m].rearrange(h3, d=DH) for m in range(3))
                        cs.link(dve.tensor_tensor(kn, k4[:, i, j].rearrange(h3, d=DH), bcast(r_k[:, i, j], 2, DH), ALU.mult))
                        dve.tensor_tensor(kb, kn, bcast(bt[:, i, j], 2, DH), ALU.mult)
                        dve.tensor_tensor(qn, q4[:, i, j].rearrange(h3, d=DH), bcast(r_q[:, i, j], 2, DH),
                                          ALU.mult).then_inc(S["scaled"], 1)
                    cm.turn(i)
                    for j in range(2):
                        dve.wait_ge(S["a_ready"], i * 2 + j + 1)
                        dve.tensor_tensor(at[:, j], py[:, j], tile4(K["before"]), ALU.mult).then_inc(S["a_masked"], 1)
                        dve.tensor_tensor(yv[:, j], py[:, j], tile4(K["level0"]), ALU.mult)
                        cm.link(dve.tensor_tensor(x[:, j], px[:, j], tile4(K["level0_lower"]), ALU.mult))
                        dve.tensor_tensor(yv[:, j], tile4(K["ident"]), yv[:, j], ALU.subtract)
                        dve.tensor_tensor(x[:, j], tile4(K["ident"]), x[:, j], ALU.subtract).then_inc(S["xy_started"], 1)
                        dve.wait_ge(S["local_ready"], i * 2 + j + 1)
                        cm.link(dve.tensor_tensor(lt[:, j], p1[:, j], tile4(K["upto"]), ALU.mult))
                        dve.sem_inc(S["local_masked"], 1)
                    for level in range(NL):
                        for j in range(2):
                            dve.wait_ge(S["step_ready"], i * (2 * NL) + (level * 2 + j + 1))
                            if level < NL - 1:
                                dve.tensor_tensor(x[:, j], x[:, j], px[:, j], ALU.subtract)
                            dve.tensor_tensor(yv[:, j], yv[:, j], py[:, j], ALU.subtract).then_inc(S["updated"], 1)
                    for j in range(2):
                        dve.wait_ge(S["u_ready"], i * 2 + j + 1)
                        dve.tensor_copy(u[:, j], pu[:, j, 0:D]).then_inc(S["u_copied"], 1)
                    for j in range(2):
                        dve.wait_ge(S["o_ready"], i * 2 + j + 1)
                        dve.tensor_copy(out4[:, i, j], pu[:, j, 128:128 + D]).then_inc(S["stored"], 1)

            @block.scalar
            def _(act):
                with act.Fori(0, B // 2) as i:
                    for j in range(2):
                        act.wait_ge(S["turned"], i * 2 + j + 1)
                        for h in range(H4):
                            act.activation(fsp[:, j, :, h], p1[:, j, 0:3], ACT.Identity, scale=K["headmask32"][:, h:h + 1])
                        act.copy(ft[:, j], p1[:, j, 0:3]).then_inc(S["turned_copied"], 1)
                    for level in range(NL):
                        for j in range(2):
                            act.wait_ge(S["ax_ready"], i * (2 * NL) + (level * 2 + j + 1))
                            act.copy(t1[:, j], p1[:, j]).then_inc(S["ax_copied"], 1)

            @block.tensor
            def _(pe):
                vb4 = pairs(vb)
                with pe.Fori(0, B // 2) as i:
                    for j in range(2):
                        pe.wait_ge(S["scaled"], i * 2 + j + 1)
                        for m in range(3):
                            last = pe.transpose(p1[:, j, m], st[:, j, m], K["ident"])
                        last.then_inc(S["turned"], 1)
                    for j in range(2):
                        pe.wait_ge(S["turned_copied"], i * 2 + j + 1)
                        pe.matmul(py[:, j], ft[:, j, 0], fsp[:, j, 1], start=True, stop=True)
                        pe.matmul(px[:, j], ft[:, j, 1], fsp[:, j, 0], start=True, stop=True).then_inc(S["a_ready"], 1)
                        pe.matmul(p1[:, j], ft[:, j, 0], fsp[:, j, 2], start=True, stop=True).then_inc(S["local_ready"], 1)
                    for level in range(NL):
                        for j in range(2):
                            if level == 0:
                                pe.wait_ge(S["xy_started"], i * 2 + j + 1)
                                pe.wait_ge(S["local_masked"], i * 2 + j + 1)
                            else:
                                pe.wait_ge(S["updated"], i * (2 * NL) + (level * 2 + j - 1))
                            pe.wait_ge(S["levels_ready"], i * (2 * NL) + (level * 2 + j + 1))
                            for h in range(H4):
                                last = pe.matmul(p1[:, j, h], atl[:, j, level, h], x[:, j, h], start=True, stop=True)
                            last.then_inc(S["ax_ready"], 1)
                        for j in range(2):
                            pe.wait_ge(S["ax_copied"], i * (2 * NL) + (level * 2 + j + 1))
                            for h in range(H4):
                                if level < NL - 1:
                                    pe.matmul(px[:, j, h], yv[:, j, h], t1[:, j, h], start=True, stop=True)
                                last = pe.matmul(py[:, j, h], t1[:, j, h], yv[:, j, h], start=True, stop=True)
                            last.then_inc(S["step_ready"], 1)
                    for j in range(2):
                        pe.wait_ge(S["updated"], i * (2 * NL) + ((NL - 1) * 2 + j + 1))
                        for h in range(H4):
                            c = slice(DH * h, DH * h + DH)
                            last = pe.matmul(pu[:, j, c], yv[:, j, h], vb4[:, i, j, c], start=True, stop=True)
                        last.then_inc(S["u_ready"], 1)
                    for j in range(2):
                        pe.wait_ge(S["u_copied"], i * 2 + j + 1)
                        for h in range(H4):
                            c = slice(DH * h, DH * h + DH)
                            last = pe.matmul(pu[:, j, 128 + DH * h:128 + DH * h + DH], lt[:, j, h], u[:, j, c],
                                             start=True, stop=True)
                        last.then_inc(S["o_ready"], 1)
                    pe.wait_ge(S["stored"], i * 2 + 2)


def head_stats(nc, K, sources, stats):
    with Stage(nc) as s:
        sq, dev = s.sb("squares", [P, 2, B, D]), s.sb("deviations", [P, 2, B, D])
        m = s.sb("means", [P, 2, B * H4])
        sums = s.sb("sums", [P, 4, 3, B * H4])
        S = {n: s.sem("stats_" + n) for n in "squared mean_ready deviated dev_squared used summed chain".split()}
        with s.block() as block:
            @block.gpsimd
            def _(pool):
                for k, src in enumerate(sources):
                    pool.wait_ge(S["mean_ready"], k + 1)
                    wait(pool, S["used"], k - 1)
                    pool.tensor_tensor(by_head(dev[:, k % 2]), by_head(src), bcast(m[:, k % 2], 2, DH),
                                       ALU.subtract).then_inc(S["deviated"], 1)

            @block.scalar
            def _(act):
                for k, src in enumerate(sources):
                    wait(act, S["used"], k - 1)
                    act.activation(sq[:, k % 2], src, ACT.Square).then_inc(S["squared"], 1)
                    act.wait_ge(S["deviated"], k + 1)
                    act.activation(dev[:, k % 2], dev[:, k % 2], ACT.Square).then_inc(S["dev_squared"], 1)
                act.wait_ge(S["summed"], 1)
                for k in range(len(sources)):
                    act.activation(stats[:, :, :, 4 * k + 3], sums[:, k, 2].rearrange("p (b h) -> p b h", h=H4), ACT.Sqrt)

            @block.vector
            def _(dve):
                c = Chain(dve, S["chain"])
                for k, src in enumerate(sources):
                    b3 = "p (b h) -> p b h"
                    c.link(dve.tensor_reduce(m[:, k % 2], by_head(src), AX.X, ALU.add))
                    dve.tensor_scalar(m[:, k % 2], m[:, k % 2], 1.0 / DH, None, ALU.mult).then_inc(S["mean_ready"], 1)
                    dve.tensor_reduce(sums[:, k, 0], by_head(src), AX.X, ALU.add, apply_absolute_value=True)
                    dve.wait_ge(S["squared"], k + 1)
                    dve.tensor_reduce(sums[:, k, 2], by_head(sq[:, k % 2]), AX.X, ALU.add)
                    dve.wait_ge(S["dev_squared"], k + 1)
                    c.link(dve.tensor_reduce(sums[:, k, 1], by_head(dev[:, k % 2]), AX.X, ALU.add))
                    dve.engine_nop().then_inc(S["used"], 1)
                    dve.tensor_copy(stats[:, :, :, 4 * k], m[:, k % 2].rearrange(b3, h=H4))
                    dve.tensor_scalar(stats[:, :, :, 4 * k + 1], sums[:, k, 1].rearrange(b3, h=H4), 1.0 / DH, None, ALU.mult)
                    c.link(dve.tensor_scalar(stats[:, :, :, 4 * k + 2], sums[:, k, 0].rearrange(b3, h=H4), 1.0 / DH, None, ALU.mult))
                dve.engine_nop().then_inc(S["summed"], 1)


def head_gate(nc, K, w, XT, stats, logits):
    NS = H4 * 16
    with Stage(nc) as s:
        w1, w1s = s.sb("w1_x", [D, D]), s.sb("w1_stats", [NS, H4, D])
        b1, w2 = s.sb("b1", [D, 1]), s.sb("w2", [D, H4])
        with s.block() as block:
            @block.vector
            def _(dve):
                dve.memset(w1s[:], 0.0)
        load(nc, s, [(w1[:], w["L2_attn_W1"][0:D]), (b1[:], column(w["L2_attn_b1"])), (w2[:], w["L2_attn_W2"])]
             + [(w1s[16 * h:16 * h + 16, h], w["L2_attn_W1"][D:D + 16]) for h in range(H4)])
        sT = s.sb("stats_turned", [NS, B, T])
        h1 = s.sb("hidden", [D, 2, H4, T])
        pt = s.ps("p_stats", [P, GROUP, T])
        ph = s.ps("p_hidden", [P, 2, H4, T])
        pl = s.ps("p_logits", [P, 2, 512])
        S = {n: s.sem("gate_" + n) for n in "turned copied hidden_ready active logits_ready stored".split()}
        with s.block() as block:
            @block.tensor
            def _(pe):
                for g in range(GROUPS):
                    wait(pe, S["copied"], g)
                    for j in range(GROUP):
                        last = pe.transpose(pt[0:NS, j], stats[:, GROUP * g + j].rearrange("t h k -> t (h k)"), K["ident"])
                    last.then_inc(S["turned"], 1)
                pe.wait_ge(S["copied"], GROUPS)
                xt, st = pairs(XT), pairs(sT[:])

                def hidden(n, j, i):
                    wait(pe, S["active"], n - 1)
                    for h in range(H4):
                        pe.matmul(ph[:, j, h], w1[:], xt[:, i, j], start=True, stop=False)
                        last = pe.matmul(ph[:, j, h], w1s[:, h], st[:, i, j], start=False, stop=True)
                    last.then_inc(S["hidden_ready"], 1)

                def logit(n, j):
                    wait(pe, S["active"], n + 1)
                    wait(pe, S["stored"], n - 1)
                    for h in range(H4):
                        last = pe.matmul(pl[:, j, 4 * h:4 * h + 4], h1[:, j, h], w2[:], start=True, stop=True)
                    last.then_inc(S["logits_ready"], 1)

                def turn(n, j, i):
                    hidden(n, j, i)
                    if not (isinstance(n, int) and n == 0):
                        logit(n - 1, 1 - j)
                first_then_loop(pe, B, turn)
                logit(B - 1, 1)

            @block.scalar
            def _(act):
                for g in range(GROUPS):
                    act.wait_ge(S["turned"], g + 1)
                    act.copy(sT[:, GROUP * g:GROUP * g + GROUP], pt[0:NS]).then_inc(S["copied"], 1)

                def turn(n, j, i):
                    wait(act, S["hidden_ready"], n + 1)
                    wait(act, S["logits_ready"], n - 1)
                    act.activation(h1[:, j], ph[:, j], ACT.Gelu, bias=b1[:]).then_inc(S["active"], 1)
                first_then_loop(act, B, turn)

            @block.vector
            def _(dve):
                lg = logits.rearrange("t (i j) h k -> t i j (h k)", j=2)

                def turn(n, j, i):
                    wait(dve, S["logits_ready"], n + 1)
                    dve.tensor_copy(lg[:, i, j], pl[:, j, 0:16]).then_inc(S["stored"], 1)
                first_then_loop(dve, B, turn)


def head_mix(nc, K, w, sources, logits, X):
    with Stage(nc) as s:
        wo, rw = s.sb("w_o", [D, D]), s.sb("rms_w", [D, 1])
        rows = s.sb("head_rows", [1, 16 + 4 + 4 + 4])
        full = s.sb("head_row_full", [1, 3, H4, 4])
        tmp = s.sb("head_row_tmp", [1, 8])
        hb = s.sb("head_rows_spread", [P, 3, H4, 4])
        load(nc, s, [(wo[:], w["L2_attn_Wo"]), (rows[:, 0:16], row(w["L2_attn_base_bias"].rearrange("h k -> (h k)"))),
                     (rows[:, 16:20], row(w["L2_attn_b2"])), (rows[:, 20:24], row(w["L2_attn_log_temp"])),
                     (rows[:, 24:28], row(w["L2_attn_conv_residual_logit"]))]
             + [(rw[DH * h:DH * h + DH, :], column(w["L2_attn_rms_w"])) for h in range(H4)])
        pr = s.sb("p", [P, B, H4, 4])
        m = s.sb("row", [P, B, H4])
        o, part = s.sb("mix", [P, B, D]), s.sb("mix_part", [P, 2, B, D])
        oT = s.sb("mix_turned", [D, B, T])
        p_small = s.ps("p_small", [P, 48])
        pt = s.ps("p_turned", [P, 2, GROUP, T])
        po = s.ps("p_out", [P, 2, GROUP, D])
        names = ("rows_ready temp_abs temp_soft full_ready spread spread_copied shifted exp_ready p_ready part_ready part_used "
                 "mixed squared summed rooted normed turned turned_copied out_ready chain")
        S = {n: s.sem("mix_" + n) for n in names.split()}
        flat = "p b h k -> p (b h) k"
        m_flat = m[:].rearrange("p b h -> p (b h)")
        f3 = "p (b h) -> p b h"
        with s.block() as block:
            @block.scalar
            def _(act):
                c = Chain(act, S["temp_abs"])
                c.link(act.activation(tmp[:, 0:4], rows[:, 20:24], ACT.Abs))
                c.link(act.activation(tmp[:, 0:4], tmp[:, 0:4], ACT.Exp, scale=-1.0))
                act.activation(tmp[:, 0:4], tmp[:, 0:4], ACT.Ln, bias=1.0)
                act.activation(tmp[:, 4:8], rows[:, 24:28], ACT.Sigmoid).then_inc(S["temp_soft"], 1)
                act.wait_ge(S["spread"], 1)
                act.copy(hb[:], p_small[:].rearrange("p (a h k) -> p a h k", a=3, h=H4)).then_inc(S["spread_copied"], 1)
                act.wait_ge(S["shifted"], 1)
                act.activation(pr[:], pr[:], ACT.Exp).then_inc(S["exp_ready"], 1)
                act.wait_ge(S["mixed"], 1)
                act.activation(part[:, 0], o[:], ACT.Square).then_inc(S["squared"], 1)
                act.wait_ge(S["summed"], 1)
                act.activation(m[:], m[:], ACT.Sqrt).then_inc(S["rooted"], 1)
                for g in range(GROUPS):
                    act.wait_ge(S["turned"], g + 1)
                    act.activation(oT[:, GROUP * g:GROUP * g + GROUP], pt[:, g % 2], ACT.Identity,
                                   scale=rw[:]).then_inc(S["turned_copied"], 1)

            @block.tensor
            def _(pe):
                pe.wait_ge(S["full_ready"], 1)
                pe.matmul(p_small[:], K["ones"][0:1, :], full[:].rearrange("p a h k -> p (a h k)"),
                          start=True, stop=True).then_inc(S["spread"], 1)
                pe.wait_ge(S["normed"], 1)
                for g in range(GROUPS):
                    wait(pe, S["turned_copied"], g - 1)
                    for j in range(GROUP):
                        last = pe.transpose(pt[:, g % 2, j], o[:, GROUP * g + j], K["ident"])
                    last.then_inc(S["turned"], 1)
                for g in range(GROUPS):
                    pe.wait_ge(S["turned_copied"], g + 1)
                    wait(pe, S["out_ready"], 0)
                    wait(pe, S["part_used"], 4 + (g - 1) if g >= 2 else 0)
                    for j in range(GROUP):
                        last = pe.matmul(po[:, g % 2, j], oT[:, GROUP * g + j], wo[:], start=True, stop=True)
                    last.then_inc(S["out_ready"], 1)

            @block.gpsimd
            def _(pool):
                pool.wait_ge(S["part_ready"], 1)
                for k in range(1, 4):
                    pool.wait_ge(S["part_ready"], k + 1)
                    wait(pool, S["part_used"], k - 1)
                    pool.tensor_tensor(o[:], o[:], part[:, k % 2], ALU.add).then_inc(S["part_used"], 1)

            @block.vector
            def _(dve):
                c = Chain(dve, S["chain"])
                dve.wait_ge(S["temp_soft"], 1)
                base = rows[:, 0:16].rearrange("p (h k) -> p h k", k=4)
                dve.tensor_tensor(full[:, 0], base, bcast(rows[:, 16:20], 1, H4), ALU.add)
                c.link(dve.scalar_tensor_tensor(tmp[:, 0:4], rows[:, 20:24], 0.0, tmp[:, 0:4], ALU.max, ALU.add))
                c.link(dve.tensor_scalar(tmp[:, 0:4], tmp[:, 0:4], 1e-4, None, ALU.add))
                c.link(dve.reciprocal(tmp[:, 0:4], tmp[:, 0:4]))
                dve.tensor_copy(full[:, 1], bcast(tmp[:, 0:4], 2, 4))
                dve.tensor_scalar(full[:, 2], bcast(tmp[:, 4:8], 2, 4), 0.5, None, ALU.mult).then_inc(S["full_ready"], 1)
                dve.wait_ge(S["spread_copied"], 1)
                c.link(dve.tensor_tensor(pr[:], logits, bcast(hb[:, 0], 1, B), ALU.add))
                c.link(dve.tensor_tensor(pr[:], pr[:], bcast(hb[:, 1], 1, B), ALU.mult))
                c.link(dve.tensor_reduce(m_flat, pr[:].rearrange(flat), AX.X, ALU.max))
                dve.tensor_tensor(pr[:].rearrange(flat), pr[:].rearrange(flat), bcast(m_flat, 2, 4),
                                  ALU.subtract).then_inc(S["shifted"], 1)
                dve.wait_ge(S["exp_ready"], 1)

                def to_one():
                    c.link(dve.tensor_reduce(m_flat, pr[:].rearrange(flat), AX.X, ALU.add))
                    c.link(dve.reciprocal(m_flat, m_flat))
                    c.link(dve.tensor_tensor(pr[:].rearrange(flat), pr[:].rearrange(flat), bcast(m_flat, 2, 4), ALU.mult))
                to_one()
                dve.tensor_scalar(pr[:, :, :, 0:2], pr[:, :, :, 0:2], 0.05, None, ALU.max)
                c.link(dve.tensor_scalar(pr[:, :, :, 2:4], pr[:, :, :, 2:4], 0.0, None, ALU.max))
                to_one()
                c.link(dve.tensor_tensor(pr[:, :, :, 0], pr[:, :, :, 0], bcast(hb[:, 2, :, 0], 1, B), ALU.add))
                for k, src in enumerate(sources):
                    wait(dve, S["part_used"], k - 2)
                    dst = o[:] if k == 0 else part[:, k % 2]
                    dve.tensor_tensor(by_head(dst), by_head(src), bcast(pr[:].rearrange(flat)[:, :, k], 2, DH),
                                      ALU.mult).then_inc(S["part_ready"], 1)
                dve.wait_ge(S["part_used"], 3)
                dve.engine_nop().then_inc(S["mixed"], 1)
                dve.wait_ge(S["squared"], 1)
                c.link(dve.tensor_reduce(m_flat, by_head(part[:, 0]), AX.X, ALU.add))
                dve.tensor_scalar(m[:], m[:], 1.0 / DH, 1e-5, ALU.mult, ALU.add).then_inc(S["summed"], 1)
                dve.wait_ge(S["rooted"], 1)
                c.link(dve.reciprocal(m[:], m[:]))
                dve.tensor_tensor(by_head(o[:]), by_head(o[:]), bcast(m_flat, 2, DH), ALU.mult).then_inc(S["normed"], 1)
                for g in range(GROUPS):
                    dve.wait_ge(S["out_ready"], g + 1)
                    grp = slice(GROUP * g, GROUP * g + GROUP)
                    dve.tensor_tensor(X[:, grp], X[:, grp], po[:, g % 2], ALU.add).then_inc(S["part_used"], 1)


def l2_attn(nc, K, w, X, XN, XT):
    layernorm(nc, K, X, XN, XT)
    with Stage(nc) as s:
        v, fs, fl = (s.sb(n, [P, B, D]) for n in ("v", "f_short", "f_long"))
        delta = s.sb("delta_out", [P, B, D])
        with Stage(nc) as s2:
            q, k = s2.sb("q", [P, B, D]), s2.sb("k", [P, B, D])
            beta, rq, rk = (s2.sb(n, [P, B, H4]) for n in ("beta", "q_scale", "k_scale"))
            taps(nc, K, w, XT, q[:], k[:], v[:], fs[:], fl[:])
            vb = s2.sb("v_beta", [P, B, D])
            delta_scales(nc, K, w, XT, q[:], k[:], v[:], vb[:], beta[:], rq[:], rk[:])
            delta_rule(nc, K, q[:], k[:], vb[:], beta[:], rq[:], rk[:], delta[:])
        stats, logits = s.sb("stats", [P, B, H4, 16]), s.sb("logits", [P, B, H4, 4])
        sources = [fs[:], fl[:], delta[:], v[:]]
        head_stats(nc, K, sources, stats[:])
        head_gate(nc, K, w, XT, stats[:], logits[:])
        head_mix(nc, K, w, sources, logits[:], X)



BIAS_COLUMNS = ["L1_ffn_b1", "L3_ffn_rb1", "L3_ffn_rb2", "L3_ffn_sb1", "L3_ffn_sb2", "L3_attn_b1"]
TRANSPOSED = ["L1_xattn_W_l", "L1_ffn_Wg", "L1_ffn_Wo", "L3_attn_Wd", "L3_attn_Wbc", "L3_attn_W1", "L3_attn_W2"]


def host_layout(inputs):
    arrays = {}
    for name, a in inputs.items():
        a = np.asarray(a)
        if a.ndim == 0:
            a = a.reshape(1)
        if name in TRANSPOSED:
            a = a.T
        if name == "L1_ffn_W1":
            a = a.transpose(0, 2, 1)
        if name in BIAS_COLUMNS:
            a = np.moveaxis(a.reshape(*a.shape[:-1], -1, P), -1, -2)
        arrays[name] = np.ascontiguousarray(a)
    return arrays



def kernel(**inputs):
    import concourse.bacc as bacc
    from concourse.bass_utils import run_bass_kernel_spmd

    arrays = host_layout(inputs)
    arrays["constants"] = constant_blob()
    nc = bacc.Bacc("TRN2", target_bir_lowering=False, num_devices=1)
    w = {name: nc.dram_tensor(f"in_{name}", a.shape, mybir.dt.from_np(a.dtype), kind="ExternalInput").ap()
         for name, a in arrays.items()}
    out = nc.dram_tensor("out_x", (B, T, D), F32, kind="ExternalOutput").ap()
    program(nc, w, out)
    r = run_bass_kernel_spmd(nc, [{f"in_{name}": a for name, a in arrays.items()}], core_ids=[0])
    return r.results[0]["out_x"]
```

```python
from contextlib import ExitStack
from itertools import islice

import numpy as np

import concourse.bass as bass
from concourse import mybir

ALU = mybir.AluOpType
ACT = mybir.ActivationFunctionType
F32 = mybir.dt.float32
BF16 = mybir.dt.bfloat16
F32R = mybir.dt.float32r
I32 = mybir.dt.int32
AX = mybir.AxisListType

P = 128
B = 16
T = 128
D = 128
CTX = 77
HEADS = 16
EXPERTS = 8
GROUP = 4
GROUPS = B // GROUP
NEG = -1e30
LN_EPS = 1e-5
LEVELS = 7
ALL_RANKS = 8 * -(-CTX // 8)
FEW_RANKS = ALL_RANKS // 16 * 8



def rope_tables(heads, head_dim):
    inv = (1.0 / 10000.0 ** (np.arange(0, head_dim, 2, dtype=np.float32) / np.float32(head_dim))).astype(np.float32)
    angle = (np.arange(T, dtype=np.float32)[None, :] * inv[:, None]).astype(np.float32)
    angle = np.tile(np.repeat(angle, 2, axis=0), (heads, 1))
    c = heads * head_dim
    swap = np.zeros((c, c), np.float32)
    for k in range(0, c, 2):
        swap[k + 1, k] = -1.0
        swap[k, k + 1] = 1.0
    return np.cos(angle).astype(np.float32), np.sin(angle).astype(np.float32), swap


def constants():
    out = {"ident": np.eye(P, dtype=np.float32)}
    t = np.arange(P)
    out["ident_thrice"] = np.tile(np.eye(32, dtype=np.float32), (3, 1))
    out["causal"] = np.where(t[None, :] <= t[:, None], 0.0, NEG).astype(np.float32)
    out["ones"] = np.ones((P, P), np.float32)
    for ranks in (FEW_RANKS, ALL_RANKS):
        rank = np.arange(ranks, dtype=np.float32) + 1
        out[f"scan_keep{ranks}"] = np.tile((rank > 1).astype(np.float32), (P, HEADS // 2))
        out[f"inv_rank{ranks}"] = np.tile(np.float32(1) / rank, (P, HEADS // 2))
    out["before"] = (t[:, None] < t[None, :]).astype(np.float32)
    out["upto"] = (t[:, None] <= t[None, :]).astype(np.float32)
    out["headmask32"] = (t[:, None] // 32 == np.arange(4)[None, :]).astype(np.float32)
    for level in range(LEVELS - 1):
        m = 1 << level
        pair = ((t[None, :] // m) % 2 == 1) & (t[:, None] // m == t[None, :] // m - 1)
        if level == 0:
            out["level0"] = pair.astype(np.float32)
        out[f"level{level}_lower"] = pair.T.astype(np.float32)
    out["half"] = np.stack([t < P // 2, t >= P // 2], 1).astype(np.float32)
    out["expert_order"] = np.tile(EXPERTS - np.arange(EXPERTS, dtype=np.float32), (P, 1))
    for hd in (8, 4):
        c = HEADS * hd
        copies = (P // c, 1)
        out[f"headmask{hd}"] = np.tile((np.arange(c)[:, None] // hd == np.arange(HEADS)[None, :]).astype(np.float32), copies)
        cos, sin, swap = rope_tables(HEADS, hd)
        out[f"cos{hd}"] = np.tile(np.concatenate([cos, cos], 1), copies)
        out[f"sin{hd}"] = np.tile(np.concatenate([sin, sin], 1), copies)
        out[f"swap{hd}"] = swap
    return out


CONST = constants()
CONST_AT = {}
for _name, _a in CONST.items():
    CONST_AT[_name] = (sum(w for _, _, w in CONST_AT.values()), _a.shape[0], _a.shape[1])
CONST_W = sum(w for _, _, w in CONST_AT.values())


def constant_blob():
    blob = np.zeros((P, CONST_W), np.float32)
    for name, (at, rows, width) in CONST_AT.items():
        blob[:rows, at:at + width] = CONST[name]
    return blob



def wait(eng, sem, value, alone=None):
    if isinstance(value, int):
        if value > 0:
            eng.wait_ge(sem, value)
        return
    eng.wait_ge(sem, value)
    if alone is not None:
        eng.sem_inc(alone, 1)


class Chain:

    def __init__(self, eng, sem, per=0, alone=None):
        self.eng, self.sem, self.per, self.n, self.k, self.alone = eng, sem, per, 0, 0, alone

    def turn(self, n):
        assert self.k in (0, self.per), f"a turn has {self.k} steps, not {self.per}"
        self.n, self.k = n, 0

    def link(self, ins, lag=0):
        self.count(ins)
        self.until(lag)

    def count(self, ins):
        self.k += 1
        ins.then_inc(self.sem, 1)

    def until(self, lag):
        wait(self.eng, self.sem, self.n * self.per + self.k - lag, self.alone)


class Stage:

    def __init__(self, nc):
        self.nc, self.ctx, self.sems = nc, ExitStack(), []
        self.tag = f"_{nc.next_id()}"

    def __enter__(self):
        return self

    def sb(self, name, shape, dt=F32):
        return self.ctx.enter_context(self.nc.sbuf_tensor(name + self.tag, shape, dt))

    def ps(self, name, shape, dt=F32):
        return self.ctx.enter_context(self.nc.psum_tensor(name + self.tag, shape, dt))

    def sem(self, name):
        self.sems.append(self.nc.alloc_semaphore(name=name + self.tag))
        return self.sems[-1]

    def block(self):
        return self.nc.Block()

    def __exit__(self, *exc):
        if exc[0] is None:
            self.nc.clear_and_free_semaphores(self.sems)
            self.nc.all_engine_barrier()
        self.ctx.close()


HIGH_BITS = -4096


def high_part(dve, dst, src):
    return dve.tensor_scalar(dst.bitcast(I32), src.bitcast(I32), HIGH_BITS, None, ALU.bitwise_and)


def split_matmul(pe, out, lhsT, rhs, start=True, stop=True):
    (lh, ll), (rh, rl) = lhsT, rhs
    pe.matmul(out, lh, rh, start=start, stop=False)
    pe.matmul(out, lh, rl, start=False, stop=False)
    return pe.matmul(out, ll, rh, start=False, stop=stop)


def pairs(t):
    return t.rearrange("p (i j) n -> p i j n", j=2)


def over_pairs(eng, turn, count=B):
    for j in range(2):
        turn(j, j, 0)
    if count > 4:
        with eng.Fori(1, count // 2 - 1) as i:
            for j in range(2):
                turn(i * 2 + j, j, i)
    if count > 2:
        for j in range(2):
            turn(count - 2 + j, j, count // 2 - 1)


def bcast(ap, axis, n):
    ap = ap.unsqueeze(axis)
    shape = list(ap.shape)
    shape[axis] = n
    return ap.broadcast_to(shape)



def layernorm(nc, K, x, xn, xT, scale=None, bias=None, eps=LN_EPS, rms=False, loads=()):
    HALVES = (slice(0, B // 2), slice(B // 2, B))
    with Stage(nc) as s:
        sq = s.sb("ln_square", [P, B, D])
        mean, var = s.sb("ln_mean", [P, B]), s.sb("ln_var", [P, B])
        pt = s.ps("ln_transposed", [P, 4, GROUP, T])
        chain = s.sem("ln_chain")
        centred, squared, summed, std_ready = (s.sem(n) for n in ("ln_centred", "ln_squared", "ln_summed", "ln_std"))
        normed, transposed, loaded = s.sem("ln_normed"), s.sem("ln_transposed_s"), s.sem("ln_weights_loaded")
        src = x if rms else xn
        with s.block() as block:
            @block.sync
            def _(sp):
                for tile, source in loads:
                    sp.dma_start(tile, source).then_inc(loaded, 16)
                wait(sp, loaded, 16 * len(loads))

            @block.vector
            def _(dve):
                c = Chain(dve, chain)
                if not rms:
                    for h in HALVES:
                        c.count(dve.tensor_reduce(mean[:, h], x[:, h], AX.X, ALU.add))
                    for k, h in enumerate(HALVES):
                        c.until(1)
                        c.count(dve.tensor_scalar(mean[:, h], mean[:, h], 1.0 / D, None, ALU.mult))
                    for k, h in enumerate(HALVES):
                        c.until(1 - k)
                        dve.tensor_tensor(xn[:, h], x[:, h], bcast(mean[:, h], 2, D), ALU.subtract).then_inc(centred, 1)
                for k, h in enumerate(HALVES):
                    dve.wait_ge(squared, k + 1)
                    c.link(dve.tensor_reduce(var[:, h], sq[:, h], AX.X, ALU.add))
                    dve.tensor_scalar(var[:, h], var[:, h], 1.0 / D, eps, ALU.mult, ALU.add).then_inc(summed, 1)
                wait(dve, centred, 0 if rms else 2)
                for k, h in enumerate(HALVES):
                    dve.wait_ge(std_ready, k + 1)
                    c.link(dve.reciprocal(mean[:, h], var[:, h]))
                    for g in (2 * k, 2 * k + 1):
                        part = slice(GROUP * g, GROUP * g + GROUP)
                        dve.tensor_tensor(xn[:, part], src[:, part], bcast(mean[:, part], 2, D), ALU.mult).then_inc(normed, 1)

            @block.scalar
            def _(act):
                for k, h in enumerate(HALVES):
                    wait(act, centred, 0 if rms else k + 1)
                    act.activation(sq[:, h], src[:, h], ACT.Square).then_inc(squared, 1)
                for k, h in enumerate(HALVES):
                    act.wait_ge(summed, k + 1)
                    act.activation(var[:, h], var[:, h], ACT.Sqrt).then_inc(std_ready, 1)
                for g in range(GROUPS):
                    act.wait_ge(transposed, g + 1)
                    act.activation(xT[:, GROUP * g:GROUP * g + GROUP], pt[:, g], ACT.Identity,
                                   bias=bias if bias is not None else 0.0, scale=scale if scale is not None else 1.0)

            @block.tensor
            def _(pe):
                for g in range(GROUPS):
                    pe.wait_ge(normed, g + 1)
                    for j in range(GROUP):
                        last = pe.transpose(pt[:, g, j], xn[:, GROUP * g + j], K["ident"])
                    last.then_inc(transposed, 1)



def attention(nc, K, name, C, hd, q_src, kv_src, keys, wq, wk, wv, wo, res_in, res_out, bo=None, bqkv=None,
              rope=False, causal=False, ranks=None, tails=None):
    sparse = ranks is not None
    stacked = rope and 2 * C == P
    CS = 2 * C if stacked else C
    HALF = HEADS // 2
    QUADS = HEADS // GROUP
    TURNED = 2
    SCORE_BANK = (0, 1, 2, 0)
    same = kv_src is q_src
    din = q_src.shape[0]
    dout = wo.shape[1]
    sc = float(hd) ** -0.5
    with Stage(nc) as s:
        xs = s.sb("x_staged", [din, 2, T])
        cs = xs if same else s.sb("ctx_staged", [kv_src.shape[0], 2, keys])
        qT = s.sb("qT", [CS, 2, T])
        kT = s.sb("kT", [CS, 2, keys])
        rot = s.sb("rotated", [CS, 2 * T]) if rope else None
        wr = s.sb("w_rotated", [din, 2, CS]) if rope else None
        wT = s.sb("w_transposed", [C, 2, din]) if rope else None
        kspread = s.sb("k_spread", [CS, 2, HEADS, keys], F32R if stacked else F32)
        if stacked:
            w_own = (wq, wk)
            w_twice = s.sb("w_twice", [din, 2, CS])
            wq, wk = w_twice[:, 0], w_twice[:, 1]
            q_cut, k_cut, k_low = (s.sb(n, [CS, T]) for n in ("q_cut_off", "k_cut_off", "k_low"))
            q_parts = s.sb("q_high_over_low", [CS, 2, T], F32R)
            lowspread = s.sb("k_low_spread", [CS, 2, HEADS, keys], F32R)
        else:
            w_own = (wq, wk)
        vh = s.sb("v_held", [keys, 2, C])
        va = s.sb("v_and_ones", [keys, 2, HEADS, hd + 1])
        top = s.sb("row_max", [P, 2, QUADS, GROUP])
        pr = s.sb("probs", [P, 2, 2, HALF, keys])
        prT = s.sb("probs_transposed", [keys, QUADS, GROUP, T])
        inv = s.sb("inverse_sum", [P, 2, HEADS])
        o = s.sb("mixed_o", [P, 2, C])
        oT = s.sb("oT", [C, 2, T])
        if sparse:
            work = s.sb("unsorted_rest", [P, 2, HALF, keys])
            ranked = s.sb("sorted", [P, 2, HALF, ranks])
            lowered = s.sb("sorted_less_max", [P, 2, HALF, ranks])
            sums = s.sb("sorted_sums", [P, 2, HALF, ranks])
            tau = s.sb("threshold", [P, 2, HALF])
        p_qk = s.ps("p_qk", [P, 4, T])
        p_misc = s.ps("p_misc", [P, 512])
        p_v = s.ps("p_v", [keys, C])[:]
        p_s = s.ps("p_scores", [P, 3, GROUP, T])
        p_t = s.ps("p_probsT", [P, TURNED, GROUP, T])
        p_o = p_misc[:, 128:128 + HEADS * (hd + 1)]
        p_oT = p_misc[0:C, 272:400]
        p_y = p_misc[:, 272:272 + dout]
        names = ("staged projected qkv_ready scores_ready shifted probs_ready probsT_ready probsT_copied mixed "
                 "normed oT_ready oT_copied out_ready added ones_ready w_turned w_turned_copied w_rotated "
                 "w_rotated_copied w_doubled k_ready k_spread k_low_ready k_low_spread v_ready tau_ready shifted_probs passed chain_sparse chain_in chain_top chain_inv")
        S = {n: s.sem(f"{name}_{n}") for n in names.split()}
        q4, kv4 = pairs(q_src), pairs(kv_src)
        rin, rout = pairs(res_in), pairs(res_out)

        with s.block() as block:
            @block.gpsimd
            def _(pool):
                pool.memset(va[:], 1.0).then_inc(S["ones_ready"], 1)

                def stage(n, j, i):
                    wait(pool, S["projected"], n - 1, alone=S["passed"])
                    last = pool.tensor_copy(xs[:, j], q4[:, i, j])
                    if not same:
                        last = pool.tensor_copy(cs[:, j], kv4[:, i, j])
                    last.then_inc(S["staged"], 1)

                def spread_v(n, j):
                    wait(pool, S["qkv_ready"], n + 1, alone=S["passed"])
                    wait(pool, S["mixed"], n - 1, alone=S["passed"])
                    pool.tensor_copy(va[:, j, :, 0:hd], vh[:, j].rearrange("k (h d) -> k h d", d=hd)).then_inc(S["v_ready"], 1)

                def threshold(n, j):
                    for hf in range(2):
                        wait(pool, S["tau_ready"], n * 2 + hf + 1)
                        largest = top[:, j].rearrange("p q h -> p (q h)")[:, HALF * hf:HALF * hf + HALF]
                        pool.tensor_tensor(pr[:, j, hf], pr[:, j, hf], bcast(largest, 2, keys),
                                           ALU.subtract).then_inc(S["shifted_probs"], 1)
                        wait(pool, S["shifted_probs"], n * 2 + hf + 1)
                        pool.tensor_tensor(pr[:, j, hf], pr[:, j, hf], bcast(tau[:, hf], 2, keys),
                                           ALU.subtract).then_inc(S["probs_ready"], 1)

                def spread_low(n, j):
                    wait(pool, S["k_low_ready"], n + 1, alone=S["passed"])
                    pool.tensor_tensor(lowspread[:, j, HALF:], bcast(k_low[:], 1, HALF),
                                       bcast(K[f"headmask{hd}"][:, HALF:], 2, keys), ALU.mult).then_inc(S["k_low_spread"], 1)

                def spread_k(n, j):
                    wait(pool, S["k_ready"], n + 1, alone=S["passed"])
                    pool.tensor_tensor(kspread[:, j], bcast(kT[:, j], 1, HEADS), bcast(K[f"headmask{hd}"], 2, keys),
                                       ALU.mult).then_inc(S["k_spread"], 1)

                def turn(n, j, i):
                    if isinstance(n, int) and n == 0:
                        pool.wait_ge(S["ones_ready"], 1)
                        stage(0, 0, 0)
                        if sparse:
                            stage(1, 1, 0)
                            spread_k(0, 0)
                    if sparse and not (isinstance(n, int) and n == B - 1):
                        spread_k(n + 1, 1 - j)
                    if stacked:
                        spread_low(n, j)
                    if sparse:
                        if not (isinstance(n, int) and n >= B - 2):
                            stage(n + 2, j, i + 1)
                    elif not (isinstance(n, int) and n == B - 1):
                        stage(n + 1, 1 - j, i if j == 0 else i + 1)
                    spread_v(n, j)
                    if sparse:
                        threshold(n, j)
                over_pairs(pool, turn)

            @block.tensor
            def _(pe):
                if rope:
                    for m, w in enumerate(w_own):
                        last = pe.transpose(p_t[0:C, 0, m, 0:din], w, K["ident"][0:din, 0:din])
                    last.then_inc(S["w_turned"], 1)
                    pe.wait_ge(S["w_turned_copied"], 1)
                    for m in range(2):
                        last = pe.matmul(p_misc[0:din, m * C:(m + 1) * C], wT[:, m], K[f"swap{hd}"], start=True, stop=True)
                    last.then_inc(S["w_rotated"], 1)
                    pe.wait_ge(S["w_rotated_copied"], 1)
                if stacked:
                    pe.wait_ge(S["w_doubled"], 2)

                def project(n, j):
                    wait(pe, S["staged"], n + 1, alone=S["passed"] if C < P else None)
                    wait(pe, S["qkv_ready"], n, alone=S["passed"] if C < P else None)
                    pe.matmul(p_qk[0:CS, 0, 0:T], wq, xs[:, j], start=True, stop=True)
                    pe.matmul(p_qk[0:CS, 1, 0:keys], wk, cs[:, j], start=True, stop=True)
                    if rope:
                        pe.matmul(p_qk[0:CS, 2, 0:T], wr[:, 0], xs[:, j], start=True, stop=True)
                        pe.matmul(p_qk[0:CS, 3, 0:T], wr[:, 1], xs[:, j], start=True, stop=True)
                    last = pe.matmul(p_v, cs[:, j], wv, start=True, stop=bqkv is None)
                    if bqkv is not None:
                        last = pe.matmul(p_v, K["ones"][0:1, 0:keys], bqkv[2], start=False, stop=True)
                    last.then_inc(S["projected"], 1)

                def scores(n, j):
                    wait(pe, S["qkv_ready"], n + 1)
                    if sparse:
                        wait(pe, S["k_spread"], n + 1)
                    for q in range(QUADS):
                        if q == 0:
                            wait(pe, S["shifted"], n * QUADS)
                        if q == QUADS - 1:
                            wait(pe, S["shifted"], n * QUADS + 1)
                        bank = p_s[:, SCORE_BANK[q], :, 0:keys]
                        quad = slice(q * GROUP, (q + 1) * GROUP)
                        if stacked and q == QUADS // 2:
                            wait(pe, S["k_low_spread"], n + 1)
                        last = pe.matmul(bank, (q_parts if stacked else qT)[:, j], kspread[:, j, quad], start=True,
                                         stop=not (causal or stacked))
                        if stacked:
                            last = pe.matmul(bank, q_parts[:, j], lowspread[:, j, quad], start=False, stop=not causal)
                        if causal:
                            last = pe.matmul(bank, K["ident_bf16"], bcast(K["causal_bf16"], 1, GROUP), start=False, stop=True)
                        last.then_inc(S["scores_ready"], 1)

                def mix(n, j):
                    def turn_quad(q):
                        if q % 2 == 0:
                            wait(pe, S["probs_ready"], n * 2 + q // 2 + 1)
                        wait(pe, S["probsT_copied"], n * QUADS + q - TURNED + 1)
                        for h in range(GROUP):
                            last = pe.transpose(p_t[0:keys, q % TURNED, h], pr[:, j, q // 2, (q % 2) * GROUP + h], K["ident"])
                        last.then_inc(S["probsT_ready"], 1)

                    turn_quad(0)
                    for q in range(QUADS):
                        if q < QUADS - 1:
                            turn_quad(q + 1)
                        if q == 0:
                            wait(pe, S["added"], n)
                            wait(pe, S["v_ready"], n + 1)
                        wait(pe, S["probsT_copied"], n * QUADS + q + 1)
                        for h in range(GROUP):
                            hh = q * GROUP + h
                            last = pe.matmul(p_o[:, hh * (hd + 1):(hh + 1) * (hd + 1)], prT[:, q, h], va[:, j, hh],
                                             start=True, stop=True)
                    last.then_inc(S["mixed"], 1)

                def output(n, j):
                    wait(pe, S["normed"], n + 1, alone=S["passed"] if C < P else None)
                    pe.transpose(p_oT, o[:, j], K["ident"]).then_inc(S["oT_ready"], 1)
                    wait(pe, S["oT_copied"], n + 1)
                    last = pe.matmul(p_y, oT[:, j], wo, start=True, stop=bo is None)
                    if bo is not None:
                        last = pe.matmul(p_y, K["ones"][0:1, :], bo, start=False, stop=True)
                    last.then_inc(S["out_ready"], 1)

                def turn(n, j, i):
                    if isinstance(n, int) and n == 0:
                        project(0, 0)
                    scores(n, j)
                    if sparse and not (isinstance(n, int) and n == B - 1):
                        project(n + 1, 1 - j)
                    if not (isinstance(n, int) and n < 2):
                        output(n - 2, j)
                    if not sparse and not (isinstance(n, int) and n == B - 1):
                        project(n + 1, 1 - j)
                    if not (isinstance(n, int) and n == 0):
                        mix(n - 1, 1 - j)
                over_pairs(pe, turn)
                output(B - 2, 0)
                mix(B - 1, 1)
                output(B - 1, 1)

            @block.vector
            def _(dve):
                if rope:
                    dve.wait_ge(S["w_turned"], 1)
                    dve.tensor_copy(wT[:], p_t[0:C, 0, 0:2, 0:din]).then_inc(S["w_turned_copied"], 1)
                    dve.wait_ge(S["w_rotated"], 1)
                    rotated = p_misc[0:din, 0:2 * C].rearrange("d (m c) -> d m c", m=2)
                    copies = CS // C
                    dve.tensor_copy(wr[:].rearrange("d m (a c) -> d m a c", a=copies), bcast(rotated, 2, copies)).then_inc(
                        S["w_rotated_copied"], 1)
                if stacked:
                    for m in range(2):
                        dve.tensor_copy(w_twice[:, m].rearrange("d (a c) -> d a c", a=2), bcast(w_own[m], 1, 2)).then_inc(
                            S["w_doubled"], 1)
                c_in = Chain(dve, S["chain_in"], 4 if stacked else 3 if rope else 1 if bqkv is not None and not sparse else 0)
                c_top = Chain(dve, S["chain_top"], QUADS)
                c_inv = Chain(dve, S["chain_inv"], 1)

                def evacuate(n, j):
                    c_in.turn(n)
                    wait(dve, S["projected"], n + 1)
                    if rope:
                        cos = K[f"cos{hd}"].rearrange("c (a t) -> c a t", a=2)
                        sin = K[f"sin{hd}"].rearrange("c (a t) -> c a t", a=2)
                        r3 = rot[:].rearrange("c (a t) -> c a t", a=2)
                        c_in.link(dve.tensor_tensor(r3, p_qk[0:CS, 2:4], sin, ALU.mult))
                        dve.tensor_tensor(qT[:, j], p_qk[0:CS, 0], cos[:, 0], ALU.mult)
                        c_in.link(dve.tensor_tensor(kT[:, j], p_qk[0:CS, 1], cos[:, 0], ALU.mult))
                        dve.tensor_tensor(qT[:, j], qT[:, j], rot[:, 0:T], ALU.add)
                        c_in.link(dve.tensor_tensor(kT[:, j], kT[:, j], rot[:, T:2 * T], ALU.add))
                        ksrc = kT[:, j]
                        if stacked:
                            high_part(dve, q_cut[:], qT[:, j])
                            c_in.link(high_part(dve, k_cut[:], kT[:, j]))
                            dve.tensor_copy(q_parts[0:C, j], q_cut[0:C])
                            dve.tensor_tensor(q_parts[C:CS, j], qT[C:CS, j], q_cut[C:CS], ALU.subtract)
                            wait(dve, S["k_low_spread"], n)
                            dve.tensor_tensor(k_low[:], kT[:, j], k_cut[:], ALU.subtract).then_inc(S["k_low_ready"], 1)
                            wait(dve, S["k_low_ready"], n + 1)
                            dve.tensor_tensor(lowspread[:, j, 0:HALF], bcast(k_low[:], 1, HALF),
                                              bcast(K[f"headmask{hd}"][:, 0:HALF], 2, keys), ALU.mult)
                            ksrc = k_cut[:]
                    elif bqkv is not None:
                        dve.tensor_scalar(qT[:, j], p_qk[0:C, 0], bqkv[0], sc, ALU.add, ALU.mult)
                        if sparse:
                            wait(dve, S["k_spread"], n - 1)
                        k_out = dve.tensor_scalar(kT[:, j], p_qk[0:C, 1, 0:keys], bqkv[1], None, ALU.add)
                        if sparse:
                            k_out.then_inc(S["k_ready"], 1)
                        else:
                            c_in.link(k_out)
                        ksrc = kT[:, j]
                    else:
                        dve.tensor_copy(qT[:, j], p_qk[0:C, 0])
                        ksrc = p_qk[0:C, 1, 0:keys]
                    if not sparse:
                        dve.tensor_tensor(kspread[:, j], bcast(ksrc, 1, HEADS), bcast(K[f"headmask{hd}"], 2, keys), ALU.mult)
                    wait(dve, S["v_ready"], n - 1)
                    dve.tensor_copy(vh[:, j], p_v).then_inc(S["qkv_ready"], 1)

                def shift(n, j):
                    def bank(q):
                        return p_s[:, SCORE_BANK[q], :, 0:keys]

                    def find_top(q):
                        wait(dve, S["scores_ready"], n * QUADS + q + 1)
                        c_top.count(dve.tensor_reduce(top[:, j, q], bank(q), AX.X, ALU.max))
                    find_top(0)
                    for q in range(QUADS):
                        ahead = q < QUADS - 2
                        if ahead:
                            find_top(q + 1)
                        c_top.until(1 if ahead else 0)
                        if q % 2 == 0:
                            wait(dve, S["probsT_ready"], (n - 2) * QUADS + q + 2)
                        dve.tensor_tensor(pr[:, j, q // 2, (q % 2) * GROUP:(q % 2 + 1) * GROUP], bank(q),
                                          bcast(top[:, j, q], 2, keys), ALU.subtract).then_inc(S["shifted"], 1)
                        if q == QUADS - 2:
                            find_top(q + 1)

                c_sp = Chain(dve, S["chain_sparse"], 2 * (2 * (ranks // 8) + 2) if sparse else 0, alone=S["passed"])

                def find_thresholds(n, j, i):
                    for r in range(ranks // 8):
                        for hf in range(2):
                            if r == 0:
                                wait(dve, S["shifted"], n * QUADS + 2 * (hf + 1), alone=S["passed"])
                            for h in range(HALF):
                                last = dve.max(ranked[:, hf, h, 8 * r:8 * r + 8], (work[:, hf, h] if r else pr[:, j, hf, h]))
                            c_sp.link(last, lag=1)
                        if r == 0 and not (isinstance(n, int) and n < 2):
                            add(n - 2, j, i - 1)
                        if r < ranks // 8 - 1:
                            for hf in range(2):
                                for h in range(HALF):
                                    last = dve.match_replace(work[:, hf, h], ranked[:, hf, h, 8 * r:8 * r + 8],
                                                             (work[:, hf, h] if r else pr[:, j, hf, h]), NEG)
                                c_sp.link(last, lag=1)
                    flat = "p h k -> p (h k)"
                    dve.tensor_copy(top[:, j].rearrange("p q h -> p (q h)").rearrange("p (f h) -> p f h", f=2),
                                    ranked[:, :, :, 0])
                    for hf in range(2):
                        c_sp.link(dve.tensor_tensor(lowered[:, hf], ranked[:, hf], bcast(ranked[:, hf, :, 0], 2, ranks),
                                                    ALU.subtract), lag=1)
                    for hf in range(2):
                        c_sp.link(dve.tensor_tensor_scan(sums[:, hf].rearrange(flat), K[f"scan_keep{ranks}"],
                                                         lowered[:, hf].rearrange(flat), 0.0, ALU.mult, ALU.add), lag=1)
                    for hf in range(2):
                        c_sp.link(dve.scalar_tensor_tensor(sums[:, hf].rearrange(flat), sums[:, hf].rearrange(flat), -1.0,
                                                           K[f"inv_rank{ranks}"], ALU.add, ALU.mult), lag=1 - hf)
                    wait(dve, S["probs_ready"], n * 2)
                    for hf in range(2):
                        dve.tensor_reduce(tau[:, hf], sums[:, hf], AX.X, ALU.max).then_inc(S["tau_ready"], 1)
                    if tails is not None:
                        wait(dve, S["tau_ready"], n * 2 + 2)
                        dve.tensor_tensor(tails[:, i, j], lowered[:, :, :, ranks - 1], tau[:], ALU.subtract)

                def normalise(n, j):
                    c_inv.turn(n)
                    wait(dve, S["mixed"], n + 1)
                    o4 = p_o.rearrange("p (h d) -> p h d", d=hd + 1)
                    c_inv.link(dve.reciprocal(inv[:, j], o4[:, :, hd]))
                    dve.tensor_tensor(o[:, j].rearrange("p (h d) -> p h d", d=hd), o4[:, :, 0:hd],
                                      bcast(inv[:, j], 2, hd), ALU.mult).then_inc(S["normed"], 1)

                def add(n, j, i):
                    wait(dve, S["out_ready"], n + 1)
                    dve.tensor_tensor(rout[:, i, j], rin[:, i, j], p_y, ALU.add).then_inc(S["added"], 1)

                def turn(n, j, i):
                    if isinstance(n, int) and n == 0:
                        evacuate(0, 0)
                    c_top.turn(n)
                    c_sp.turn(n)
                    if not sparse:
                        shift(n, j)
                    if not sparse and not (isinstance(n, int) and n < 2):
                        add(n - 2, j, i - 1)
                    if not (isinstance(n, int) and n == B - 1):
                        evacuate(n + 1, 1 - j)
                    if sparse:
                        find_thresholds(n, j, i)
                    if not (isinstance(n, int) and n == 0):
                        normalise(n - 1, 1 - j)
                over_pairs(dve, turn)
                add(B - 2, 0, B // 2 - 1)
                normalise(B - 1, 1)
                add(B - 1, 1, B // 2 - 1)

            @block.scalar
            def _(act):
                def probs(n, j, hf):
                    wait(act, S["shifted"], n * QUADS + 2 * (hf + 1))
                    act.activation(pr[:, j, hf], pr[:, j, hf], ACT.Exp, scale=sc).then_inc(S["probs_ready"], 1)

                def copy_quads(n, hf):
                    for q in (2 * hf, 2 * hf + 1):
                        wait(act, S["probsT_ready"], n * QUADS + q + 1)
                        wait(act, S["mixed"], n)
                        act.activation(prT[:, q], p_t[0:keys, q % TURNED], ACT.Relu if sparse else ACT.Copy).then_inc(
                            S["probsT_copied"], 1)

                def copy_o(n, j):
                    wait(act, S["oT_ready"], n + 1)
                    act.copy(oT[:, j], p_oT).then_inc(S["oT_copied"], 1)

                def take_scores(n, j):
                    for q in range(QUADS):
                        wait(act, S["scores_ready"], n * QUADS + q + 1)
                        if q % 2 == 0:
                            wait(act, S["probsT_ready"], (n - 2) * QUADS + q + 2)
                        act.copy(pr[:, j, q // 2, (q % 2) * GROUP:(q % 2 + 1) * GROUP],
                                 p_s[:, SCORE_BANK[q], :, 0:keys]).then_inc(S["shifted"], 1)

                def turn(n, j, i):
                    if sparse:
                        take_scores(n, j)
                    if not (isinstance(n, int) and n < 2):
                        copy_o(n - 2, j)
                    for hf in range(2):
                        if not sparse:
                            probs(n, j, hf)
                        if not (isinstance(n, int) and n == 0):
                            copy_quads(n - 1, hf)
                over_pairs(act, turn)
                copy_o(B - 2, 0)
                for hf in range(2):
                    copy_quads(B - 1, hf)
                copy_o(B - 1, 1)



def load_constants(nc, K, K_tile, X, x_dram, consts, ctx, ctxT, ctx_dram):
    with Stage(nc) as s:
        loaded = s.sem("loaded")
        turned, copied = s.sem("ctx_turned"), s.sem("ctx_copied")
        pt = s.ps("p_ctxT", [P, GROUPS, GROUP, T])
        with s.block() as block:
            @block.sync
            def _(sp):
                sp.dma_start(X, x_dram.rearrange("b t d -> t b d")).then_inc(loaded, 16)
                sp.dma_start(K_tile, consts).then_inc(loaded, 16)

            @block.scalar
            def _(act):
                act.dma_start(ctx, ctx_dram.rearrange("b k d -> k b d")).then_inc(loaded, 16)
                for g in range(GROUPS):
                    act.wait_ge(turned, g + 1)
                    act.copy(ctxT[:, GROUP * g:GROUP * g + GROUP], pt[:, g, :, 0:CTX]).then_inc(copied, 1)

            @block.vector
            def _(dve):
                dve.wait_ge(loaded, 48)
                dve.tensor_copy(K["ident_bf16"], K["ident"])
                dve.tensor_copy(K["causal_bf16"], K["causal"])

            @block.tensor
            def _(pe):
                pe.wait_ge(loaded, 48)
                for g in range(GROUPS):
                    for j in range(GROUP):
                        last = pe.transpose(pt[:, g, j, 0:CTX], ctx[:, GROUP * g + j], K["ident"][0:CTX, 0:CTX])
                    last.then_inc(turned, 1)


def store_result(nc, X, out):
    with Stage(nc) as s:
        stored = s.sem("stored")
        with s.block() as block:
            @block.sync
            def _(sp):
                sp.dma_start(out.rearrange("b t d -> t b d"), X).then_inc(stored, 16)
                sp.wait_ge(stored, 16)


def load(nc, s, loads):
    loaded = s.sem("weights_loaded")
    with s.block() as block:
        @block.sync
        def _(sp):
            for dst, src in loads[0::2]:
                sp.dma_start(dst, src).then_inc(loaded, 16)

        @block.scalar
        def _(act):
            for dst, src in loads[1::2]:
                act.dma_start(dst, src).then_inc(loaded, 16)
            act.wait_ge(loaded, 16 * len(loads))


def row(ap):
    return ap.rearrange("(a n) -> a n", a=1)


def column(ap):
    return ap.rearrange("(p a) -> p a", a=1)


def program(nc, w, out, first=0, last=12):
    ctx = ExitStack()
    with ctx:
        def sb(name, shape, dt=F32):
            return ctx.enter_context(nc.sbuf_tensor(name, shape, dt))

        X = sb("x_residual", [P, B, D])
        XN = sb("x_normed", [P, B, D])
        XT = sb("x_transposed", [P, B, T])
        KT = sb("constants", [P, CONST_W])
        K = {n: KT[:rows, at:at + width] for n, (at, rows, width) in CONST_AT.items()}
        K["ident_bf16"], K["causal_bf16"] = sb("ident_bf16", [P, P], BF16)[:], sb("causal_bf16", [P, P], BF16)[:]
        K["ctx"] = sb("context", [CTX, B, D])[:]
        K["ctxT"] = sb("context_transposed", [D, B, CTX])[:]
        load_constants(nc, K, KT[:], X[:], w["x"], w["constants"], K["ctx"], K["ctxT"], w["ctx_1024"])
        stages = [l0_attn, l0_xattn, l0_ffn, l1_attn, l1_xattn, l1_ffn, l2_attn, l2_xattn, l2_ffn, l3_attn, l3_xattn,
                  l3_ffn]
        for stage in stages[first:last]:
            stage(nc, K, w, X[:], XN[:], XT[:])
        store_result(nc, X[:], out)


def l0_attn(nc, K, w, X, XN, XT):
    with Stage(nc) as s:
        wqkv, wp, bp = s.sb("w_qkv", [D, 3 * D]), s.sb("w_proj", [D, D]), s.sb("b_proj", [1, D])
        layernorm(nc, K, X, XN, XT, loads=[(wqkv[:], w["L0_attn_w_qkv"]), (wp[:], w["L0_attn_w_proj"]), (bp[:], row(w["L0_attn_b_proj"]))])
        attention(nc, K, "l0a", D, 8, XT, XT, T, wqkv[:, 0:D], wqkv[:, D:2 * D], wqkv[:, 2 * D:], wp[:], X, X, bo=bp[:])


def l1_attn(nc, K, w, X, XN, XT):
    with Stage(nc) as s:
        wqkv, wp, bp = s.sb("w_qkv", [D, 3 * D]), s.sb("w_out", [D, D]), s.sb("b_out", [1, D])
        layernorm(nc, K, X, XN, XT, loads=[(wqkv[:], w["L1_attn_Wqkv"]), (wp[:], w["L1_attn_Wout"]), (bp[:], row(w["L1_attn_bout"]))])
        attention(nc, K, "l1a", D, 8, XT, XT, T, wqkv[:, 0:D], wqkv[:, D:2 * D], wqkv[:, 2 * D:], wp[:], X, X, bo=bp[:],
                  rope=True, causal=True)


def l0_xattn(nc, K, w, X, XN, XT):
    layernorm(nc, K, X, XN, XT)
    sc = float(D) ** -0.5
    with Stage(nc) as s:
        top = s.sb("row_max", [P, B])
        inv = s.sb("inverse_sum", [P, B])
        pr = s.sb("probs", [P, B, CTX])
        prT = s.sb("probs_transposed", [CTX, B, T])
        mixed = s.sb("mixed", [P, B, D])
        p_s = s.ps("p_scores", [P, 2, GROUP, T])
        p_t = s.ps("p_probsT", [P, 2, GROUP, T])
        p_o = s.ps("p_mixed", [P, 2, GROUP, D])
        scores_ready, shifted, probs_ready, turned, turned_copied, mixed_ready, scaled, chain = (
            s.sem("x0_" + n) for n in "scores_ready shifted probs_ready turned turned_copied mixed_ready scaled chain".split())

        def group(g):
            return slice(GROUP * g, GROUP * g + GROUP)

        with s.block() as block:
            @block.tensor
            def _(pe):
                def scores(g):
                    wait(pe, shifted, g - 1)
                    for j in range(GROUP):
                        last = pe.matmul(p_s[:, g % 2, j, 0:CTX], XT[:, GROUP * g + j], K["ctxT"][:, GROUP * g + j],
                                         start=True, stop=True)
                    last.then_inc(scores_ready, 1)

                def mix(g):
                    pe.wait_ge(probs_ready, g + 1)
                    wait(pe, turned_copied, g - 1)
                    for j in range(GROUP):
                        last = pe.transpose(p_t[0:CTX, g % 2, j], pr[:, GROUP * g + j], K["ident"])
                    last.then_inc(turned, 1)
                    pe.wait_ge(turned_copied, g + 1)
                    wait(pe, scaled, g - 1)
                    for j in range(GROUP):
                        last = pe.matmul(p_o[:, g % 2, j], prT[:, GROUP * g + j], K["ctx"][:, GROUP * g + j],
                                         start=True, stop=True)
                    last.then_inc(mixed_ready, 1)

                scores(0)
                for g in range(GROUPS):
                    if g < GROUPS - 1:
                        scores(g + 1)
                    mix(g)

            @block.vector
            def _(dve):
                c = Chain(dve, chain)

                def softmax(g):
                    dve.wait_ge(scores_ready, g + 1)
                    c.link(dve.tensor_reduce(top[:, group(g)], p_s[:, g % 2, :, 0:CTX], AX.X, ALU.max))
                    dve.tensor_tensor(pr[:, group(g)], p_s[:, g % 2, :, 0:CTX], bcast(top[:, group(g)], 2, CTX),
                                      ALU.subtract).then_inc(shifted, 1)
                    dve.wait_ge(probs_ready, g + 1)
                    c.link(dve.tensor_reduce(inv[:, group(g)], pr[:, group(g)], AX.X, ALU.add))
                    c.link(dve.reciprocal(inv[:, group(g)], inv[:, group(g)]))

                def add(g):
                    dve.wait_ge(mixed_ready, g + 1)
                    dve.tensor_tensor(mixed[:, group(g)], p_o[:, g % 2], bcast(inv[:, group(g)], 2, D),
                                      ALU.mult).then_inc(scaled, 1)
                    dve.wait_ge(scaled, g + 1)
                    c.link(dve.tensor_tensor(X[:, group(g)], X[:, group(g)], mixed[:, group(g)], ALU.add))

                for g in range(GROUPS):
                    softmax(g)
                    if g:
                        add(g - 1)
                add(GROUPS - 1)

            @block.scalar
            def _(act):
                for g in range(GROUPS):
                    act.wait_ge(shifted, g + 1)
                    act.activation(pr[:, group(g)], pr[:, group(g)], ACT.Exp, scale=sc).then_inc(probs_ready, 1)
                    act.wait_ge(turned, g + 1)
                    act.copy(prT[:, group(g)], p_t[0:CTX, g % 2]).then_inc(turned_copied, 1)


def l2_xattn(nc, K, w, X, XN, XT):
    with Stage(nc) as s:
        wq, wk, wv, wo = (s.sb(n, [D, D]) for n in ("w_q", "w_k", "w_v", "w_o"))
        bq, bk = s.sb("b_q", [D, 1]), s.sb("b_k", [D, 1])
        bv, bo = s.sb("b_v", [1, D]), s.sb("b_o", [1, D])
        layernorm(nc, K, X, XN, XT, loads=[(wq[:], w["L2_xattn_Wq"]), (wk[:], w["L2_xattn_Wk"]), (wv[:], w["L2_xattn_Wv"]),
            (wo[:], w["L2_xattn_Wo"]), (bq[:], column(w["L2_xattn_bq"])), (bk[:], column(w["L2_xattn_bk"])),
            (bv[:], row(w["L2_xattn_bv"])), (bo[:], row(w["L2_xattn_bo"]))])
        tails = s.sb("tails", [P, B // 2, 2, 2, HEADS // 2])
        unresolved = s.sb("unresolved", [1, 1], mybir.dt.int32)

        def attend(ranks, tails=None):
            attention(nc, K, f"l2x{ranks}", D, 8, XT, K["ctxT"], CTX, wq[:], wk[:], wv[:], wo[:], X, XN, bo=bo[:],
                      bqkv=(bq[:], bk[:], bv[:]), ranks=ranks, tails=tails)
        attend(FEW_RANKS, tails[:])
        any_above_zero(nc, K, tails[:].rearrange("p i j f h -> p (i j f h)"), unresolved[:])
        with nc.If(nc.values_load(unresolved[:], min_val=0, max_val=1) > 0):
            nc.all_engine_barrier()
            attend(ALL_RANKS)
        copy_all(nc, X, XN)


def any_above_zero(nc, K, values, flag):
    with Stage(nc) as s:
        most = s.sb("most", [P, 1])
        top = s.sb("top", [1, 1])
        pt = s.ps("p_most", [1, P])
        reduced, turned, chain = (s.sem("any_" + n) for n in ("reduced", "turned", "chain"))
        with s.block() as block:
            @block.vector
            def _(dve):
                dve.tensor_reduce(most[:], values, AX.X, ALU.max).then_inc(reduced, 1)
                dve.wait_ge(turned, 1)
                Chain(dve, chain).link(dve.tensor_reduce(top[:], pt[:], AX.X, ALU.max))
                dve.tensor_scalar(flag, top[:], 0.0, None, ALU.is_gt)

            @block.tensor
            def _(pe):
                pe.wait_ge(reduced, 1)
                pe.transpose(pt[:], most[:], K["ident"]).then_inc(turned, 1)


def copy_all(nc, dst, src):
    with Stage(nc) as s:
        with s.block() as block:
            @block.vector
            def _(dve):
                dve.tensor_copy(dst[:, 0:7], src[:, 0:7])

            @block.scalar
            def _(act):
                act.copy(dst[:, 7:12], src[:, 7:12])

            @block.gpsimd
            def _(pool):
                pool.tensor_copy(dst[:, 12:B], src[:, 12:B])



def first_then_loop(eng, count, turn):
    for j in range(2):
        turn(j, j, 0)
    if count > 2:
        with eng.Fori(1, count // 2) as i:
            for j in range(2):
                turn(i * 2 + j, j, i)


def pair_of(src, i, j):
    if len(src.shape) == 2:
        return src.rearrange("(i j) a -> i j a", j=2)[i, j]
    return src.rearrange("(i j) a b -> i j a b", j=2)[i, j]


def routing(K, s, tT, wr, gates, gate_bias=None, top2=True, renorm=True, eps=0.0, probs_out=None):
    pr = probs_out if probs_out is not None else s.sb("probs", [P, B, EXPERTS])
    rank, rest, first = (s.sb(n, [P, B, EXPERTS]) for n in ("rank", "rest", "first"))
    m, m2, r = (s.sb(n, [P, B]) for n in ("largest", "second", "rank_best"))
    pl = s.ps("p_logits", [P, B, EXPERTS])
    logits_ready, shifted, exp_ready, chain = (s.sem("router_" + n) for n in ("logits", "shifted", "exp", "chain"))

    def logits(pe):
        if gate_bias is not None:
            pe.matmul(pl[:], K["ones"][0:1, :], bcast(gate_bias, 1, B), start=True, stop=False)
        for b in range(B):
            last = pe.matmul(pl[:, b], tT[:, b], wr, start=gate_bias is None,
                             stop=gate_bias is None or b == B - 1)
        last.then_inc(logits_ready, 1)

    def exponentials(act):
        act.wait_ge(shifted, 1)
        act.activation(pr[:], pr[:], ACT.Exp).then_inc(exp_ready, 1)

    def choose(dve):
        c = Chain(dve, chain)
        E = EXPERTS
        dve.wait_ge(logits_ready, 1)
        c.link(dve.tensor_reduce(m[:], pl[:], AX.X, ALU.max))
        dve.tensor_tensor(pr[:], pl[:], bcast(m[:], 2, E), ALU.subtract).then_inc(shifted, 1)
        dve.wait_ge(exp_ready, 1)
        c.link(dve.tensor_reduce(m[:], pr[:], AX.X, ALU.add))
        c.link(dve.reciprocal(m[:], m[:]))
        c.link(dve.tensor_tensor(pr[:], pr[:], bcast(m[:], 2, E), ALU.mult))
        if not top2:
            return

        def one_hot(src, largest, dst):
            c.link(dve.tensor_reduce(largest, src, AX.X, ALU.max))
            c.link(dve.tensor_tensor(rank[:], src, bcast(largest, 2, E), ALU.is_equal))
            c.link(dve.tensor_tensor(rank[:], rank[:], bcast(K["expert_order"], 1, B), ALU.mult))
            c.link(dve.tensor_reduce(r[:], rank[:], AX.X, ALU.max))
            c.link(dve.tensor_tensor(dst, rank[:], bcast(r[:], 2, E), ALU.is_equal))

        one_hot(pr[:], m[:], first[:])
        c.link(dve.scalar_tensor_tensor(rest[:], first[:], -2.0, pr[:], ALU.mult, ALU.add))
        one_hot(rest[:], m2[:], gates)
        c.link(dve.tensor_tensor(gates, gates, bcast(m2[:], 2, E), ALU.mult))
        c.link(dve.tensor_tensor(first[:], first[:], bcast(m[:], 2, E), ALU.mult))
        c.link(dve.tensor_tensor(gates, gates, first[:], ALU.add))
        if renorm:
            c.link(dve.scalar_tensor_tensor(m[:], m[:], eps, m2[:], ALU.add, ALU.add))
            c.link(dve.reciprocal(m[:], m[:]))
            c.link(dve.tensor_tensor(gates, gates, bcast(m[:], 2, E), ALU.mult))
    return logits, exponentials, choose


def router(nc, K, *args, **options):
    with Stage(nc) as s:
        logits, exponentials, choose = routing(K, s, *args, **options)
        with s.block() as block:
            @block.tensor
            def _(pe):
                logits(pe)

            @block.scalar
            def _(act):
                exponentials(act)

            @block.vector
            def _(dve):
                choose(dve)


def experts(nc, K, name, tT, gates, acc, count, F, func, w_in, w_mul, w_out, b_in=None, b_mul=None, b_out=None,
            route=None):
    NC = F // P
    with Stage(nc) as s:
        n_in = F if w_mul is None else 2 * F
        w2 = w_mul is not None
        raw = s.sb("w_in_and_mul", [P, 2, n_in])
        cut, x_cut = s.sb("weights_cut_off", [P, 2, n_in]), s.sb("tokens_cut_off", [P, B, T])
        high, low = (s.sb(n, [P, 2, n_in], F32R) for n in ("weights_high", "weights_low"))
        xh, xl = (s.sb(n, [P, B, T], F32R) for n in ("tokens_high", "tokens_low"))
        wo = s.sb("w_out", [P, 2, NC, D])
        b1 = s.sb("b_in", [P, 2, NC]) if b_in is not None else None
        b2 = s.sb("b_mul", [P, 2, NC]) if b_mul is not None else None
        bo = s.sb("b_out", [1, 2, D]) if b_out is not None else None
        acted = s.sb("activated", [P, 2, GROUP * T]) if w_mul is not None else None
        hid = s.sb("hidden", [P, 2, NC, GROUP * T])
        gated = s.sb("gated", [P, 2, GROUP, D])
        p1 = s.ps("p_in", [P, 2, GROUP * T])
        p2 = s.ps("p_mul", [P, 2, GROUP * T])
        py = s.ps("p_out", [P, 2, GROUP, D])
        S = {n: s.sem(f"{name}_{n}") for n in
             "in_ready mul_ready act_done hidden_ready out_ready gated_s added passed loaded0 loaded1 tokens_cut tokens_split "
             "weights_cut weights_split tokens_high weights_high".split()}
        loaded = (S["loaded0"], S["loaded1"])
        if route is not None:
            logits, exponentials, choose = routing(K, s, tT, gates=gates, **route)
        loads = [(lambda j: raw[:, j, 0:F], w_in, lambda a: a)]
        if w2:
            loads.append((lambda j: raw[:, j, F:2 * F], w_mul, lambda a: a))
        loads.append((lambda j: wo[:, j], w_out, lambda a: a.rearrange("(c p) d -> p c d", p=P)))
        for tile, src in ((b1, b_in), (b2, b_mul)):
            if src is not None:
                loads.append((lambda j, tile=tile: tile[:, j], src, lambda a: a))
        if b_out is not None:
            loads.append((lambda j: bo[:, j], b_out, lambda a: row(a)))
        hid_sem = S["hidden_ready"] if w_mul is not None else S["act_done"]
        last_i = count // 2 - 1

        def is_last(e):
            return isinstance(e, int) and e == count - 1

        with s.block() as block:
            @block.sync
            def _(sp):
                def turn(e, j, i):
                    wait(sp, S["out_ready"], (e - 1) * GROUPS)
                    for tile, src, view in loads:
                        one = src[2 * i + j] if src.shape[0] == count and isinstance(e, int) else (
                            pair_of(src, i, j) if src.shape[0] == count else src[0])
                        sp.dma_start(tile(j), view(one)).then_inc(loaded[j], 16)
                first_then_loop(sp, count, turn)

            @block.tensor
            def _(pe):
                def both(j, at):
                    return high[:, j, at:at + P], low[:, j, at:at + P]

                def project(e, j, i, g):
                    u = e * GROUPS + g
                    tokens = [x[:, GROUP * g:GROUP * g + GROUP] for x in (xh, xl)]
                    if g == 0:
                        wait(pe, S["weights_split"], e + 1)
                        wait(pe, S["weights_high"], e + 1)
                    if isinstance(e, int) and e == 0:
                        pe.wait_ge(S["tokens_high"], g + 1)
                        pe.wait_ge(S["tokens_split"], g + 1)
                    for c in range(NC):
                        q = u * NC + c
                        wait(pe, S["act_done"], q - 1)
                        split_matmul(pe, p1[:, c % 2], both(j, c * P), tokens).then_inc(S["in_ready"], 1)
                        if w2:
                            wait(pe, S["hidden_ready"], q - 1)
                            split_matmul(pe, p2[:, c % 2], both(j, F + c * P), tokens).then_inc(S["mul_ready"], 1)

                def combine(e, j, g):
                    u = e * GROUPS + g
                    wait(pe, hid_sem, (u + 1) * NC)
                    wait(pe, S["gated_s"], u - 1)
                    for t in range(GROUP):
                        for c in range(NC):
                            last = pe.matmul(py[:, g % 2, t], hid[:, g % 2, c, t * P:(t + 1) * P], wo[:, j, c],
                                             start=c == 0, stop=bo is None and c == NC - 1)
                        if bo is not None:
                            last = pe.matmul(py[:, g % 2, t], K["ones"][0:1, :], bo[:, j], start=False, stop=True)
                    last.then_inc(S["out_ready"], 1)

                def turn(e, j, i):
                    for g in range(GROUPS):
                        project(e, j, i, g)
                        if g:
                            combine(e, j, g - 1)
                        elif not (isinstance(e, int) and e == 0):
                            combine(e - 1, 1 - j, GROUPS - 1)
                if route is not None:
                    logits(pe)
                over_pairs(pe, turn, count)
                combine(count - 1, 1, GROUPS - 1)

            @block.scalar
            def _(act):
                def take_weights(e, j):
                    wait(act, S["weights_cut"], e + 1)
                    act.copy(high[:, j], cut[:, j]).then_inc(S["weights_high"], 1)

                def take_tokens(g):
                    part = slice(GROUP * g, GROUP * g + GROUP)
                    act.wait_ge(S["tokens_cut"], g + 1)
                    act.copy(xh[:, part], x_cut[:, part]).then_inc(S["tokens_high"], 1)

                def turn(e, j, i):
                    for g in range(GROUPS):
                        u = e * GROUPS + g
                        for c in range(NC):
                            q = u * NC + c
                            wait(act, S["in_ready"], q + 1)
                            bias = b1[:, j, c:c + 1] if b1 is not None else 0.0
                            if not w2:
                                if c == 0:
                                    wait(act, S["out_ready"], u - 1)
                                act.activation(hid[:, g % 2, c], p1[:, c % 2], func, bias=bias).then_inc(S["act_done"], 1)
                            else:
                                wait(act, S["hidden_ready"], q - 1)
                                act.activation(acted[:, c % 2], p1[:, c % 2], func, bias=bias).then_inc(S["act_done"], 1)
                        if g == 2 and not is_last(e):
                            take_weights(e + 1, 1 - j)
                take_tokens(0)
                take_weights(0, 0)
                for g in range(1, GROUPS):
                    take_tokens(g)
                if route is not None:
                    exponentials(act)
                over_pairs(act, turn, count)

            @block.vector
            def _(dve):
                ge = gates.rearrange("p b (i j) -> p b i j", j=2)

                def cut_tokens(g):
                    part = slice(GROUP * g, GROUP * g + GROUP)
                    high_part(dve, x_cut[:, part], tT[:, part]).then_inc(S["tokens_cut"], 1)

                def cut_weights(e, j, i):
                    dve.wait_ge(loaded[j], (i + 1) * (16 * len(loads)))
                    wait(dve, S["out_ready"], (e - 1) * GROUPS)
                    high_part(dve, cut[:, j], raw[:, j]).then_inc(S["weights_cut"], 1)

                def weigh(e, j, i, g):
                    u = e * GROUPS + g
                    wait(dve, S["out_ready"], u + 1)
                    wait(dve, S["added"], u - 1)
                    dve.tensor_tensor(gated[:, g % 2], py[:, g % 2], bcast(ge[:, GROUP * g:GROUP * g + GROUP, i, j], 2, D),
                                      ALU.mult).then_inc(S["gated_s"], 1)

                def turn(e, j, i):
                    for g in range(GROUPS):
                        u = e * GROUPS + g
                        if w2:
                            for c in range(NC):
                                q = u * NC + c
                                wait(dve, S["mul_ready"], q + 1)
                                wait(dve, S["act_done"], q + 1)
                                if c == 0:
                                    wait(dve, S["out_ready"], u - 1)
                                if b2 is not None:
                                    ins = dve.scalar_tensor_tensor(hid[:, g % 2, c], p2[:, c % 2], b2[:, j, c:c + 1],
                                                                   acted[:, c % 2], ALU.add, ALU.mult)
                                else:
                                    ins = dve.tensor_tensor(hid[:, g % 2, c], p2[:, c % 2], acted[:, c % 2], ALU.mult)
                                ins.then_inc(S["hidden_ready"], 1)
                        if g:
                            weigh(e, j, i, g - 1)
                        elif not (isinstance(e, int) and e == 0):
                            weigh(e - 1, 1 - j, i - 1 if j == 0 else i, GROUPS - 1)
                        if g == 2 and not is_last(e):
                            cut_weights(e + 1, 1 - j, i if j == 0 else i + 1)
                cut_tokens(0)
                cut_weights(0, 0, 0)
                for g in range(1, GROUPS):
                    cut_tokens(g)
                if route is not None:
                    choose(dve)
                over_pairs(dve, turn, count)
                weigh(count - 1, 1, last_i, GROUPS - 1)

            @block.gpsimd
            def _(pool):
                def split_tokens(g):
                    part = slice(GROUP * g, GROUP * g + GROUP)
                    pool.wait_ge(S["tokens_cut"], g + 1)
                    pool.tensor_tensor(xl[:, part], tT[:, part], x_cut[:, part], ALU.subtract).then_inc(S["tokens_split"], 1)

                def split_weights(e, j):
                    wait(pool, S["weights_cut"], e + 1)
                    pool.tensor_tensor(low[:, j], raw[:, j], cut[:, j], ALU.subtract).then_inc(S["weights_split"], 1)

                def turn(e, j, i):
                    for g in range(GROUPS):
                        if g == 2 and not is_last(e):
                            split_weights(e + 1, 1 - j)
                        wait(pool, S["gated_s"], e * GROUPS + g + 1, alone=S["passed"])
                        part = acc[:, GROUP * g:GROUP * g + GROUP]
                        pool.tensor_tensor(part, part, gated[:, g % 2], ALU.add).then_inc(S["added"], 1)
                split_tokens(0)
                split_weights(0, 0)
                for g in range(1, GROUPS):
                    split_tokens(g)
                over_pairs(pool, turn, count)


def add_into(nc, dst, src):
    with Stage(nc) as s:
        with s.block() as block:
            @block.vector
            def _(dve):
                dve.tensor_tensor(dst, dst, src, ALU.add)


def project_all(nc, src, w, dst):
    C = w.shape[1]
    with Stage(nc) as s:
        p = s.ps("p_project", [P, GROUPS, GROUP, T])
        ready = s.sem("project_ready")
        with s.block() as block:
            @block.tensor
            def _(pe):
                for g in range(GROUPS):
                    pe.matmul(p[0:C, g], w, src[:, GROUP * g:GROUP * g + GROUP], start=True, stop=True).then_inc(ready, 1)

            @block.scalar
            def _(act):
                for g in range(GROUPS):
                    act.wait_ge(ready, g + 1)
                    act.copy(dst[:, GROUP * g:GROUP * g + GROUP], p[0:C, g])


def l0_ffn(nc, K, w, X, XN, XT):
    L = w["L0_ffn_w_down"].shape[1]
    F = w["L0_ffn_w1"].shape[2]
    with Stage(nc) as s:
        wd, wr, wup = s.sb("w_down", [D, L]), s.sb("w_router", [D, EXPERTS]), s.sb("w_up", [L, D])
        wqkv = s.sb("w_qkv", [L, 3, L])
        g1, g2 = s.sb("g1", [D, 1]), s.sb("g2", [D, 1])
        res = s.sb("latent_residual", [P, B, D])
        gates = s.sb("gates", [P, B, EXPERTS])
        layernorm(nc, K, X, XN, XT, loads=[(wd[:], w["L0_ffn_w_down"]), (wr[:], w["L0_ffn_router_w"]), (wup[:], w["L0_ffn_w_up"]),
            (wqkv[:, 0], w["L0_ffn_wq"]), (wqkv[:, 1], w["L0_ffn_wk"]), (wqkv[:, 2], w["L0_ffn_wv"]),
            (g1[:], column(w["L0_ffn_g1"])), (g2[:], column(w["L0_ffn_g2"]))])
        layernorm(nc, K, XN, res[:], XT, scale=g1[:], eps=1e-5, rms=True)
        with Stage(nc) as s2:
            cT = s2.sb("latent", [L, B, T])
            project_all(nc, XT, wd[:], cT[:])
            attention(nc, K, "l0f", L, L // HEADS, cT[:], cT[:], T, wqkv[:, 0], wqkv[:, 1], wqkv[:, 2], wup[:], XN, res[:],
                      rope=True, causal=True)
        layernorm(nc, K, res[:], XN, XT, scale=g2[:], eps=1e-5, rms=True)
        add_into(nc, X, res[:])
        experts(nc, K, "l0e", XT, gates[:], X, EXPERTS, F, ACT.Silu, w["L0_ffn_w1"], w["L0_ffn_w3"], w["L0_ffn_w2"],
                route={"wr": wr[:]})


def l1_ffn(nc, K, w, X, XN, XT):
    H = w["L1_ffn_Wo"].shape[0]
    with Stage(nc) as s:
        wg = s.sb("w_gate", [D, EXPERTS])
        gates = s.sb("gates", [P, B, EXPERTS])
        layernorm(nc, K, X, XN, XT, loads=[(wg[:], w["L1_ffn_Wg"])])
        w1, b1 = w["L1_ffn_W1"], w["L1_ffn_b1"]
        experts(nc, K, "l1e", XT, gates[:], X, EXPERTS, H, ACT.Sigmoid, w1[:, :, H:2 * H], w1[:, :, 0:H],
                w["L1_ffn_Wo"].rearrange("(a f) d -> a f d", a=1), b1[:, :, H // P:2 * H // P], b1[:, :, 0:H // P],
                w["L1_ffn_bo"].rearrange("(a d) -> a d", a=1), route={"wr": wg[:], "eps": 1e-9})


def l3_ffn(nc, K, w, X, XN, XT):
    F = w["L3_ffn_rw1"].shape[2]
    with Stage(nc) as s:
        wg, bg = s.sb("w_gate", [D, EXPERTS]), s.sb("b_gate", [1, EXPERTS])
        gates = s.sb("gates", [P, B, EXPERTS])
        halves = s.sb("shared_gates", [P, B, 2])
        layernorm(nc, K, X, XN, XT, loads=[(wg[:], w["L3_ffn_gate_w"]), (bg[:], row(w["L3_ffn_gate_b"]))])
        with s.block() as block:
            @block.vector
            def _(dve):
                dve.memset(halves[:], 0.5)
        routed = {"wr": wg[:], "gate_bias": bg[:], "renorm": False}
        for kind, g, n, route in (("r", gates, EXPERTS, routed), ("s", halves, 2, None)):
            v = {k: w[f"L3_ffn_{kind}{k}"] for k in ("w1", "w2", "w3", "b1", "b2", "b3")}
            experts(nc, K, f"l3{kind}", XT, g[:], X, n, F, ACT.Silu, v["w1"], v["w2"], v["w3"], v["b1"], v["b2"], v["b3"],
                    route=route)



def expert_choice(nc, K, probs, gates, capacity):
    assert B * EXPERTS == P and capacity % 8 == 0
    with Stage(nc) as s:
        by_pair, left, kept = (s.sb(n, [P, T]) for n in ("by_pair", "left", "kept"))
        best = s.sb("best", [P, 8])
        pt = s.ps("p_turned", [P, T])
        turned, chosen, back, chain = (s.sem("choice_" + n) for n in ("turned", "chosen", "back", "chain"))
        flat = "t b e -> t (b e)"
        with s.block() as block:
            @block.tensor
            def _(pe):
                pe.transpose(pt[:], probs.rearrange(flat), K["ident"]).then_inc(turned, 1)
                pe.wait_ge(chosen, 1)
                pe.transpose(pt[:], kept[:], K["ident"]).then_inc(back, 1)

            @block.vector
            def _(dve):
                c = Chain(dve, chain)
                dve.wait_ge(turned, 1)
                c.link(dve.tensor_copy(by_pair[:], pt[:]))
                src = by_pair
                for r in range(capacity // 8):
                    c.link(dve.max(best[:], src[:]))
                    c.link(dve.match_replace(left[:], best[:], src[:], -1.0))
                    src = left
                c.link(dve.tensor_scalar(left[:], left[:], 0.0, None, ALU.is_lt))
                dve.tensor_tensor(kept[:], by_pair[:], left[:], ALU.mult).then_inc(chosen, 1)
                dve.wait_ge(back, 1)
                dve.tensor_copy(gates.rearrange(flat), pt[:])


def l2_ffn(nc, K, w, X, XN, XT):
    F = w["L2_ffn_w1"].shape[2]
    with Stage(nc) as s:
        wg = s.sb("w_gate", [D, EXPERTS])
        probs, gates = s.sb("router_probs", [P, B, EXPERTS]), s.sb("gates", [P, B, EXPERTS])
        layernorm(nc, K, X, XN, XT, loads=[(wg[:], w["L2_ffn_gate_w"])])
        router(nc, K, XT, wg[:], None, top2=False, probs_out=probs)
        expert_choice(nc, K, probs[:], gates[:], 2 * T // EXPERTS)
        experts(nc, K, "l2e", XT, gates[:], X, EXPERTS, F, ACT.Gelu, w["L2_ffn_w1"], None, w["L2_ffn_w2"])


def l1_xattn(nc, K, w, X, XN, XT):
    with Stage(nc) as s:
        wcols = s.sb("w_cq_c_q", [D, 3])
        bs = s.sb("score_biases", [1, 3])
        wl, bl = s.sb("w_l", [D, 4, D]), s.sb("b_l", [1, D])
        qw = s.sb("ctx_weighted", [D, B, CTX])
        qs = s.sb("ctx_scored", [D, B, CTX])
        bsum, ball = s.sb("bias_sum", [1, 1]), s.sb("bias_all", [P, 1])
        sc = s.sb("scores", [P, B, CTX])
        top, inv = s.sb("row_max", [P, B]), s.sb("inverse_sum", [P, B])
        prT = s.sb("probs_transposed", [CTX, 2, GROUP, T])
        aT = s.sb("c2q_transposed", [D, B, T])
        bt = s.sb("b_att_transposed", [B, T])
        bm = s.sb("b_att_scalars", [B, 2])
        batt = s.sb("b_att", [P, B])
        q2c = s.sb("q2c", [D, B])
        cc = s.sb("c_times_c2q", [D, B, T])
        cq = s.sb("c_times_q2c", [D, B, T])
        layernorm(nc, K, X, XN, XT, loads=[(wcols[:, 0:1], column(w["L1_xattn_w_cq"])), (wcols[:, 1:2], column(w["L1_xattn_w_c"])),
            (wcols[:, 2:3], column(w["L1_xattn_w_q"])), (bs[:, 0:1], row(w["L1_xattn_b_cq"])),
            (bs[:, 1:2], row(w["L1_xattn_b_c"])), (bs[:, 2:3], row(w["L1_xattn_b_q"])),
            (wl[:], w["L1_xattn_W_l"].rearrange("(c p) n -> p c n", p=P)), (bl[:], row(w["L1_xattn_b_l"]))])
        p_s = s.ps("p_scores", [P, 2, GROUP, T])
        p_t = s.ps("p_probsT", [P, GROUP, T])
        p_a = s.ps("p_c2q", [P, GROUP, T])
        p_z = s.ps("p_z", [P, 2, GROUP, D])
        p_m = s.ps("p_small", [P, 512])
        names = ("weighted bias_ready ball_ready ball_copied scores_ready scored shifted probs_ready normed turned turned_copied "
                 "c2q_ready c2q_copied tops_ready tops_turned tops_shifted b_exp b_normed b_back b_copied q2c_ready q2c_copied "
                 "products z_ready z_added chain chain_pool")
        S = {n: s.sem("x1_" + n) for n in names.split()}

        def group(g):
            return slice(GROUP * g, GROUP * g + GROUP)

        with s.block() as block:
            @block.tensor
            def _(pe):
                pe.wait_ge(S["bias_ready"], 1)
                pe.matmul(p_m[:, 0:1], K["ones"][0:1, :], bsum[:], start=True, stop=True).then_inc(S["ball_ready"], 1)

                def scores(g):
                    wait(pe, S["weighted"], 2)
                    wait(pe, S["scored"], g - 1)
                    for j in range(GROUP):
                        b = GROUP * g + j
                        pe.matmul(p_s[:, g % 2, j, 0:CTX], XT[:, b], qw[:, b], start=True, stop=False)
                        last = pe.matmul(p_s[:, g % 2, j, 0:CTX], K["ones"], qs[:, b], start=False, stop=True)
                    last.then_inc(S["scores_ready"], 1)

                def mix(g):
                    pe.wait_ge(S["normed"], g + 1)
                    wait(pe, S["turned_copied"], g)
                    for j in range(GROUP):
                        last = pe.transpose(p_t[0:CTX, j], sc[:, GROUP * g + j], K["ident"])
                    last.then_inc(S["turned"], 1)
                    pe.wait_ge(S["turned_copied"], g + 1)
                    wait(pe, S["c2q_copied"], g)
                    for j in range(GROUP):
                        last = pe.matmul(p_a[:, j], K["ctx"][:, GROUP * g + j], prT[:, g % 2, j], start=True, stop=True)
                    last.then_inc(S["c2q_ready"], 1)

                scores(0)
                for g in range(GROUPS):
                    if g < GROUPS - 1:
                        scores(g + 1)
                    mix(g)
                pe.wait_ge(S["tops_ready"], GROUPS)
                pe.wait_ge(S["ball_copied"], 1)
                pe.transpose(p_m[0:B, 0:T], top[:], K["ident"]).then_inc(S["tops_turned"], 1)
                pe.wait_ge(S["b_normed"], 1)
                pe.transpose(p_m[:, 128:128 + B], bt[:], K["ident"][0:B, 0:B]).then_inc(S["b_back"], 1)
                pe.wait_ge(S["b_copied"], 1)
                for b in range(B):
                    last = pe.matmul(p_m[:, 256 + b:257 + b], XN[:, b], batt[:, b:b + 1], start=True, stop=True)
                last.then_inc(S["q2c_ready"], 1)
                for g in range(GROUPS):
                    pe.wait_ge(S["products"], 2 * (g + 1))
                    wait(pe, S["z_added"], g - 1)
                    for j in range(GROUP):
                        b = GROUP * g + j
                        for n, part in enumerate((XT, aT, cc, cq)):
                            pe.matmul(p_z[:, g % 2, j], part[:, b], wl[:, n], start=n == 0, stop=False)
                        last = pe.matmul(p_z[:, g % 2, j], K["ones"][0:1, :], bl[:], start=False, stop=True)
                    last.then_inc(S["z_ready"], 1)

            @block.vector
            def _(dve):
                c = Chain(dve, S["chain"])
                dve.tensor_reduce(bsum[:], bs[:], AX.X, ALU.add).then_inc(S["bias_ready"], 1)
                dve.tensor_scalar(qw[:], K["ctxT"], wcols[:, 0:1], wcols[:, 1:2], ALU.mult, ALU.add).then_inc(S["weighted"], 1)
                dve.wait_ge(S["ball_ready"], 1)
                dve.tensor_copy(ball[:], p_m[:, 0:1]).then_inc(S["ball_copied"], 1)

                def softmax(g):
                    dve.wait_ge(S["scored"], g + 1)
                    dve.tensor_reduce(top[:, group(g)], sc[:, group(g)], AX.X, ALU.max).then_inc(S["tops_ready"], 1)
                    dve.wait_ge(S["tops_ready"], g + 1)
                    dve.tensor_tensor(sc[:, group(g)], sc[:, group(g)], bcast(top[:, group(g)], 2, CTX),
                                      ALU.subtract).then_inc(S["shifted"], 1)
                    dve.wait_ge(S["probs_ready"], g + 1)
                    c.link(dve.tensor_reduce(inv[:, group(g)], sc[:, group(g)], AX.X, ALU.add))
                    c.link(dve.reciprocal(inv[:, group(g)], inv[:, group(g)]))
                    dve.tensor_tensor(sc[:, group(g)], sc[:, group(g)], bcast(inv[:, group(g)], 2, CTX),
                                      ALU.mult).then_inc(S["normed"], 1)

                for g in range(GROUPS):
                    softmax(g)
                dve.wait_ge(S["tops_turned"], 1)
                c.link(dve.tensor_reduce(bm[:, 0:1], p_m[0:B, 0:T], AX.X, ALU.max))
                dve.tensor_scalar(bt[:], p_m[0:B, 0:T], bm[:, 0:1], None, ALU.subtract).then_inc(S["tops_shifted"], 1)
                dve.wait_ge(S["b_exp"], 1)
                c.link(dve.tensor_reduce(bm[:, 1:2], bt[:], AX.X, ALU.add))
                c.link(dve.reciprocal(bm[:, 1:2], bm[:, 1:2]))
                dve.tensor_scalar(bt[:], bt[:], bm[:, 1:2], None, ALU.mult).then_inc(S["b_normed"], 1)
                dve.wait_ge(S["b_back"], 1)
                dve.tensor_copy(batt[:], p_m[:, 128:128 + B]).then_inc(S["b_copied"], 1)
                dve.wait_ge(S["q2c_ready"], 1)
                dve.tensor_copy(q2c[:], p_m[:, 256:256 + B]).then_inc(S["q2c_copied"], 1)
                for g in range(GROUPS):
                    dve.wait_ge(S["c2q_copied"], g + 1)
                    dve.wait_ge(S["q2c_copied"], 1)
                    dve.tensor_tensor(cc[:, group(g)], XT[:, group(g)], aT[:, group(g)], ALU.mult).then_inc(S["products"], 1)
                    dve.tensor_tensor(cq[:, group(g)], XT[:, group(g)], bcast(q2c[:, group(g)], 2, T),
                                      ALU.mult).then_inc(S["products"], 1)
                for g in range(GROUPS):
                    dve.wait_ge(S["z_ready"], g + 1)
                    dve.tensor_tensor(X[:, group(g)], X[:, group(g)], p_z[:, g % 2], ALU.add).then_inc(S["z_added"], 1)

            @block.gpsimd
            def _(pool):
                pool.tensor_scalar(qs[:], K["ctxT"], wcols[:, 2:3], None, ALU.mult).then_inc(S["weighted"], 1)

            @block.scalar
            def _(act):
                act.wait_ge(S["ball_copied"], 1)
                for g in range(GROUPS):
                    act.wait_ge(S["scores_ready"], g + 1)
                    act.activation(sc[:, group(g)], p_s[:, g % 2, :, 0:CTX], ACT.Identity, bias=ball[:]).then_inc(S["scored"], 1)
                    act.wait_ge(S["shifted"], g + 1)
                    act.activation(sc[:, group(g)], sc[:, group(g)], ACT.Exp).then_inc(S["probs_ready"], 1)
                    act.wait_ge(S["turned"], g + 1)
                    wait(act, S["c2q_ready"], g - 1)
                    act.copy(prT[:, g % 2], p_t[0:CTX]).then_inc(S["turned_copied"], 1)
                    act.wait_ge(S["c2q_ready"], g + 1)
                    act.copy(aT[:, group(g)], p_a[:]).then_inc(S["c2q_copied"], 1)
                act.wait_ge(S["tops_shifted"], 1)
                act.activation(bt[:], bt[:], ACT.Exp).then_inc(S["b_exp"], 1)



def scan_channels(nc, K, w, xT, delta, bc, a, y):
    N = a.shape[1]
    HALF = B // 2
    with Stage(nc) as s:
        u = s.sb("delta_x", [P, B, T])
        decay = s.sb("decay", [P, 2, B, T])
        h = s.sb("states", [P, B, T])
        hc = s.sb("states_times_c", [P, 2, B, T])
        pick = s.sb("pick_row", [3 * 2 * N, 2, 2, P], BF16)
        p_b = s.ps("p_b", [P, 2, HALF, T])
        p_c = s.ps("p_c", [P, 2, HALF, T])
        names = "passed picked b_ready b_used c_ready c_used decayed cleared u_ready scanned added zeroed chain"
        S = {n: s.sem("ssm_" + n) for n in names.split()}
        flat = "p b t -> p (b t)"

        def halves(ap):
            return [ap[:, 0:HALF], ap[:, HALF:B]]

        with s.block() as block:
            @block.gpsimd
            def _(pool):
                pool.memset(y, 0.0).then_inc(S["zeroed"], 1)
                ident = K["ident_thrice"].rearrange("r (k i j) -> r k i j", k=2, j=2)

                def pick_rows(n, j, i):
                    wait(pool, S["c_ready"], 2 * (n - 1), alone=S["passed"])
                    pool.tensor_copy(pick[:, j], bcast(ident[:, :, i, j], 2, P)).then_inc(S["picked"], 1)

                def clear(n, j, i):
                    wait(pool, S["decayed"], n + 1, alone=S["passed"])
                    pool.memset(decay[:, j, :, 0:1], 0.0).then_inc(S["cleared"], 1)

                def turn(n, j, i):
                    pick_rows(n, j, i)
                    clear(n, j, i)
                    if isinstance(n, int) and n == 0:
                        pool.wait_ge(S["zeroed"], 1)
                    else:
                        sum_up(n - 1, 1 - j)

                def sum_up(n, j):
                    for hf in range(2):
                        wait(pool, S["c_used"], 2 * n + hf + 1, alone=S["passed"])
                        wait(pool, S["added"], 2 * n + hf - 1, alone=S["passed"])
                        pool.tensor_tensor(halves(y)[hf], halves(y)[hf], halves(hc[:, j])[hf],
                                           ALU.add).then_inc(S["added"], 1)
                first_then_loop(pool, N, turn)
                sum_up(N - 1, 1)

            @block.tensor
            def _(pe):
                def turn(n, j, i):
                    wait(pe, S["picked"], n + 1)
                    for k, (p, ready, used) in enumerate(((p_b, "b_ready", "b_used"), (p_c, "c_ready", "c_used"))):
                        for hf in range(2):
                            wait(pe, S[used], 2 * n + hf - 1)
                            for q in range(2):
                                b = HALF * hf + GROUP * q
                                last = pe.matmul(p[:, hf, GROUP * q:GROUP * q + GROUP], pick[:, j, k], bc[:, b:b + GROUP],
                                                 start=True, stop=True)
                            last.then_inc(S[ready], 1)
                first_then_loop(pe, N, turn)

            @block.scalar
            def _(act):
                a2 = a.rearrange("p (i j) -> p i j", j=2)

                def turn(n, j, i):
                    wait(act, S["scanned"], n - 1)
                    act.activation(decay[:, j], delta, ACT.Exp, scale=a2[:, i, j:j + 1]).then_inc(S["decayed"], 1)
                first_then_loop(act, N, turn)

            @block.vector
            def _(dve):
                dve.tensor_tensor(u[:], delta, xT, ALU.mult).then_inc(S["u_ready"], 1)
                dve.wait_ge(S["u_ready"], 1)

                def turn(n, j, i):
                    wait(dve, S["added"], 2 * (n - 1))
                    for hf in range(2):
                        wait(dve, S["b_ready"], 2 * n + hf + 1)
                        dve.tensor_tensor(halves(hc[:, j])[hf], halves(u)[hf], p_b[:, hf], ALU.mult).then_inc(S["b_used"], 1)
                    wait(dve, S["b_used"], 2 * n + 2)
                    wait(dve, S["cleared"], n + 1)
                    wait(dve, S["c_used"], 2 * n)
                    dve.tensor_tensor_scan(h[:].rearrange(flat), decay[:, j].rearrange(flat), hc[:, j].rearrange(flat), 0.0,
                                           ALU.mult, ALU.add).then_inc(S["scanned"], 1)
                    wait(dve, S["scanned"], n + 1)
                    for hf in range(2):
                        wait(dve, S["c_ready"], 2 * n + hf + 1)
                        dve.tensor_tensor(halves(hc[:, j])[hf], halves(h)[hf], p_c[:, hf], ALU.mult).then_inc(S["c_used"], 1)
                first_then_loop(dve, N, turn)


def l3_attn(nc, K, w, X, XN, XT):
    N = w["L3_attn_A_log"].shape[1]
    F = w["L3_attn_W1"].shape[1]
    with Stage(nc) as s:
        cols = s.sb("columns", [D, 6])
        g1, b1, g2, b2, bd, dskip = (cols[:, k:k + 1] for k in range(6))
        wd, wbc, bbc = s.sb("w_delta", [D, D]), s.sb("w_bc", [D, 3, 2 * N]), s.sb("b_bc", [3 * 2 * N, 1])
        a, bout = s.sb("a", [D, N]), s.sb("b_2", [1, D])
        ssm = s.sb("ssm_out", [P, B, D])
        layernorm(nc, K, X, XN, XT, loads=[(g1, column(w["L3_attn_ln1_g"])), (b1, column(w["L3_attn_ln1_b"])), (g2, column(w["L3_attn_ln2_g"])),
            (b2, column(w["L3_attn_ln2_b"])), (bd, column(w["L3_attn_bd"])), (dskip, column(w["L3_attn_D"])),
            (wd[:], w["L3_attn_Wd"]), 
            (a[:], w["L3_attn_A_log"]), (bout[:], row(w["L3_attn_b2"]))]
            + [(wbc[:, m], w["L3_attn_Wbc"]) for m in range(3)]
            + [(bbc[2 * N * m:2 * N * (m + 1)], column(w["L3_attn_bbc"])) for m in range(3)])
        layernorm(nc, K, XN, ssm[:], XT, scale=g1, bias=b1)
        with Stage(nc) as s2:
            R = 2 * N
            delta, y = s2.sb("delta", [P, B, T]), s2.sb("y", [P, B, T])
            bc = s2.sb("b_and_c_parts", [3 * R, B, T], BF16)
            with Stage(nc) as s3:
                z, soft = s3.sb("z", [P, B, T]), s3.sb("softplus", [P, B, T])
                p = s3.ps("p_delta", [P, 2, GROUP, T])
                pb = s3.ps("p_bc", [P, 2, GROUP, T])
                value = s3.sb("b_and_c", [3 * R, B, T])
                high, middle = (s3.sb(n, [3 * R, B, T], BF16) for n in ("high_part", "middle_part"))
                ready, copied, z_ready, split, chain = (s3.sem("delta_" + n) for n in ("ready", "copied", "z", "split", "chain"))
                with s3.block() as block:
                    @block.tensor
                    def _(pe):
                        for g in range(GROUPS):
                            part = XT[:, GROUP * g:GROUP * g + GROUP]
                            wait(pe, copied, g - 1)
                            pe.matmul(p[:, g % 2], wd[:], part, start=True, stop=True)
                            pe.matmul(pb[0:3 * R, g % 2], wbc[:].rearrange("d m r -> d (m r)"), part, start=True, stop=True).then_inc(ready, 1)

                    @block.scalar
                    def _(act):
                        c = Chain(act, chain)
                        c.link(act.activation(a[:], a[:], ACT.Exp))
                        act.mul(a[:], a[:], -1.0)
                        for g in range(GROUPS):
                            act.wait_ge(ready, g + 1)
                            part = slice(GROUP * g, GROUP * g + GROUP)
                            act.activation(z[:, part], p[:, g % 2], ACT.Identity, bias=bd)
                            act.activation(value[:, part], pb[0:3 * R, g % 2], ACT.Identity, bias=bbc[:]).then_inc(copied, 1)
                        act.wait_ge(copied, GROUPS)
                        c.link(act.activation(soft[:], z[:], ACT.Abs))
                        c.link(act.activation(soft[:], soft[:], ACT.Exp, scale=-1.0))
                        act.activation(soft[:], soft[:], ACT.Ln, bias=1.0).then_inc(z_ready, 1)

                    @block.vector
                    def _(dve):
                        c = Chain(dve, split)
                        dve.wait_ge(copied, GROUPS)
                        c.link(dve.tensor_copy(high[:], value[:]))
                        c.link(dve.tensor_tensor(value[:], value[:], high[:], ALU.subtract))
                        c.link(dve.tensor_copy(middle[:], value[:]))
                        dve.tensor_tensor(bc[2 * R:3 * R], value[2 * R:3 * R], middle[2 * R:3 * R], ALU.subtract)
                        dve.tensor_copy(bc[0:R], high[0:R])
                        dve.tensor_copy(bc[R:2 * R], middle[R:2 * R])
                        dve.wait_ge(z_ready, 1)
                        dve.scalar_tensor_tensor(delta[:], z[:], 0.0, soft[:], ALU.max, ALU.add)
            scan_channels(nc, K, w, XT, delta[:], bc[:], a[:], y[:])
            with Stage(nc) as s3:
                p = s3.ps("p_turned", [P, GROUPS, GROUP, D])
                pbias = s3.ps("p_bias", [P, D])
                bias = s3.sb("bias_rows", [P, D])
                skip, turned, bias_ready, chain = (s3.sem("ssmout_" + n) for n in ("skip", "turned", "bias", "chain"))
                with s3.block() as block:
                    @block.tensor
                    def _(pe):
                        pe.matmul(pbias[:], K["ones"][0:1, :], bout[:], start=True, stop=True).then_inc(bias_ready, 1)
                        pe.wait_ge(skip, 1)
                        for g in range(GROUPS):
                            for j in range(GROUP):
                                last = pe.transpose(p[:, g, j], y[:, GROUP * g + j], K["ident"])
                            last.then_inc(turned, 1)

                    @block.vector
                    def _(dve):
                        c = Chain(dve, chain)
                        dve.scalar_tensor_tensor(y[:], XT, dskip, y[:], ALU.mult, ALU.add).then_inc(skip, 1)
                        dve.wait_ge(bias_ready, 1)
                        c.link(dve.tensor_copy(bias[:], pbias[:]))
                        c.link(dve.tensor_tensor(X, X, bcast(bias[:], 1, B), ALU.add))
                        for g in range(GROUPS):
                            part = slice(GROUP * g, GROUP * g + GROUP)
                            dve.wait_ge(turned, g + 1)
                            c.link(dve.tensor_tensor(ssm[:, part], XN[:, part], p[:, g], ALU.add))
                            c.link(dve.tensor_tensor(X[:, part], X[:, part], ssm[:, part], ALU.add))
        layernorm(nc, K, ssm[:], XN, XT, scale=g2, bias=b2)
        gates = s.sb("gates_of_one", [P, B, 2])
        with s.block() as block:
            @block.vector
            def _(dve):
                dve.memset(gates[:], 1.0)
        experts(nc, K, "l3m", XT, gates[:], X, 2, F // 2, ACT.Gelu, w["L3_attn_W1"].rearrange("d (e f) -> e d f", e=2), None,
                w["L3_attn_W2"].rearrange("(e f) d -> e f d", e=2), b_in=w["L3_attn_b1"].rearrange("p (e c) -> e p c", e=2))


def l3_xattn(nc, K, w, X, XN, XT):
    layernorm(nc, K, X, XN, XT)
    BIG = 1e30
    I, J = CTX, T
    UNROLL = 4
    TRIPS = (I - 1) // UNROLL
    assert TRIPS * UNROLL == I - 1
    with Stage(nc) as s:
        path = s.sb("path", [I, B, J])
        with Stage(nc) as s2:
            lf = s2.sb("dist_then_left", [B, I, J + 1])
            R = s2.sb("cost_then_path", [B, I + 1, J + 1])
            W = s2.sb("diag_and_up", [B, I, 2, J], BF16)
            with Stage(nc) as s3:
                dist = s3.sb("distances", [I, B, J])
                sq = s3.sb("squares", [P, 2, GROUP, T])
                cm = s3.sb("ctxT_times_minus_2", [D, B, CTX])
                csq = s3.sb("ctx_squares", [CTX, B, D])
                aa = s3.sb("ctx_norms", [CTX, B])
                p_d = s3.ps("p_dist", [P, 2, GROUP, T])
                names = "scaled squared csq_ready dist_ready dist_copied rooted moved chain"
                S = {n: s3.sem("dist_" + n) for n in names.split()}

                def group(g):
                    return slice(GROUP * g, GROUP * g + GROUP)

                with s3.block() as block:
                    @block.gpsimd
                    def _(pool):
                        pool.tensor_scalar(cm[:], K["ctxT"], -2.0, None, ALU.mult).then_inc(S["scaled"], 1)

                    @block.scalar
                    def _(act):
                        act.activation(csq[:], K["ctx"], ACT.Square).then_inc(S["csq_ready"], 1)
                        for g in range(GROUPS):
                            wait(act, S["dist_ready"], g - 1)
                            act.activation(sq[:, g % 2], XT[:, group(g)], ACT.Square).then_inc(S["squared"], 1)
                        for g in range(GROUPS):
                            act.wait_ge(S["dist_copied"], g + 1)
                            act.activation(dist[:, group(g)], dist[:, group(g)], ACT.Sqrt).then_inc(S["rooted"], 1)

                    @block.tensor
                    def _(pe):
                        pe.wait_ge(S["scaled"], 1)
                        for g in range(GROUPS):
                            pe.wait_ge(S["squared"], g + 1)
                            wait(pe, S["dist_copied"], g - 1)
                            for j in range(GROUP):
                                pe.matmul(p_d[0:CTX, g % 2, j], cm[:, GROUP * g + j], XT[:, GROUP * g + j],
                                          start=True, stop=False)
                                last = pe.matmul(p_d[0:CTX, g % 2, j], K["ones"][:, 0:CTX], sq[:, g % 2, j],
                                                 start=False, stop=True)
                            last.then_inc(S["dist_ready"], 1)

                    @block.vector
                    def _(dve):
                        c = Chain(dve, S["chain"])
                        dve.wait_ge(S["csq_ready"], 1)
                        c.link(dve.tensor_reduce(aa[:], csq[:], AX.X, ALU.add))
                        for g in range(GROUPS):
                            dve.wait_ge(S["dist_ready"], g + 1)
                            c.link(dve.tensor_tensor(dist[:, group(g)], p_d[0:CTX, g % 2], bcast(aa[:, group(g)], 2, T), ALU.add))
                            dve.tensor_scalar(dist[:, group(g)], dist[:, group(g)], 0.0, None, ALU.max).then_inc(S["dist_copied"], 1)

                    @block.sync
                    def _(sp):
                        for b in range(B):
                            sp.wait_ge(S["rooted"], b // GROUP + 1)
                            sp.dma_start(lf[b:b + 1, :, 0:J], dist[:, b]).then_inc(S["moved"], 16)
                        sp.wait_ge(S["moved"], 16 * B)
            with Stage(nc) as s3:
                best = s3.sb("best_above", [B, 2, J])
                steeper = s3.sb("diagonal_before_up", [B, 2, J])
                taken = s3.sb("taken", [B, 2, J + 1])
                inflow = s3.sb("inflow", [B, J])
                chain = s3.sem("dtw_chain")
                fwd, back = s3.sem("dtw_forward"), s3.sem("dtw_back")
                moved = s3.sem("dtw_moved")
                on_row = s3.sb("path_row", [B, 2, J])
                left_row = s3.sb("left_row", [B, 2, J + 1])
                chosen, left_copied, row_ready, row_stored, passed = (
                    s3.sem("dtw_" + n) for n in ("chosen", "left_copied", "row_ready", "row_stored", "passed"))
                on = R[:, 0:I, 0:J]
                o_trips = R[:, 0:I - 1, 0:J].rearrange("b (i a) j -> b i a j", a=UNROLL)
                l_trips = lf[:, 0:I - 1].rearrange("b (i a) j -> b i a j", a=UNROLL)
                w_trips = W[:, 1:I].rearrange("b (i a) m j -> b i a m j", a=UNROLL)
                with s3.block() as block:
                    @block.vector
                    def _(dve):
                        c = Chain(dve, chain)
                        c.link(dve.memset(R[:, 0], BIG))
                        c.link(dve.memset(R[:, :, 0:1], BIG))
                        c.link(dve.memset(R[:, 0, 0:1], 0.0))
                        c.link(dve.memset(lf[:, :, J:J + 1], 0.0))
                        wl = lf[:, :, 0:J]

                        def above(row, slot):
                            return dve.tensor_tensor(best[:, slot], row[:, 0:J], row[:, 1:J + 1], ALU.min)

                        def cost(row, d, slot):
                            return dve.tensor_tensor_scan(row[:, 1:J + 1], best[:, slot], d, BIG, ALU.min, ALU.add)

                        def goes_left(this, d, slot):
                            return dve.tensor_tensor(d, this[:, 0:J], best[:, slot], ALU.is_lt)

                        def compare(row, slot):
                            return dve.tensor_tensor(steeper[:, slot], row[:, 0:J], row[:, 1:J + 1], ALU.is_le)

                        def goes_diagonal(dst, left, slot):
                            return dve.tensor_tensor(dst[:, 0], steeper[:, slot], left, ALU.is_gt)

                        def goes_up(dst, left, slot):
                            return dve.scalar_tensor_tensor(dst[:, 1], steeper[:, slot], 0.5, left, ALU.is_lt, ALU.is_gt)

                        c.link(above(R[:, 0], 0))
                        c.link(cost(R[:, 1], wl[:, 0], 0))
                        f = Chain(dve, fwd, 6 * UNROLL)
                        R0, R1, R2 = (R[:, k:k + I - 1].rearrange("b (i a) j -> b i a j", a=UNROLL) for k in range(3))
                        d0, d1 = (wl[:, k:k + I - 1].rearrange("b (i a) j -> b i a j", a=UNROLL) for k in range(2))
                        w0 = W[:, 0:I - 1].rearrange("b (i a) m j -> b i a m j", a=UNROLL)
                        with dve.Fori(0, TRIPS) as n:
                            f.turn(n)
                            for j in range(UNROLL):
                                f.count(above(R1[:, n, j], 1 - j % 2))
                                f.count(goes_left(R1[:, n, j], d0[:, n, j], j % 2))
                                f.count(compare(R0[:, n, j], j % 2))
                                f.until(2)
                                f.count(cost(R2[:, n, j], d1[:, n, j], 1 - j % 2))
                                f.until(1)
                                f.count(goes_diagonal(w0[:, n, j], d0[:, n, j], j % 2))
                                f.count(goes_up(w0[:, n, j], d0[:, n, j], j % 2))
                                f.until(2)
                        c.link(goes_left(R[:, I], wl[:, I - 1], (I - 1) % 2))
                        c.link(compare(R[:, I - 1], 0))
                        c.link(goes_diagonal(W[:, I - 1], wl[:, I - 1], 0))
                        c.link(goes_up(W[:, I - 1], wl[:, I - 1], 0))
                        dve.memset(taken[:], 0.0)
                        c.link(dve.memset(inflow[:], 0.0))
                        c.link(dve.memset(inflow[:, J - 1:J], 1.0))

                        def row_back(j):
                            return dve.tensor_tensor_scan(on_row[:, j, ::-1], left_row[:, j, J:0:-1], inflow[:, ::-1], 0.0,
                                                          ALU.mult, ALU.add)
                        dve.engine_nop().then_inc(chosen, 1)
                        dve.wait_ge(left_copied, 1)
                        row_back(0).then_inc(row_ready, 1)
                        k = Chain(dve, back, 2)
                        with dve.Fori(0, TRIPS) as n:
                            for j in range(UNROLL):
                                m = n * UNROLL + j
                                k.turn(m)
                                dve.wait_ge(row_stored, 1 + m)
                                dve.wait_ge(left_copied, m + 2)
                                wait(dve, row_ready, 1 + m + 1, alone=passed)
                                k.link(dve.tensor_tensor(taken[:, :, 0:J], bcast(on_row[:, j % 2], 1, 2),
                                                         w_trips[:, TRIPS - 1 - n, UNROLL - 1 - j], ALU.mult))
                                k.link(dve.tensor_tensor(inflow[:], taken[:, 0, 1:J + 1], taken[:, 1, 0:J], ALU.add))
                                row_back(1 - j % 2).then_inc(row_ready, 1)

                    @block.scalar
                    def _(act):
                        act.wait_ge(chosen, 1)
                        act.sem_inc(row_ready, 1)
                        act.sem_inc(row_stored, 1)
                        act.copy(left_row[:, 0], lf[:, I - 1]).then_inc(left_copied, 1)
                        with act.Fori(0, TRIPS) as n:
                            for j in range(UNROLL):
                                act.wait_ge(row_ready, 1 + n * UNROLL + j)
                                act.copy(left_row[:, 1 - j % 2], l_trips[:, TRIPS - 1 - n, UNROLL - 1 - j]).then_inc(left_copied, 1)

                    @block.gpsimd
                    def _(pool):
                        pool.wait_ge(row_ready, 1 + 1)
                        pool.tensor_copy(on[:, I - 1], on_row[:, 0]).then_inc(row_stored, 1)
                        with pool.Fori(0, TRIPS) as n:
                            for j in range(UNROLL):
                                wait(pool, row_ready, 1 + n * UNROLL + (j + 2), alone=passed)
                                pool.tensor_copy(o_trips[:, TRIPS - 1 - n, UNROLL - 1 - j], on_row[:, 1 - j % 2]).then_inc(row_stored, 1)

                    @block.sync
                    def _(sp):
                        sp.wait_ge(row_stored, 1 + I)
                        for b in range(B):
                            sp.dma_start(path[:, b], R[b:b + 1, 0:I, 0:J]).then_inc(moved, 16)
                        sp.wait_ge(moved, 16 * B)
        with Stage(nc) as s2:
            p = s2.ps("p_expanded", [P, GROUPS, GROUP, D])
            ready = s2.sem("expanded")
            with s2.block() as block:
                @block.tensor
                def _(pe):
                    for g in range(GROUPS):
                        for j in range(GROUP):
                            last = pe.matmul(p[:, g, j], path[:, GROUP * g + j], K["ctx"][:, GROUP * g + j], start=True, stop=True)
                        last.then_inc(ready, 1)

                @block.vector
                def _(dve):
                    for g in range(GROUPS):
                        part = slice(GROUP * g, GROUP * g + GROUP)
                        dve.wait_ge(ready, g + 1)
                        dve.tensor_tensor(X[:, part], X[:, part], p[:, g], ALU.add)



FIR_DVE, FIR_POOL = 33, 14
H4, DH = 4, 32
CONV, SHORT, LONG = 4, 5, 64
NS = 4 * 4 * H4


def by_head(ap):
    return ap.rearrange("t b (h d) -> t (b h) d", d=DH)


def taps(nc, K, w, XT, q_tok, k_tok, v_tok, fs_tok, fl_tok):
    PRODUCTS = 4
    PAD = LONG - 1
    FIR_PE = LONG - FIR_DVE - FIR_POOL
    HALF = B // 2
    with Stage(nc) as s:
        wqkv, cw, fl, fs = (w[n] for n in ("w_qkv", "conv_taps", "fir_long", "fir_short"))
        pre = s.sb("projected", [P, B, CONV - 1 + T])
        y = s.sb("convolved", [P, B, T])
        qk = s.sb("silu_qk", [P, B, T])
        vp = s.sb("v_padded", [P, B, PAD + T])
        diag = s.sb("diagonals", [P, FIR_PE + SHORT, P])
        product = s.sb("products", [P, PRODUCTS, HALF, T])
        part_dve, part_pool = s.sb("part_dve", [P, B, T]), s.sb("part_pool", [P, B, T])
        f = s.sb("filtered", [P, B, T])
        p = s.ps("p_wide", [P, GROUPS, GROUP, T])
        pt = s.ps("p_turned", [P, GROUPS, GROUP, T])
        S = {n: s.sem("taps_" + n) for n in
             "padded projected copied convolved active diag_ready filtered_ready filtered turned turned_copied chain "
             "product pool_added".split()}

        def group(g):
            return slice(GROUP * g, GROUP * g + GROUP)

        halves = (slice(0, HALF), slice(HALF, B))

        with s.block() as block:
            @block.gpsimd
            def _(pool):
                pool.memset(pre[:, :, 0:CONV - 1], 0.0).then_inc(S["padded"], 1)
                pool.memset(vp[:, :, 0:PAD], 0.0).then_inc(S["padded"], 1)
                pool.tensor_tensor(diag[:, FIR_PE:], bcast(K["ident"], 1, SHORT), bcast(fs[:], 2, P), ALU.mult)
                pool.tensor_tensor(diag[:, 0:FIR_PE], bcast(K["ident"], 1, FIR_PE), bcast(fl[:, 0:FIR_PE], 2, P),
                                   ALU.mult).then_inc(S["diag_ready"], 1)
                for u in range(2 * FIR_POOL):
                    b = halves[u % 2]
                    pool.wait_ge(S["product"], u + 1)
                    wait(pool, S["pool_added"], u - 1)
                    if u < 2:
                        ins = pool.tensor_copy(part_pool[:, b], product[:, u % PRODUCTS])
                    else:
                        ins = pool.tensor_tensor(part_pool[:, b], part_pool[:, b], product[:, u % PRODUCTS], ALU.add)
                    ins.then_inc(S["pool_added"], 1)

            @block.tensor
            def _(pe):
                def turn_back(src, k):
                    for g in range(GROUPS):
                        wait(pe, S["turned_copied"], 4 * (k - 1) + g + 1)
                        for j in range(GROUP):
                            last = pe.transpose(pt[:, g, j], src[:, GROUP * g + j], K["ident"])
                        last.then_inc(S["turned"], 1)

                def project(m):
                    for g in range(GROUPS):
                        wait(pe, S["copied"], 4 * (m - 1) + g + 1)
                        pe.matmul(p[:, g], wqkv[:, m], XT[:, group(g)], start=True, stop=True).then_inc(S["projected"], 1)

                def fir(at, count, first, k):
                    for g in range(GROUPS):
                        wait(pe, S["copied"], 12)
                        wait(pe, S["filtered"], 4 * (k - 1) + g + 1)
                        for n in range(count):
                            last = pe.matmul(p[:, g], diag[:, at + n], vp[:, group(g), first + n:first + n + T],
                                             start=n == 0, stop=n == count - 1)
                        last.then_inc(S["filtered_ready"], 1)

                project(0)
                project(1)
                pe.wait_ge(S["active"], 1)
                turn_back(qk, 0)
                project(2)
                pe.wait_ge(S["active"], 2)
                turn_back(qk, 1)
                pe.wait_ge(S["active"], 3)
                turn_back(vp[:, :, PAD:], 2)
                pe.wait_ge(S["diag_ready"], 1)
                fir(FIR_PE, SHORT, LONG - SHORT, 0)
                pe.wait_ge(S["filtered"], 4)
                turn_back(f, 3)
                fir(0, FIR_PE, 0, 1)
                pe.wait_ge(S["filtered"], 8)
                turn_back(f, 4)

            @block.vector
            def _(dve):
                c = Chain(dve, S["chain"])
                dve.wait_ge(S["padded"], 2)
                for m in range(3):
                    dve.wait_ge(S["copied"], 4 * (m + 1))
                    wait(dve, S["active"], m)
                    for k in range(CONV):
                        src = pre[:, :, k:k + T]
                        if k == 0:
                            ins = dve.tensor_scalar(y[:], src, cw[:, m, 0:1], None, ALU.mult)
                        else:
                            ins = dve.scalar_tensor_tensor(y[:], src, cw[:, m, k:k + 1], y[:], ALU.mult, ALU.add)
                        if k < CONV - 1:
                            c.link(ins)
                    ins.then_inc(S["convolved"], 1)
                dve.wait_ge(S["active"], 3)
                for n in range(FIR_PE, FIR_PE + FIR_DVE):
                    for b in halves:
                        src, tap = vp[:, b, n:n + T], fl[:, n:n + 1]
                        if n == FIR_PE:
                            ins = dve.tensor_scalar(part_dve[:, b], src, tap, None, ALU.mult)
                        else:
                            ins = dve.scalar_tensor_tensor(part_dve[:, b], src, tap, part_dve[:, b], ALU.mult, ALU.add)
                        c.link(ins, lag=1)
                wait(dve, S["chain"], c.k)
                dve.wait_ge(S["pool_added"], 2 * FIR_POOL)
                c.link(dve.tensor_tensor(part_dve[:], part_dve[:], part_pool[:], ALU.add))
                for g in range(GROUPS):
                    dve.wait_ge(S["filtered_ready"], 4 + g + 1)
                    dve.tensor_tensor(f[:, group(g)], p[:, g], part_dve[:, group(g)], ALU.add).then_inc(S["filtered"], 1)

            @block.scalar
            def _(act):
                def project_out(m):
                    wait(act, S["padded"], 2)
                    wait(act, S["convolved"], m)
                    for g in range(GROUPS):
                        act.wait_ge(S["projected"], 4 * m + g + 1)
                        act.copy(pre[:, group(g), CONV - 1:], p[:, g]).then_inc(S["copied"], 1)

                def activate(m, dst):
                    act.wait_ge(S["convolved"], m + 1)
                    act.activation(dst, y[:], ACT.Silu).then_inc(S["active"], 1)

                units = iter(range(2 * FIR_POOL))

                def products(count):
                    for u in islice(units, count):
                        n = FIR_PE + FIR_DVE + u // 2
                        wait(act, S["pool_added"], u - PRODUCTS + 1)
                        act.activation(product[:, u % PRODUCTS], vp[:, halves[u % 2], n:n + T], ACT.Copy,
                                       scale=fl[:, n:n + 1]).then_inc(S["product"], 1)

                def turned_out(k, dst):
                    for g in range(GROUPS):
                        act.wait_ge(S["turned"], 4 * k + g + 1)
                        act.copy(dst[:, group(g)], pt[:, g]).then_inc(S["turned_copied"], 1)
                        if k in (2, 3):
                            products(3)

                def filtered_out():
                    for g in range(GROUPS):
                        act.wait_ge(S["filtered_ready"], g + 1)
                        act.copy(f[:, group(g)], p[:, g]).then_inc(S["filtered"], 1)

                project_out(0)
                activate(0, qk[:])
                project_out(1)
                turned_out(0, q_tok)
                activate(1, qk[:])
                project_out(2)
                turned_out(1, k_tok)
                activate(2, vp[:, :, PAD:])
                act.wait_ge(S["active"], 3)
                products(2)
                turned_out(2, v_tok)
                filtered_out()
                turned_out(3, fs_tok)
                products(2 * FIR_POOL)
                turned_out(4, fl_tok)


def delta_scales(nc, K, w, XT, q_tok, k_tok, v_tok, vb, beta, rq, rk):
    with Stage(nc) as s:
        wb = w["w_beta"]
        sq = s.sb("squares", [P, 2, B, D])
        p = s.ps("p_beta", [P, B, H4])
        beta_p, beta_ready, squared, summed, rooted, chain = (
            s.sem("dscale_" + n) for n in ("beta_p", "beta", "squared", "summed", "rooted", "chain"))
        with s.block() as block:
            @block.tensor
            def _(pe):
                for b in range(B):
                    last = pe.matmul(p[:, b], XT[:, b], wb[:], start=True, stop=True)
                last.then_inc(beta_p, 1)

            @block.scalar
            def _(act):
                act.activation(sq[:, 0], q_tok, ACT.Square).then_inc(squared, 1)
                act.activation(sq[:, 1], k_tok, ACT.Square).then_inc(squared, 1)
                act.wait_ge(beta_p, 1)
                act.activation(beta, p[:], ACT.Sigmoid).then_inc(beta_ready, 1)
                act.wait_ge(summed, 2)
                act.activation(rq, rq, ACT.Sqrt)
                act.activation(rk, rk, ACT.Sqrt).then_inc(rooted, 1)

            @block.vector
            def _(dve):
                c = Chain(dve, chain)
                for m, r in enumerate((rq, rk)):
                    dve.wait_ge(squared, m + 1)
                    flat = r.rearrange("p b h -> p (b h)")
                    c.link(dve.tensor_reduce(flat, by_head(sq[:, m]), AX.X, ALU.add))
                    dve.tensor_scalar(r, r, 1e-6, None, ALU.add).then_inc(summed, 1)
                dve.wait_ge(beta_ready, 1)
                dve.tensor_tensor(by_head(vb), by_head(v_tok), bcast(beta.rearrange("p b h -> p (b h)"), 2, DH), ALU.mult)
                dve.wait_ge(rooted, 1)
                dve.reciprocal(rq, rq)
                dve.reciprocal(rk, rk)


def delta_rule(nc, K, q_tok, k_tok, vb, beta, rq, rk, out):
    NL = LEVELS - 2
    PAIRS = B // 2
    with Stage(nc) as s:
        st = s.sb("scaled_tok", [P, 2, 3, D])
        ft = s.sb("scaled_ch", [P, 2, 3, T])
        fsp = s.sb("scaled_ch_spread", [P, 2, 3, H4, T])
        at = s.sb("a_turned", [P, 2, 2, H4, T])
        lt = s.sb("local_turned", [P, 2, 2, H4, T])
        x = s.sb("x_inverse", [P, 2, 2, H4, T])
        yv = s.sb("y_inverse_turned", [P, 2, 2, H4, T])
        t1 = s.sb("a_times_x", [P, 2, H4, T])
        u0, u0_first, zc, u = (s.sb(n, [P, 2, D]) for n in ("u_before_last", "u_first_half", "a_times_u", "u"))
        p1 = s.ps("p_one", [P, 2, H4, T])
        px = s.ps("p_x", [P, 2, H4, T])
        py = s.ps("p_y", [P, 2, H4, T])
        pz = s.ps("p_next", [P, 2, H4, T])
        names = ("passed scaled turned turned_copied a_turned_ready a_turned_masked a_ready a_masked local_ready local_masked "
                 "started ax_ready ax_masked step_ready updated u0_ready u0_copied z_ready z_copied w_ready u_ready o_ready "
                 "stored chain_scale")
        S = {n: s.sem("delta_" + n) for n in names.split()}
        h3 = "p (h d) -> p h d"

        def tile4(ap):
            return bcast(ap, 1, H4)

        def by_pair(t):
            if len(t.shape) == 2:
                return t.rearrange("p (i m j) -> p i m j", m=2, j=2)
            return t.rearrange("p (i m j) t -> p i m j t", m=2, j=2)

        def nth(n, j):
            return n * 2 + (j + 1)

        def nth_level(n, level, j):
            return n * (2 * NL) + (level * 2 + j + 1)

        def pair_behind(n, m, i):
            if isinstance(n, int) and n == PAIRS - 1:
                return None
            return n + 1, 1 - m, (i if m == 0 else i + 1)

        with s.block() as block:
            @block.gpsimd
            def _(pool):
                def start(n, m, i):
                    for j in range(2):
                        wait(pool, S["a_masked"], nth(n, j), alone=S["passed"])
                        pool.tensor_tensor(yv[:, m, j], tile4(K["ident"]), yv[:, m, j], ALU.subtract)
                        pool.tensor_tensor(x[:, m, j], tile4(K["ident"]), x[:, m, j], ALU.subtract).then_inc(S["started"], 1)
                over_pairs(pool, start, PAIRS)

            @block.vector
            def _(dve):
                q4, k4, r_q, r_k, bt, out4 = (by_pair(t) for t in (q_tok, k_tok, rq, rk, beta, out))
                cs = Chain(dve, S["chain_scale"], 2)

                def scale(n, m, i, j):
                    if j == 0:
                        cs.turn(n)
                    if not (isinstance(n, int) and n == 0):
                        wait(dve, S["turned"], nth(n - 1, j))
                    kn, kb, qn = (st[:, j, c].rearrange(h3, d=DH) for c in range(3))
                    cs.link(dve.tensor_tensor(kn, k4[:, i, m, j].rearrange(h3, d=DH), bcast(r_k[:, i, m, j], 2, DH), ALU.mult))
                    dve.tensor_tensor(kb, kn, bcast(bt[:, i, m, j], 2, DH), ALU.mult)
                    dve.tensor_tensor(qn, q4[:, i, m, j].rearrange(h3, d=DH), bcast(r_q[:, i, m, j], 2, DH),
                                      ALU.mult).then_inc(S["scaled"], 1)

                def mask_a_turned(n, m, i, j):
                    wait(dve, S["a_turned_ready"], nth(n, j))
                    dve.tensor_tensor(at[:, m, j], pz[:, j], tile4(K["before"]), ALU.mult)
                    dve.tensor_tensor(yv[:, m, j], pz[:, j], tile4(K["level0"]), ALU.mult).then_inc(S["a_turned_masked"], 1)

                def mask_a(n, m, i, j):
                    wait(dve, S["a_ready"], nth(n, j))
                    dve.tensor_tensor(x[:, m, j], pz[:, j], tile4(K["level0_lower"]), ALU.mult).then_inc(S["a_masked"], 1)

                def mask_local(n, m, i, j):
                    wait(dve, S["local_ready"], nth(n, j))
                    dve.tensor_tensor(lt[:, m, j], pz[:, j], tile4(K["upto"]), ALU.mult).then_inc(S["local_masked"], 1)

                steps = {0: scale, 2: mask_a_turned, 3: mask_a, 4: mask_local}

                def turn(n, m, i):
                    behind = pair_behind(n, m, i)
                    for level in range(NL):
                        for j in range(2):
                            wait(dve, S["ax_ready"], nth_level(n, level, j))
                            dve.tensor_tensor(t1[:, j], p1[:, j], tile4(K[f"level{level + 1}_lower"]),
                                              ALU.mult).then_inc(S["ax_masked"], 1)
                        for j in range(2):
                            if behind and level in steps:
                                steps[level](*behind, j)
                            wait(dve, S["step_ready"], nth_level(n, level, j))
                            if level < NL - 1:
                                dve.tensor_tensor(x[:, m, j], x[:, m, j], px[:, j], ALU.subtract)
                            dve.tensor_tensor(yv[:, m, j], yv[:, m, j], py[:, j], ALU.subtract).then_inc(S["updated"], 1)
                    for j in range(2):
                        wait(dve, S["w_ready"], nth(n, j))
                        dve.tensor_tensor(u[:, j], u0[:, j], p1[:, j, 2], ALU.subtract).then_inc(S["u_ready"], 1)
                    for j in range(2):
                        wait(dve, S["o_ready"], nth(n, j))
                        dve.tensor_copy(out4[:, i, m, j], p1[:, j, 3]).then_inc(S["stored"], 1)

                for step in (scale, mask_a_turned, mask_a, mask_local):
                    for j in range(2):
                        step(0, 0, 0, j)
                over_pairs(dve, turn, PAIRS)

            @block.scalar
            def _(act):
                def spread(n, j):
                    wait(act, S["turned"], nth(n, j))
                    if not (isinstance(n, int) and n == 0):
                        wait(act, S["local_ready"], nth(n - 1, j))
                    for h in range(H4):
                        act.activation(fsp[:, j, :, h], pz[:, j, 0:3], ACT.Identity, scale=K["headmask32"][:, h:h + 1])
                    act.copy(ft[:, j], pz[:, j, 0:3]).then_inc(S["turned_copied"], 1)

                def turn(n, m, i):
                    behind = pair_behind(n, m, i)
                    if behind:
                        for j in range(2):
                            spread(behind[0], j)
                    for j in range(2):
                        wait(act, S["u0_ready"], nth(n, j))
                        act.copy(u0[:, j], p1[:, j, 0])
                        act.activation(u0_first[:, j], p1[:, j, 0], ACT.Identity,
                                       scale=K["half"][:, 0:1]).then_inc(S["u0_copied"], 1)
                    for j in range(2):
                        wait(act, S["z_ready"], nth(n, j))
                        act.activation(zc[:, j], p1[:, j, 1], ACT.Identity, scale=K["half"][:, 1:2]).then_inc(S["z_copied"], 1)
                for j in range(2):
                    spread(0, j)
                over_pairs(act, turn, PAIRS)

            @block.tensor
            def _(pe):
                vb4 = by_pair(vb)

                def turn_scaled(n, j):
                    wait(pe, S["scaled"], nth(n, j))
                    if not (isinstance(n, int) and n == 0):
                        wait(pe, S["local_masked"], nth(n - 1, j))
                    for c in range(3):
                        last = pe.transpose(pz[:, j, c], st[:, j, c], K["ident"])
                    last.then_inc(S["turned"], 1)

                def a_turned(n, j):
                    wait(pe, S["turned_copied"], nth(n, j))
                    pe.matmul(pz[:, j], ft[:, j, 0], fsp[:, j, 1], start=True, stop=True).then_inc(S["a_turned_ready"], 1)

                def a_plain(n, j):
                    wait(pe, S["a_turned_masked"], nth(n, j))
                    pe.matmul(pz[:, j], ft[:, j, 1], fsp[:, j, 0], start=True, stop=True).then_inc(S["a_ready"], 1)

                def local(n, j):
                    wait(pe, S["a_masked"], nth(n, j))
                    pe.matmul(pz[:, j], ft[:, j, 0], fsp[:, j, 2], start=True, stop=True).then_inc(S["local_ready"], 1)

                steps = {0: turn_scaled, 1: a_turned, 2: a_plain, 3: local}

                def by_head(ready, n, j, at_column, lhs, rhs):
                    for h in range(H4):
                        last = pe.matmul(p1[:, j, at_column, DH * h:DH * h + DH], lhs[:, h], rhs[:, DH * h:DH * h + DH],
                                         start=True, stop=True)
                    last.then_inc(S[ready], 1)

                def turn(n, m, i):
                    behind = pair_behind(n, m, i)
                    for level in range(NL):
                        for j in range(2):
                            if level == 0:
                                wait(pe, S["started"], nth(n, j))
                                if not (isinstance(n, int) and n == 0):
                                    wait(pe, S["stored"], nth(n - 1, j))
                            else:
                                wait(pe, S["updated"], nth_level(n, level - 1, j))
                            for h in range(H4):
                                last = pe.matmul(p1[:, j, h], at[:, m, j, h], x[:, m, j, h], start=True, stop=True)
                            last.then_inc(S["ax_ready"], 1)
                        for j in range(2):
                            wait(pe, S["ax_masked"], nth_level(n, level, j))
                            for h in range(H4):
                                if level < NL - 1:
                                    pe.matmul(px[:, j, h], yv[:, m, j, h], t1[:, j, h], start=True, stop=True)
                                last = pe.matmul(py[:, j, h], t1[:, j, h], yv[:, m, j, h], start=True, stop=True)
                            last.then_inc(S["step_ready"], 1)
                            if behind and level in steps:
                                steps[level](behind[0], j)
                    for j in range(2):
                        wait(pe, S["updated"], nth_level(n, NL - 1, j))
                        by_head("u0_ready", n, j, 0, yv[:, m, j], vb4[:, i, m, j])
                    for j in range(2):
                        wait(pe, S["u0_copied"], nth(n, j))
                        by_head("z_ready", n, j, 1, at[:, m, j], u0_first[:, j])
                    for j in range(2):
                        wait(pe, S["z_copied"], nth(n, j))
                        by_head("w_ready", n, j, 2, yv[:, m, j], zc[:, j])
                    for j in range(2):
                        wait(pe, S["u_ready"], nth(n, j))
                        wait(pe, S["local_masked"], nth(n, j))
                        by_head("o_ready", n, j, 3, lt[:, m, j], u[:, j])

                for step in (turn_scaled, a_turned, a_plain, local):
                    for j in range(2):
                        step(0, j)
                over_pairs(pe, turn, PAIRS)


def head_stats(nc, K, sources, stats):
    with Stage(nc) as s:
        sq, dev = s.sb("squares", [P, 2, B, D]), s.sb("deviations", [P, 2, B, D])
        m = s.sb("means", [P, 2, B * H4])
        sums = s.sb("sums", [P, 4, 3, B * H4])
        S = {n: s.sem("stats_" + n) for n in "squared mean_ready deviated dev_squared used summed chain".split()}
        with s.block() as block:
            @block.gpsimd
            def _(pool):
                for k, src in enumerate(sources):
                    pool.wait_ge(S["mean_ready"], k + 1)
                    wait(pool, S["used"], k - 1)
                    pool.tensor_tensor(by_head(dev[:, k % 2]), by_head(src), bcast(m[:, k % 2], 2, DH),
                                       ALU.subtract).then_inc(S["deviated"], 1)

            @block.scalar
            def _(act):
                for k, src in enumerate(sources):
                    wait(act, S["used"], k - 1)
                    act.activation(sq[:, k % 2], src, ACT.Square).then_inc(S["squared"], 1)
                    act.wait_ge(S["deviated"], k + 1)
                    act.activation(dev[:, k % 2], dev[:, k % 2], ACT.Square).then_inc(S["dev_squared"], 1)
                act.wait_ge(S["summed"], 1)
                for k in range(len(sources)):
                    act.activation(stats[:, :, :, 4 * k + 3], sums[:, k, 2].rearrange("p (b h) -> p b h", h=H4), ACT.Sqrt)

            @block.vector
            def _(dve):
                c = Chain(dve, S["chain"])
                for k, src in enumerate(sources):
                    b3 = "p (b h) -> p b h"
                    c.link(dve.tensor_reduce(m[:, k % 2], by_head(src), AX.X, ALU.add))
                    dve.tensor_scalar(m[:, k % 2], m[:, k % 2], 1.0 / DH, None, ALU.mult).then_inc(S["mean_ready"], 1)
                    dve.tensor_reduce(sums[:, k, 0], by_head(src), AX.X, ALU.add, apply_absolute_value=True)
                    dve.wait_ge(S["squared"], k + 1)
                    dve.tensor_reduce(sums[:, k, 2], by_head(sq[:, k % 2]), AX.X, ALU.add)
                    dve.wait_ge(S["dev_squared"], k + 1)
                    c.link(dve.tensor_reduce(sums[:, k, 1], by_head(dev[:, k % 2]), AX.X, ALU.add))
                    dve.engine_nop().then_inc(S["used"], 1)
                    dve.tensor_copy(stats[:, :, :, 4 * k], m[:, k % 2].rearrange(b3, h=H4))
                    dve.tensor_scalar(stats[:, :, :, 4 * k + 1], sums[:, k, 1].rearrange(b3, h=H4), 1.0 / DH, None, ALU.mult)
                    c.link(dve.tensor_scalar(stats[:, :, :, 4 * k + 2], sums[:, k, 0].rearrange(b3, h=H4), 1.0 / DH, None, ALU.mult))
                dve.engine_nop().then_inc(S["summed"], 1)


def head_gate(nc, K, w, XT, stats, logits):
    with Stage(nc) as s:
        w1, w1s, b1, w2 = (w[n] for n in ("w1_x", "w1_stats", "b1", "w2"))
        sT = s.sb("stats_turned", [NS, B, T])
        h1 = s.sb("hidden", [D, 2, H4, T])
        pt = s.ps("p_stats", [P, GROUP, T])
        ph = s.ps("p_hidden", [P, 2, H4, T])
        pl = s.ps("p_logits", [P, 2, 512])
        S = {n: s.sem("gate_" + n) for n in "turned copied hidden_ready active logits_ready stored".split()}
        with s.block() as block:
            @block.tensor
            def _(pe):
                for g in range(GROUPS):
                    wait(pe, S["copied"], g)
                    for j in range(GROUP):
                        last = pe.transpose(pt[0:NS, j], stats[:, GROUP * g + j].rearrange("t h k -> t (h k)"), K["ident"])
                    last.then_inc(S["turned"], 1)
                pe.wait_ge(S["copied"], GROUPS)
                xt, st = pairs(XT), pairs(sT[:])

                def hidden(n, j, i):
                    wait(pe, S["active"], n - 1)
                    for h in range(H4):
                        pe.matmul(ph[:, j, h], w1[:], xt[:, i, j], start=True, stop=False)
                        last = pe.matmul(ph[:, j, h], w1s[:, h], st[:, i, j], start=False, stop=True)
                    last.then_inc(S["hidden_ready"], 1)

                def logit(n, j):
                    wait(pe, S["active"], n + 1)
                    wait(pe, S["stored"], n - 1)
                    for h in range(H4):
                        last = pe.matmul(pl[:, j, 4 * h:4 * h + 4], h1[:, j, h], w2[:], start=True, stop=True)
                    last.then_inc(S["logits_ready"], 1)

                def turn(n, j, i):
                    hidden(n, j, i)
                    if not (isinstance(n, int) and n == 0):
                        logit(n - 1, 1 - j)
                first_then_loop(pe, B, turn)
                logit(B - 1, 1)

            @block.scalar
            def _(act):
                for g in range(GROUPS):
                    act.wait_ge(S["turned"], g + 1)
                    act.copy(sT[:, GROUP * g:GROUP * g + GROUP], pt[0:NS]).then_inc(S["copied"], 1)

                def turn(n, j, i):
                    wait(act, S["hidden_ready"], n + 1)
                    wait(act, S["logits_ready"], n - 1)
                    act.activation(h1[:, j], ph[:, j], ACT.Gelu, bias=b1[:]).then_inc(S["active"], 1)
                first_then_loop(act, B, turn)

            @block.vector
            def _(dve):
                lg = logits.rearrange("t (i j) h k -> t i j (h k)", j=2)

                def turn(n, j, i):
                    wait(dve, S["logits_ready"], n + 1)
                    dve.tensor_copy(lg[:, i, j], pl[:, j, 0:16]).then_inc(S["stored"], 1)
                first_then_loop(dve, B, turn)


def head_mix(nc, K, w, sources, logits, X):
    with Stage(nc) as s:
        wo, rw, rows = (w[n] for n in ("w_o", "rms_w", "head_rows"))
        full = s.sb("head_row_full", [1, 3, H4, 4])
        tmp = s.sb("head_row_tmp", [1, 8])
        hb = s.sb("head_rows_spread", [P, 3, H4, 4])
        pr = s.sb("p", [P, B, H4, 4])
        m = s.sb("row", [P, B, H4])
        o, part = s.sb("mix", [P, B, D]), s.sb("mix_part", [P, 2, B, D])
        oT = s.sb("mix_turned", [D, B, T])
        p_small = s.ps("p_small", [P, 48])
        pt = s.ps("p_turned", [P, 2, GROUP, T])
        po = s.ps("p_out", [P, 2, GROUP, D])
        names = ("rows_ready temp_abs temp_soft full_ready spread spread_copied shifted exp_ready p_ready part_ready part_used "
                 "mixed squared summed rooted normed turned turned_copied out_ready chain")
        S = {n: s.sem("mix_" + n) for n in names.split()}
        flat = "p b h k -> p (b h) k"
        m_flat = m[:].rearrange("p b h -> p (b h)")
        f3 = "p (b h) -> p b h"
        with s.block() as block:
            @block.scalar
            def _(act):
                c = Chain(act, S["temp_abs"])
                c.link(act.activation(tmp[:, 0:4], rows[:, 20:24], ACT.Abs))
                c.link(act.activation(tmp[:, 0:4], tmp[:, 0:4], ACT.Exp, scale=-1.0))
                act.activation(tmp[:, 0:4], tmp[:, 0:4], ACT.Ln, bias=1.0)
                act.activation(tmp[:, 4:8], rows[:, 24:28], ACT.Sigmoid).then_inc(S["temp_soft"], 1)
                act.wait_ge(S["spread"], 1)
                act.copy(hb[:], p_small[:].rearrange("p (a h k) -> p a h k", a=3, h=H4)).then_inc(S["spread_copied"], 1)
                act.wait_ge(S["shifted"], 1)
                act.activation(pr[:], pr[:], ACT.Exp).then_inc(S["exp_ready"], 1)
                act.wait_ge(S["mixed"], 1)
                act.activation(part[:, 0], o[:], ACT.Square).then_inc(S["squared"], 1)
                act.wait_ge(S["summed"], 1)
                act.activation(m[:], m[:], ACT.Sqrt).then_inc(S["rooted"], 1)
                for g in range(GROUPS):
                    act.wait_ge(S["turned"], g + 1)
                    act.activation(oT[:, GROUP * g:GROUP * g + GROUP], pt[:, g % 2], ACT.Identity,
                                   scale=rw[:]).then_inc(S["turned_copied"], 1)

            @block.tensor
            def _(pe):
                pe.wait_ge(S["full_ready"], 1)
                pe.matmul(p_small[:], K["ones"][0:1, :], full[:].rearrange("p a h k -> p (a h k)"),
                          start=True, stop=True).then_inc(S["spread"], 1)
                pe.wait_ge(S["normed"], 1)
                for g in range(GROUPS):
                    wait(pe, S["turned_copied"], g - 1)
                    for j in range(GROUP):
                        last = pe.transpose(pt[:, g % 2, j], o[:, GROUP * g + j], K["ident"])
                    last.then_inc(S["turned"], 1)
                for g in range(GROUPS):
                    pe.wait_ge(S["turned_copied"], g + 1)
                    wait(pe, S["out_ready"], 0)
                    wait(pe, S["part_used"], 4 + (g - 1) if g >= 2 else 0)
                    for j in range(GROUP):
                        last = pe.matmul(po[:, g % 2, j], oT[:, GROUP * g + j], wo[:], start=True, stop=True)
                    last.then_inc(S["out_ready"], 1)

            @block.gpsimd
            def _(pool):
                pool.wait_ge(S["part_ready"], 1)
                for k in range(1, 4):
                    pool.wait_ge(S["part_ready"], k + 1)
                    wait(pool, S["part_used"], k - 1)
                    pool.tensor_tensor(o[:], o[:], part[:, k % 2], ALU.add).then_inc(S["part_used"], 1)

            @block.vector
            def _(dve):
                c = Chain(dve, S["chain"])
                dve.wait_ge(S["temp_soft"], 1)
                base = rows[:, 0:16].rearrange("p (h k) -> p h k", k=4)
                dve.tensor_tensor(full[:, 0], base, bcast(rows[:, 16:20], 1, H4), ALU.add)
                c.link(dve.scalar_tensor_tensor(tmp[:, 0:4], rows[:, 20:24], 0.0, tmp[:, 0:4], ALU.max, ALU.add))
                c.link(dve.tensor_scalar(tmp[:, 0:4], tmp[:, 0:4], 1e-4, None, ALU.add))
                c.link(dve.reciprocal(tmp[:, 0:4], tmp[:, 0:4]))
                dve.tensor_copy(full[:, 1], bcast(tmp[:, 0:4], 2, 4))
                dve.tensor_scalar(full[:, 2], bcast(tmp[:, 4:8], 2, 4), 0.5, None, ALU.mult).then_inc(S["full_ready"], 1)
                dve.wait_ge(S["spread_copied"], 1)
                c.link(dve.tensor_tensor(pr[:], logits, bcast(hb[:, 0], 1, B), ALU.add))
                c.link(dve.tensor_tensor(pr[:], pr[:], bcast(hb[:, 1], 1, B), ALU.mult))
                c.link(dve.tensor_reduce(m_flat, pr[:].rearrange(flat), AX.X, ALU.max))
                dve.tensor_tensor(pr[:].rearrange(flat), pr[:].rearrange(flat), bcast(m_flat, 2, 4),
                                  ALU.subtract).then_inc(S["shifted"], 1)
                dve.wait_ge(S["exp_ready"], 1)

                def to_one():
                    c.link(dve.tensor_reduce(m_flat, pr[:].rearrange(flat), AX.X, ALU.add))
                    c.link(dve.reciprocal(m_flat, m_flat))
                    c.link(dve.tensor_tensor(pr[:].rearrange(flat), pr[:].rearrange(flat), bcast(m_flat, 2, 4), ALU.mult))
                to_one()
                dve.tensor_scalar(pr[:, :, :, 0:2], pr[:, :, :, 0:2], 0.05, None, ALU.max)
                c.link(dve.tensor_scalar(pr[:, :, :, 2:4], pr[:, :, :, 2:4], 0.0, None, ALU.max))
                to_one()
                c.link(dve.tensor_tensor(pr[:, :, :, 0], pr[:, :, :, 0], bcast(hb[:, 2, :, 0], 1, B), ALU.add))
                for k, src in enumerate(sources):
                    wait(dve, S["part_used"], k - 2)
                    dst = o[:] if k == 0 else part[:, k % 2]
                    dve.tensor_tensor(by_head(dst), by_head(src), bcast(pr[:].rearrange(flat)[:, :, k], 2, DH),
                                      ALU.mult).then_inc(S["part_ready"], 1)
                dve.wait_ge(S["part_used"], 3)
                dve.engine_nop().then_inc(S["mixed"], 1)
                dve.wait_ge(S["squared"], 1)
                c.link(dve.tensor_reduce(m_flat, by_head(part[:, 0]), AX.X, ALU.add))
                dve.tensor_scalar(m[:], m[:], 1.0 / DH, 1e-5, ALU.mult, ALU.add).then_inc(S["summed"], 1)
                dve.wait_ge(S["rooted"], 1)
                c.link(dve.reciprocal(m[:], m[:]))
                dve.tensor_tensor(by_head(o[:]), by_head(o[:]), bcast(m_flat, 2, DH), ALU.mult).then_inc(S["normed"], 1)
                for g in range(GROUPS):
                    dve.wait_ge(S["out_ready"], g + 1)
                    grp = slice(GROUP * g, GROUP * g + GROUP)
                    dve.tensor_tensor(X[:, grp], X[:, grp], po[:, g % 2], ALU.add).then_inc(S["part_used"], 1)


def delta_weights(nc, s, w):
    W = {n: s.sb(n, shape) for n, shape in {
        "w_qkv": [D, 3, D], "conv_taps": [P, 3, CONV], "fir_long": [P, LONG], "fir_short": [P, SHORT],
        "w_beta": [D, H4], "w1_x": [D, D], "w1_stats": [NS, H4, D], "b1": [D, 1], "w2": [D, H4], "w_o": [D, D],
        "rms_w": [D, 1],
        "head_rows": [1, 16 + 4 + 4 + 4]}.items()}
    rows = W["head_rows"]
    loads = [(W["w_qkv"][:, 0], w["L2_attn_Wq"]), (W["w_qkv"][:, 1], w["L2_attn_Wk"]), (W["w_qkv"][:, 2], w["L2_attn_Wv"]),
             (W["conv_taps"][:, 0], w["L2_attn_conv_q"]), (W["conv_taps"][:, 1], w["L2_attn_conv_k"]),
             (W["conv_taps"][:, 2], w["L2_attn_conv_v"]),
             (W["fir_long"][:], w["L2_attn_fir_long"].rearrange("h d k -> (h d) k")),
             (W["fir_short"][:], w["L2_attn_fir_short"].rearrange("h d k -> (h d) k")),
             (W["w_beta"][:], w["L2_attn_Wb"]), (W["w1_x"][:], w["L2_attn_W1"][0:D]), (W["b1"][:], column(w["L2_attn_b1"])),
             (W["w2"][:], w["L2_attn_W2"]), (W["w_o"][:], w["L2_attn_Wo"]),
             (rows[:, 0:16], row(w["L2_attn_base_bias"].rearrange("h k -> (h k)"))),
             (rows[:, 16:20], row(w["L2_attn_b2"])), (rows[:, 20:24], row(w["L2_attn_log_temp"])),
             (rows[:, 24:28], row(w["L2_attn_conv_residual_logit"]))]
    loads += [(W["w1_stats"][16 * h:16 * h + 16, h], w["L2_attn_W1"][D:D + 16]) for h in range(H4)]
    loads += [(W["rms_w"][DH * h:DH * h + DH, :], column(w["L2_attn_rms_w"])) for h in range(H4)]
    with s.block() as block:
        @block.vector
        def _(dve):
            dve.memset(W["w1_stats"][:], 0.0)
    return W, loads


def l2_attn(nc, K, w, X, XN, XT):
    with Stage(nc) as s:
        w, loads = delta_weights(nc, s, w)
        layernorm(nc, K, X, XN, XT, loads=loads)
        v, fs, fl = (s.sb(n, [P, B, D]) for n in ("v", "f_short", "f_long"))
        delta = s.sb("delta_out", [P, B, D])
        with Stage(nc) as s2:
            q, k = s2.sb("q", [P, B, D]), s2.sb("k", [P, B, D])
            beta, rq, rk = (s2.sb(n, [P, B, H4]) for n in ("beta", "q_scale", "k_scale"))
            taps(nc, K, w, XT, q[:], k[:], v[:], fs[:], fl[:])
            vb = s2.sb("v_beta", [P, B, D])
            delta_scales(nc, K, w, XT, q[:], k[:], v[:], vb[:], beta[:], rq[:], rk[:])
            delta_rule(nc, K, q[:], k[:], vb[:], beta[:], rq[:], rk[:], delta[:])
        stats, logits = s.sb("stats", [P, B, H4, 16]), s.sb("logits", [P, B, H4, 4])
        sources = [fs[:], fl[:], delta[:], v[:]]
        head_stats(nc, K, sources, stats[:])
        head_gate(nc, K, w, XT, stats[:], logits[:])
        head_mix(nc, K, w, sources, logits[:], X)



BIAS_COLUMNS = ["L1_ffn_b1", "L3_ffn_rb1", "L3_ffn_rb2", "L3_ffn_sb1", "L3_ffn_sb2", "L3_attn_b1"]
TRANSPOSED = ["L1_xattn_W_l", "L1_ffn_Wg", "L1_ffn_Wo", "L3_attn_Wd", "L3_attn_Wbc", "L3_attn_W1", "L3_attn_W2"]


def host_layout(inputs):
    arrays = {}
    for name, a in inputs.items():
        a = np.asarray(a)
        if a.ndim == 0:
            a = a.reshape(1)
        if name in TRANSPOSED:
            a = a.T
        if name == "L1_ffn_W1":
            a = a.transpose(0, 2, 1)
        if name in BIAS_COLUMNS:
            a = np.moveaxis(a.reshape(*a.shape[:-1], -1, P), -1, -2)
        arrays[name] = np.ascontiguousarray(a)
    return arrays



def kernel(**inputs):
    import concourse.bacc as bacc
    from concourse.bass_utils import run_bass_kernel_spmd

    arrays = host_layout(inputs)
    arrays["constants"] = constant_blob()
    nc = bacc.Bacc("TRN2", target_bir_lowering=False, num_devices=1)
    w = {name: nc.dram_tensor(f"in_{name}", a.shape, mybir.dt.from_np(a.dtype), kind="ExternalInput").ap()
         for name, a in arrays.items()}
    out = nc.dram_tensor("out_x", (B, T, D), F32, kind="ExternalOutput").ap()
    program(nc, w, out)
    r = run_bass_kernel_spmd(nc, [{f"in_{name}": a for name, a in arrays.items()}], core_ids=[0])
    return r.results[0]["out_x"]
```
